# Optimizing a Trainium2 kernel written in Bass

```python
import numpy as np
import jax
import jax.numpy as jnp

def _softmax(x, axis=-1):
    return jax.nn.softmax(x, axis=axis)

def _gelu(x):
    return jax.nn.gelu(x, approximate=True)

def _silu(x):
    return jax.nn.silu(x)

def _sigmoid(x):
    return jax.nn.sigmoid(x)

def _layernorm(x, axis=-1, eps=1e-05):
    m = jnp.mean(x, axis=axis, keepdims=True)
    v = jnp.var(x, axis=axis, keepdims=True)
    return (x - m) / jnp.sqrt(v + eps)

def _scatter_add(tgt, idx, src, axis=0):
    return tgt.at[idx].add(src)

def _segment_sum(src, seg, n):
    return jax.ops.segment_sum(src, seg, n)
kernel_name = 'mk_gps_d2_gnn_r32_b128f1'

def setup_inputs(seed: int=0):
    np.random.seed(seed)
    _w = jnp.asarray

    def _rec_inputs():
        import jax
        import jax.numpy as jnp
        _gk = jax.random.key(seed)
        x = -8.776e-05 + 1 * jax.random.normal(jax.random.fold_in(_gk, 1), (625, 256), jnp.float32)
        src = jax.random.randint(jax.random.fold_in(_gk, 2), (20000,), 0, 625, jnp.int32)
        dst = jax.random.randint(jax.random.fold_in(_gk, 3), (20000,), 0, 625, jnp.int32)
        _o = jnp.argsort(dst, stable=True)
        src = src[_o]
        dst = dst[_o]
        edge_attr_16 = -0.000153872 + 1.00011 * jax.random.normal(jax.random.fold_in(_gk, 11), (20000, 16), jnp.float32)
        edge_attr_4 = 0.0007022 + 0.999661 * jax.random.normal(jax.random.fold_in(_gk, 12), (20000, 4), jnp.float32)
        edge_type_8 = jax.random.randint(jax.random.fold_in(_gk, 14), (20000,), 0, 8, jnp.int32)
        return (x, src, dst, edge_attr_16, edge_attr_4, edge_type_8)
    x, src, dst, edge_attr_16, edge_attr_4, edge_type_8 = _rec_inputs()

    def _L0_gnn_setup():
        import jax, jax.numpy as jnp
        import numpy as np
        N_NODES = 625
        N_EDGES = 10000
        D = 256
        R = 8

        def _xavier(key, shape):
            fan_in, fan_out = (shape[-2], shape[-1])
            bound = float(np.sqrt(6.0 / (fan_in + fan_out)))
            return jax.random.uniform(key, shape, jnp.float32, -bound, bound)

        def _rgcn_layer(x, W, self_w, b, src, dst, edge_type, num_nodes):
            xW = jnp.einsum('ni,rio->rno', x, W)
            msg = xW[edge_type, src]
            agg = jax.ops.segment_sum(msg, dst, num_segments=num_nodes)
            return agg + x @ self_w + b
        key = jax.random.key(seed)
        ks = jax.random.split(key, 10)
        x = jax.random.normal(ks[0], (N_NODES, D), jnp.float32)
        edge_index = jax.random.randint(ks[1], (2, N_EDGES), 0, N_NODES)
        edge_type = jax.random.randint(ks[2], (N_EDGES,), 0, R)
        W1 = _xavier(ks[3], (R, D, D))
        self_w1 = _xavier(ks[4], (D, D))
        b1 = jnp.zeros((D,), jnp.float32)
        W2 = _xavier(ks[5], (R, D, D))
        self_w2 = _xavier(ks[6], (D, D))
        b2 = jnp.zeros((D,), jnp.float32)
        return {'x': x, 'W1': W1, 'self_w1': self_w1, 'b1': b1, 'W2': W2, 'self_w2': self_w2, 'b2': b2, 'edge_index': edge_index, 'edge_type': edge_type}
    _L0_gnn_all = _L0_gnn_setup()
    _L0_gnn_in = {k: v for k, v in _L0_gnn_all.items() if k in ('W1', 'self_w1', 'b1', 'W2', 'self_w2', 'b2')}
    del _L0_gnn_all

    def _L0_mix_setup():
        import jax, jax.numpy as jnp
        import numpy as np
        A, Bc, Cc = (0.5, 1.0, 1.0)
        H = 8
        EPS = 1e-12

        def _normalize(t):
            n = jnp.linalg.norm(t, axis=-1, keepdims=True)
            return t / jnp.maximum(n, EPS)
        key = jax.random.key(seed)
        ks = jax.random.split(key, 5)
        B, N, C = (8, 64, 256)
        D = C // H
        x = jax.random.normal(ks[0], (B, N, C), dtype=jnp.float32)
        Wqkv = jax.random.normal(ks[1], (3 * H * D, C), dtype=jnp.float32) * 0.02
        bqkv = jnp.zeros((3 * H * D,), dtype=jnp.float32)
        Wproj = jax.random.normal(ks[2], (C, H * D), dtype=jnp.float32) * 0.02
        bproj = jnp.zeros((C,), dtype=jnp.float32)
        temperature = jnp.ones((1, H, 1, 1), dtype=jnp.float32)
        return {'x': x, 'Wqkv': Wqkv, 'bqkv': bqkv, 'Wproj': Wproj, 'bproj': bproj, 'temperature': temperature}
    _L0_mix_all = _L0_mix_setup()
    _L0_mix_in = {k: v for k, v in _L0_mix_all.items() if k in ('Wqkv', 'bqkv', 'Wproj', 'bproj', 'temperature')}
    del _L0_mix_all

    def _L0_ffn_setup():
        import jax, jax.numpy as jnp
        import numpy as np
        B, K, D = (512, 16, 256)
        E = 32
        H = int(D * 0.25)
        key = jax.random.key(seed)
        ks = jax.random.split(key, 7)
        d_rs = D ** (-0.5)
        h_rs = H ** (-0.5)
        x = jax.random.normal(ks[0], (B, K, D), dtype=jnp.float32)
        router_w = jax.random.uniform(ks[1], (E, D), jnp.float32, -d_rs, d_rs)
        router_b = jax.random.uniform(ks[2], (E,), jnp.float32, -d_rs, d_rs)
        W1 = jax.random.uniform(ks[3], (E, D, H), jnp.float32, -h_rs, h_rs)
        b1 = jax.random.uniform(ks[4], (E, H), jnp.float32, -h_rs, h_rs)
        W2 = jax.random.uniform(ks[5], (E, H, D), jnp.float32, -d_rs, d_rs)
        b2 = jax.random.uniform(ks[6], (E, D), jnp.float32, -d_rs, d_rs)
        return {'x': x, 'router_w': router_w, 'router_b': router_b, 'W1': W1, 'b1': b1, 'W2': W2, 'b2': b2}
    _L0_ffn_all = _L0_ffn_setup()
    _L0_ffn_in = {k: v for k, v in _L0_ffn_all.items() if k in ('router_w', 'router_b', 'W1', 'b1', 'W2', 'b2')}
    del _L0_ffn_all

    def _L1_gnn_setup():
        import jax, jax.numpy as jnp
        import numpy as np
        N, E, C, R, HID = (50000, 15625, 64, 16, 64)
        key = jax.random.key(seed)
        ks = jax.random.split(key, 24)
        g = lambda k, shape, s=1.0: jax.random.normal(k, shape, dtype=jnp.float32) * s
        cs = C ** (-0.5)
        inp = {'h': g(ks[0], (N, 4 * C)), 'edge_index': jax.random.randint(ks[1], (2, E), 0, N), 'edge_sh': g(ks[2], (E, 4)), 'edge_rbf': g(ks[3], (E, R)), 'W_up0': g(ks[4], (C, C), cs), 'W_up1': g(ks[5], (C, C), cs), 'M1': g(ks[6], (R, HID), R ** (-0.5)), 'M2': g(ks[7], (HID, HID), HID ** (-0.5)), 'M3': g(ks[8], (HID, HID), HID ** (-0.5)), 'M4': g(ks[9], (HID, 4 * C), HID ** (-0.5)), 'W_lin0': g(ks[10], (C, C), cs), 'W_lin1': g(ks[11], (C, C), cs), 'Wsc0': g(ks[12], (C, C), cs), 'Wsc1': g(ks[13], (C, C), cs), 'Wc0': g(ks[14], (C, 5)), 'Wc1': g(ks[15], (C, 4)), 'WB0': g(ks[16], (C, C), cs), 'WB1': g(ks[17], (C, C), cs), 'gamma0': jnp.ones((C,), jnp.float32), 'beta0': jnp.zeros((C,), jnp.float32), 'gamma1': jnp.ones((C,), jnp.float32)}
        return inp
    _L1_gnn_all = _L1_gnn_setup()
    _L1_gnn_in = {k: v for k, v in _L1_gnn_all.items() if k in ('W_up0', 'W_up1', 'M1', 'M2', 'M3', 'M4', 'W_lin0', 'W_lin1', 'Wsc0', 'Wsc1', 'Wc0', 'Wc1', 'WB0', 'WB1', 'gamma0', 'beta0', 'gamma1')}
    del _L1_gnn_all

    def _L1_mix_setup():
        import jax, jax.numpy as jnp
        import numpy as np
        HEADS = 4
        DIM_HEAD = 32
        key = jax.random.key(seed)
        k1, k2, k3 = jax.random.split(key, 3)
        B, L, D = (16, 256, 256)
        hidden = HEADS * DIM_HEAD
        x = jax.random.normal(k1, (B, L, D), dtype=jnp.float32)
        W_qkv = jax.random.normal(k2, (D, 3 * hidden), dtype=jnp.float32) * D ** (-0.5)
        W_out = jax.random.normal(k3, (hidden, D), dtype=jnp.float32) * hidden ** (-0.5)
        b_out = jnp.zeros((D,), dtype=jnp.float32)
        return {'x': x, 'W_qkv': W_qkv, 'W_out': W_out, 'b_out': b_out}
    _L1_mix_all = _L1_mix_setup()
    _L1_mix_in = {k: v for k, v in _L1_mix_all.items() if k in ('W_qkv', 'W_out', 'b_out')}
    del _L1_mix_all

    def _L1_ffn_setup():
        import jax, jax.numpy as jnp
        import numpy as np
        B, T, C = (64, 384, 256)
        NH, NKV = (4, 2)
        HD = C // NH
        NREP = NH // NKV
        NE, TOPK = (8, 2)
        HID = int(8 / 3 * C)
        EPS_RMS = 1e-06

        def _rope_tables(t_len):
            inv_freq = 1.0 / 10000.0 ** (np.arange(0, HD, 2, dtype=np.float32) / HD)
            t = np.arange(t_len, dtype=np.float32)
            freqs = np.outer(t, inv_freq)
            emb = np.concatenate([freqs, freqs], axis=-1)
            return (jnp.asarray(np.cos(emb)), jnp.asarray(np.sin(emb)))

        def _rotate_half(x):
            h = x.shape[-1] // 2
            return jnp.concatenate([-x[..., h:], x[..., :h]], axis=-1)

        def _rmsnorm(v, w):
            return v * jax.lax.rsqrt(jnp.mean(v * v, axis=-1, keepdims=True) + EPS_RMS) * w
        key = jax.random.key(seed)
        ks = jax.random.split(key, 10)
        s = lambda k, shape: jax.random.normal(k, shape, jnp.float32) * 0.02
        return {'x': jax.random.normal(ks[0], (B, T, C), jnp.float32), 'ln1_w': jnp.ones((C,), jnp.float32), 'ln2_w': jnp.ones((C,), jnp.float32), 'wq': s(ks[1], (NH * HD, C)), 'wk': s(ks[2], (NKV * HD, C)), 'wv': s(ks[3], (NKV * HD, C)), 'wo': s(ks[4], (C, C)), 'router_w': s(ks[5], (NE, C)), 'w1': s(ks[6], (NE, HID, C)), 'w2': s(ks[7], (NE, C, HID)), 'w3': s(ks[8], (NE, HID, C))}
    _L1_ffn_all = _L1_ffn_setup()
    _L1_ffn_in = {k: v for k, v in _L1_ffn_all.items() if k in ('ln1_w', 'ln2_w', 'wq', 'wk', 'wv', 'wo', 'router_w', 'w1', 'w2', 'w3')}
    del _L1_ffn_all
    return {'x': x, 'src': src, 'dst': dst, 'edge_attr_16': edge_attr_16, 'edge_attr_4': edge_attr_4, 'edge_type_8': edge_type_8, 'L0_gnn_W1': _L0_gnn_in['W1'], 'L0_gnn_self_w1': _L0_gnn_in['self_w1'], 'L0_gnn_b1': _L0_gnn_in['b1'], 'L0_gnn_W2': _L0_gnn_in['W2'], 'L0_gnn_self_w2': _L0_gnn_in['self_w2'], 'L0_gnn_b2': _L0_gnn_in['b2'], 'L0_mix_Wqkv': _L0_mix_in['Wqkv'], 'L0_mix_bqkv': _L0_mix_in['bqkv'], 'L0_mix_Wproj': _L0_mix_in['Wproj'], 'L0_mix_bproj': _L0_mix_in['bproj'], 'L0_mix_temperature': _L0_mix_in['temperature'], 'L0_ffn_router_w': _L0_ffn_in['router_w'], 'L0_ffn_router_b': _L0_ffn_in['router_b'], 'L0_ffn_W1': _L0_ffn_in['W1'], 'L0_ffn_b1': _L0_ffn_in['b1'], 'L0_ffn_W2': _L0_ffn_in['W2'], 'L0_ffn_b2': _L0_ffn_in['b2'], 'L1_gnn_W_up0': _L1_gnn_in['W_up0'], 'L1_gnn_W_up1': _L1_gnn_in['W_up1'], 'L1_gnn_M1': _L1_gnn_in['M1'], 'L1_gnn_M2': _L1_gnn_in['M2'], 'L1_gnn_M3': _L1_gnn_in['M3'], 'L1_gnn_M4': _L1_gnn_in['M4'], 'L1_gnn_W_lin0': _L1_gnn_in['W_lin0'], 'L1_gnn_W_lin1': _L1_gnn_in['W_lin1'], 'L1_gnn_Wsc0': _L1_gnn_in['Wsc0'], 'L1_gnn_Wsc1': _L1_gnn_in['Wsc1'], 'L1_gnn_Wc0': _L1_gnn_in['Wc0'], 'L1_gnn_Wc1': _L1_gnn_in['Wc1'], 'L1_gnn_WB0': _L1_gnn_in['WB0'], 'L1_gnn_WB1': _L1_gnn_in['WB1'], 'L1_gnn_gamma0': _L1_gnn_in['gamma0'], 'L1_gnn_beta0': _L1_gnn_in['beta0'], 'L1_gnn_gamma1': _L1_gnn_in['gamma1'], 'L1_mix_W_qkv': _L1_mix_in['W_qkv'], 'L1_mix_W_out': _L1_mix_in['W_out'], 'L1_mix_b_out': _L1_mix_in['b_out'], 'L1_ffn_ln1_w': _L1_ffn_in['ln1_w'], 'L1_ffn_ln2_w': _L1_ffn_in['ln2_w'], 'L1_ffn_wq': _L1_ffn_in['wq'], 'L1_ffn_wk': _L1_ffn_in['wk'], 'L1_ffn_wv': _L1_ffn_in['wv'], 'L1_ffn_wo': _L1_ffn_in['wo'], 'L1_ffn_router_w': _L1_ffn_in['router_w'], 'L1_ffn_w1': _L1_ffn_in['w1'], 'L1_ffn_w2': _L1_ffn_in['w2'], 'L1_ffn_w3': _L1_ffn_in['w3']}

def reference(x, src, dst, edge_attr_16, edge_attr_4, edge_type_8, L0_gnn_W1, L0_gnn_self_w1, L0_gnn_b1, L0_gnn_W2, L0_gnn_self_w2, L0_gnn_b2, L0_mix_Wqkv, L0_mix_bqkv, L0_mix_Wproj, L0_mix_bproj, L0_mix_temperature, L0_ffn_router_w, L0_ffn_router_b, L0_ffn_W1, L0_ffn_b1, L0_ffn_W2, L0_ffn_b2, L1_gnn_W_up0, L1_gnn_W_up1, L1_gnn_M1, L1_gnn_M2, L1_gnn_M3, L1_gnn_M4, L1_gnn_W_lin0, L1_gnn_W_lin1, L1_gnn_Wsc0, L1_gnn_Wsc1, L1_gnn_Wc0, L1_gnn_Wc1, L1_gnn_WB0, L1_gnn_WB1, L1_gnn_gamma0, L1_gnn_beta0, L1_gnn_gamma1, L1_mix_W_qkv, L1_mix_W_out, L1_mix_b_out, L1_ffn_ln1_w, L1_ffn_ln2_w, L1_ffn_wq, L1_ffn_wk, L1_ffn_wv, L1_ffn_wo, L1_ffn_router_w, L1_ffn_w1, L1_ffn_w2, L1_ffn_w3):
    import jax
    import jax.numpy as jnp

    def _L0_gnn_ref(x, W1, self_w1, b1, W2, self_w2, b2, edge_index, edge_type):
        import jax, jax.numpy as jnp
        import numpy as np
        N_NODES = 625
        N_EDGES = 10000
        D = 256
        R = 8

        def _xavier(key, shape):
            fan_in, fan_out = (shape[-2], shape[-1])
            bound = float(np.sqrt(6.0 / (fan_in + fan_out)))
            return jax.random.uniform(key, shape, jnp.float32, -bound, bound)

        def _rgcn_layer(x, W, self_w, b, src, dst, edge_type, num_nodes):
            xW = jnp.einsum('ni,rio->rno', x, W)
            msg = xW[edge_type, src]
            agg = jax.ops.segment_sum(msg, dst, num_segments=num_nodes)
            return agg + x @ self_w + b
        src, dst = (edge_index[0], edge_index[1])
        h = _rgcn_layer(x, W1, self_w1, b1, src, dst, edge_type, N_NODES)
        h = jax.nn.relu(h)
        out = _rgcn_layer(h, W2, self_w2, b2, src, dst, edge_type, N_NODES)
        return out

    def _L0_mix_ref(x, Wqkv, bqkv, Wproj, bproj, temperature):
        import jax, jax.numpy as jnp
        import numpy as np
        A, Bc, Cc = (0.5, 1.0, 1.0)
        H = 8
        EPS = 1e-12

        def _normalize(t):
            n = jnp.linalg.norm(t, axis=-1, keepdims=True)
            return t / jnp.maximum(n, EPS)
        B, N, C = x.shape
        D = C // H
        scale = float(D) ** 0.25
        qkv = (x @ Wqkv.T + bqkv).reshape(B, N, 3, H, D)
        qkv = jnp.transpose(qkv, (2, 0, 3, 1, 4))
        q, k, v = (qkv[0], qkv[1], qkv[2])
        q = q * scale
        v1 = jnp.concatenate([jnp.ones((B, H, N, 1), dtype=v.dtype), v], axis=-1)
        qn = _normalize(q) * (scale * temperature)
        kn = _normalize(k) * scale
        vN = v1 / N
        kv_mod = jnp.einsum('bhni,bhnj,bhne->bhije', kn, kn, vN)
        kv = jnp.einsum('bhnd,bhne->bhde', kn, vN)
        vsum = jnp.sum(vN, axis=-2)[:, :, None, :]
        y = A * jnp.einsum('bhni,bhnj,bhije->bhne', qn, qn, kv_mod) + scale ** 2 * Bc * jnp.einsum('bhnd,bhde->bhne', qn, kv) + scale ** 4 * Cc * vsum
        y_norm, y = (y[..., :1], y[..., 1:])
        y = y / y_norm
        out = jnp.transpose(y, (0, 2, 1, 3)).reshape(B, N, H * D)
        return out @ Wproj.T + bproj

    def _L0_ffn_ref(x, router_w, router_b, W1, b1, W2, b2):
        import jax, jax.numpy as jnp
        import numpy as np
        B, K, D = (512, 16, 256)
        E = 32
        H = int(D * 0.25)
        xf = x.reshape(-1, D)
        logits = xf @ router_w.T + router_b
        idx = jnp.argmax(logits, axis=-1)
        w1t = jnp.take(W1, idx, axis=0)
        h = jnp.einsum('nd,ndh->nh', xf, w1t) + jnp.take(b1, idx, axis=0)
        h = jax.nn.relu(h)
        w2t = jnp.take(W2, idx, axis=0)
        out = jnp.einsum('nh,nhd->nd', h, w2t) + jnp.take(b2, idx, axis=0)
        out = jax.nn.relu(out)
        return out.reshape(x.shape)

    def _L1_gnn_ref(h, edge_index, edge_sh, edge_rbf, W_up0, W_up1, M1, M2, M3, M4, W_lin0, W_lin1, Wsc0, Wsc1, Wc0, Wc1, WB0, WB1, gamma0, beta0, gamma1):
        import jax, jax.numpy as jnp
        import numpy as np
        N, E, C, R, HID = (50000, 15625, 64, 16, 64)
        n = h.shape[0]
        h0 = h[:, :C]
        h1 = h[:, C:].reshape(n, C, 3)
        up0 = h0 @ W_up0
        up1 = jnp.einsum('ncx,cd->ndx', h1, W_up1)
        r = jax.nn.silu(edge_rbf @ M1)
        r = jax.nn.silu(r @ M2)
        r = jax.nn.silu(r @ M3)
        tpw = (r @ M4).reshape(-1, 4, C)
        snd, rcv = (edge_index[0], edge_index[1])
        x0 = up0[snd]
        x1 = up1[snd]
        sh0 = edge_sh[:, 0]
        sh1 = edge_sh[:, 1:]
        inv3 = 1.0 / jnp.sqrt(jnp.float32(3.0))
        m0e = tpw[:, 0] * x0 * sh0[:, None] + tpw[:, 3] * jnp.einsum('ecx,ex->ec', x1, sh1) * inv3
        m1e = tpw[:, 1][:, :, None] * x0[:, :, None] * sh1[:, None, :] + tpw[:, 2][:, :, None] * x1 * sh0[:, None, None]
        msg0 = jax.ops.segment_sum(m0e, rcv, num_segments=n)
        msg1 = jax.ops.segment_sum(m1e, rcv, num_segments=n)
        A0 = msg0 @ W_lin0
        A1 = jnp.einsum('ncx,cd->ndx', msg1, W_lin1)
        sc0 = h0 @ Wsc0
        sc1 = jnp.einsum('ncx,cd->ndx', h1, Wsc1)
        vv = jnp.sum(A1 * A1, -1)
        B0 = Wc0[:, 0] * A0 + Wc0[:, 1] * A0 * A0 + Wc0[:, 2] * vv + Wc0[:, 3] * A0 ** 3 + Wc0[:, 4] * A0 * vv
        B1 = (Wc1[:, 0] + Wc1[:, 1] * A0 + Wc1[:, 2] * A0 * A0 + Wc1[:, 3] * vv)[..., None] * A1
        o0 = B0 @ WB0 + sc0
        o1 = jnp.einsum('ncx,cd->ndx', B1, WB1) + sc1
        eps = jnp.float32(1e-05)
        mu = jnp.mean(o0, 0)
        xc = o0 - mu
        var = jnp.mean(xc * xc, 0)
        n0 = xc * jax.lax.rsqrt(var + eps) * gamma0 + beta0
        nrm1 = jnp.mean(jnp.sum(o1 * o1, -1) / 3.0, 0)
        n1 = o1 * (jax.lax.rsqrt(nrm1 + eps) * gamma1)[None, :, None]
        return jnp.concatenate([n0, n1.reshape(n, 3 * C)], -1)

    def _L1_mix_ref(x, W_qkv, W_out, b_out):
        import jax, jax.numpy as jnp
        import numpy as np
        HEADS = 4
        DIM_HEAD = 32
        B, L, D = x.shape
        scale = DIM_HEAD ** (-0.5)
        qkv = jnp.einsum('bld,df->blf', x, W_qkv)
        qkv = qkv.reshape(B, L, 3, HEADS, DIM_HEAD)
        q = jnp.transpose(qkv[:, :, 0], (0, 2, 1, 3)) * scale
        k = jax.nn.softmax(jnp.transpose(qkv[:, :, 1], (0, 2, 1, 3)), axis=2)
        v = jnp.transpose(qkv[:, :, 2], (0, 2, 1, 3))
        context = jnp.einsum('bhld,bhle->bhde', k, v)
        out = jnp.einsum('bhde,bhld->bhle', context, q)
        out = jnp.transpose(out, (0, 2, 1, 3)).reshape(B, L, HEADS * DIM_HEAD)
        return jnp.einsum('blf,fd->bld', out, W_out) + b_out

    def _L1_ffn_ref(x, ln1_w, ln2_w, wq, wk, wv, wo, router_w, w1, w2, w3):
        import jax, jax.numpy as jnp
        import numpy as np
        B, T, C = (64, 384, 256)
        NH, NKV = (4, 2)
        HD = C // NH
        NREP = NH // NKV
        NE, TOPK = (8, 2)
        HID = int(8 / 3 * C)
        EPS_RMS = 1e-06

        def _rope_tables(t_len):
            inv_freq = 1.0 / 10000.0 ** (np.arange(0, HD, 2, dtype=np.float32) / HD)
            t = np.arange(t_len, dtype=np.float32)
            freqs = np.outer(t, inv_freq)
            emb = np.concatenate([freqs, freqs], axis=-1)
            return (jnp.asarray(np.cos(emb)), jnp.asarray(np.sin(emb)))

        def _rotate_half(x):
            h = x.shape[-1] // 2
            return jnp.concatenate([-x[..., h:], x[..., :h]], axis=-1)

        def _rmsnorm(v, w):
            return v * jax.lax.rsqrt(jnp.mean(v * v, axis=-1, keepdims=True) + EPS_RMS) * w
        Bx, Tx, Cx = x.shape
        h = _rmsnorm(x, ln1_w)
        q = (h @ wq.T).reshape(Bx, Tx, NH, HD).transpose(0, 2, 1, 3)
        k = (h @ wk.T).reshape(Bx, Tx, NKV, HD).transpose(0, 2, 1, 3)
        v = (h @ wv.T).reshape(Bx, Tx, NKV, HD).transpose(0, 2, 1, 3)
        cos, sin = _rope_tables(Tx)
        cos, sin = (cos[None, None], sin[None, None])
        q = q * cos + _rotate_half(q) * sin
        k = k * cos + _rotate_half(k) * sin
        k = jnp.repeat(k, NREP, axis=1)
        v = jnp.repeat(v, NREP, axis=1)
        scores = jnp.einsum('bhtd,bhsd->bhts', q, k) / jnp.sqrt(jnp.float32(HD))
        causal = jnp.tril(jnp.ones((Tx, Tx), dtype=bool))
        scores = jnp.where(causal[None, None], scores, jnp.float32(-1e+30))
        att = jax.nn.softmax(scores, axis=-1)
        y = jnp.einsum('bhts,bhsd->bhtd', att, v).transpose(0, 2, 1, 3).reshape(Bx, Tx, Cx)
        x = x + y @ wo.T
        flat = _rmsnorm(x, ln2_w).reshape(-1, Cx)
        probs = jax.nn.softmax(flat @ router_w.T, axis=-1)
        tp, ti = jax.lax.top_k(probs, TOPK)
        tp = tp / (jnp.sum(tp, axis=-1, keepdims=True) + 1e-09)
        weights = jnp.sum(tp[..., None] * jax.nn.one_hot(ti, NE, dtype=flat.dtype), axis=1)
        out = jnp.zeros_like(flat)
        for e in range(NE):
            hh = jax.nn.silu(flat @ w1[e].T) * (flat @ w3[e].T)
            out = out + weights[:, e:e + 1] * (hh @ w2[e].T)
        return x + out.reshape(Bx, Tx, Cx)
    edge_index = jnp.stack([src, dst])
    xn = _layernorm(x, axis=-1)
    x = x + _L0_gnn_ref(xn, L0_gnn_W1, L0_gnn_self_w1, L0_gnn_b1, L0_gnn_W2, L0_gnn_self_w2, L0_gnn_b2, edge_index, edge_type_8) + _L0_mix_ref(xn[None], L0_mix_Wqkv, L0_mix_bqkv, L0_mix_Wproj, L0_mix_bproj, L0_mix_temperature)[0]
    x = x + _L0_ffn_ref(_layernorm(x, axis=-1)[None], L0_ffn_router_w, L0_ffn_router_b, L0_ffn_W1, L0_ffn_b1, L0_ffn_W2, L0_ffn_b2)[0]
    xn = _layernorm(x, axis=-1)
    x = x + _L1_gnn_ref(xn, edge_index, edge_attr_4, edge_attr_16, L1_gnn_W_up0, L1_gnn_W_up1, L1_gnn_M1, L1_gnn_M2, L1_gnn_M3, L1_gnn_M4, L1_gnn_W_lin0, L1_gnn_W_lin1, L1_gnn_Wsc0, L1_gnn_Wsc1, L1_gnn_Wc0, L1_gnn_Wc1, L1_gnn_WB0, L1_gnn_WB1, L1_gnn_gamma0, L1_gnn_beta0, L1_gnn_gamma1) + _L1_mix_ref(xn[None], L1_mix_W_qkv, L1_mix_W_out, L1_mix_b_out)[0]
    x = x + _L1_ffn_ref(_layernorm(x, axis=-1)[None], L1_ffn_ln1_w, L1_ffn_ln2_w, L1_ffn_wq, L1_ffn_wk, L1_ffn_wv, L1_ffn_wo, L1_ffn_router_w, L1_ffn_w1, L1_ffn_w2, L1_ffn_w3)[0]
    return x

_drawn_inputs = setup_inputs


def setup_inputs(seed=0):
    import zlib

    import numpy as np

    out = dict(_drawn_inputs(seed))
    spreads = {'L0_gnn_b1': (0.0, 0.384),
     'L0_gnn_b2': (0.0, 0.8),
     'L0_mix_bqkv': (0.0, 0.8),
     'L0_mix_bproj': (0.0, 0.8),
     'L0_mix_temperature': (1.0, 0.6),
     'L1_gnn_gamma0': (1.0, 0.6),
     'L1_gnn_beta0': (0.0, 0.8),
     'L1_gnn_gamma1': (1.0, 0.6),
     'L1_mix_b_out': (0.0, 0.8),
     'L1_ffn_ln1_w': (1.0, 0.6),
     'L1_ffn_ln2_w': (1.0, 0.6)}
    factors = {'L0_mix_Wqkv': 8.0,
     'L0_mix_Wproj': 8.0,
     'L0_ffn_router_w': 8.0,
     'L0_ffn_router_b': 8.0,
     'L0_ffn_W1': 8.0,
     'L0_ffn_b1': 8.0,
     'L0_ffn_W2': 8.0,
     'L0_ffn_b2': 8.0,
     'L1_gnn_W_lin0': 3.807,
     'L1_gnn_Wsc0': 8.0,
     'L1_gnn_Wsc1': 8.0,
     'L1_gnn_Wc0': 4.095,
     'L1_gnn_WB0': 3.889,
     'L1_mix_W_qkv': 2.871,
     'L1_mix_W_out': 2.877,
     'L1_ffn_wq': 8.0,
     'L1_ffn_wk': 8.0,
     'L1_ffn_wv': 8.0,
     'L1_ffn_wo': 8.0,
     'L1_ffn_router_w': 8.0,
     'L1_ffn_w1': 8.0,
     'L1_ffn_w2': 8.0,
     'L1_ffn_w3': 8.0}
    for name, (base, spread) in spreads.items():
        noise = np.random.default_rng([zlib.crc32(name.encode()), seed]).standard_normal(out[name].shape)
        drawn = base * np.exp(spread * noise) if base else spread * noise
        out[name] = jnp.asarray(drawn.astype(out[name].dtype))
    for name, factor in factors.items():
        out[name] = (out[name] * factor).astype(out[name].dtype)
    return out
```

```python
from contextlib import ExitStack

import numpy as np
import concourse.bass as bass
from concourse import mybir

F32 = mybir.dt.float32
I32 = mybir.dt.int32
BF16 = mybir.dt.bfloat16
ALU = mybir.AluOpType
ACT = mybir.ActivationFunctionType
AX = mybir.AxisListType

N = 625
P = 125
NT = N // P
D = 256
E = 20000
ET = 160
EP = ET * 128
GROUP = 4
BUFS = 4
GROUPS = ET // GROUP
ITER = BUFS * GROUP
LOOPS = ET // ITER
R = 8
PASSES = 3
CHUNKS = NT + 1
H0, HD0 = 8, 32
E0, HID0 = 32, 64
C = 64
H1, HD1 = 4, 32
NH, NKV, HD = 4, 2, 64
NE = 8
HID = 682
HC = 114
NC = 6
TOP = 2
WORK = (TOP * N + NE * 127) // 128
TAYLOR = H0 // 2
HALVES = ((0, 313), (313, N))

ROWS = {}
_at = 0
for _name, _n in [("gnn_b1", D), ("gnn_b2", D), ("bqkv", 768), ("bproj", D), ("temp", H0),
                  ("router_b0", E0), ("b_out", D), ("ln1", D), ("ln2", D)]:
    ROWS[_name] = (_at, _n)
    _at += _n
NROWS = _at


class Kernel:

    def __init__(self):
        self.sem, self.buf = {}, {}
        self.dve_n = [0]


class Signal:

    def __init__(self, sem, base):
        self.sem, self.base = sem, base


class Chain:

    def __init__(self, eng, sem, n):
        self.eng, self.sem, self.n = eng, sem, n

    def step(self, instruction):
        instruction.then_inc(self.sem, 1)
        self.n[0] += 1
        self.eng.wait_ge(self.sem, self.n[0])


def nodes(t):
    return slice(t * P, (t + 1) * P)


def load_all(nc, K, A):
    S, B = K.sem, K.buf

    @K.block.sync
    def _(sp):
        sp.dma_start(B["x"][:], A["x"].rearrange("(t p) d -> p t d", p=P)).then_inc(S["x_loaded"], 16)
        sp.dma_start(B["rows"][:], A["rows"].partition_broadcast(P)).then_inc(S["rows_loaded"], 16)
        sp.dma_start(B["eint"][:], A["eint"]).then_inc(S["eint_loaded"], 16)
        sp.dma_start(B["dst_rows"][:], A["dst_rows"]).then_inc(S["eint_loaded"], 16)
        for c in range(2):
            sp.dma_start(B["W"][:, c, :, :], A["W1"][:, 128 * c:128 * c + 128, :].rearrange("r p n -> p r n")).then_inc(S["w1_loaded"], 16)
        sp.dma_start(B["self1"][:], A["self1"].rearrange("(c p) n -> p c n", p=128)).then_inc(S["w1_loaded"], 16)
        sp.dma_start(B["self2"][:], A["self2"].rearrange("(c p) n -> p c n", p=128)).then_inc(S["w2_loaded"], 16)
        sp.dma_start(B["wqkv0"][:], A["wqkv0"].rearrange("(c p) n -> p c n", p=128)).then_inc(S["mix0_loaded"], 16)
        sp.dma_start(B["wproj0"][:], A["wproj0"].rearrange("(c p) n -> p c n", p=128)).then_inc(S["mix0_loaded"], 16)
        sp.dma_start(B["router0"][:], A["router0"].rearrange("(c p) n -> p c n", p=128)).then_inc(S["ffn0_loaded"], 16)
        sp.dma_start(B["f1b"][:], A["f1b"]).then_inc(S["ffn0_loaded"], 16)
        sp.dma_start(B["f2b"][:], A["f2b"]).then_inc(S["ffn0_loaded"], 16)
        sp.dma_start(B["c64"][:], A["c64"]).then_inc(S["gnn1_loaded"], 16)
        sp.dma_start(B["m4"][0:C, :], A["m4"]).then_inc(S["gnn1_loaded"], 16)
        sp.dma_start(B["m4"][C:2 * C, :], A["m4"]).then_inc(S["gnn1_loaded"], 16)
        sp.dma_start(B["sh"][:], A["sh"]).then_inc(S["gnn1_loaded"], 16)
        sp.dma_start(B["r"][0:32, :], A["rbf"]).then_inc(S["rbf_loaded"], 16)
        sp.dma_start(B["wqkv1"][:], A["wqkv1"].rearrange("(c p) n -> p c n", p=128)).then_inc(S["mix1_loaded"], 16)
        sp.dma_start(B["wout1"][:], A["wout1"]).then_inc(S["mix1_loaded"], 16)
        sp.dma_start(B["wattn"][:], A["wattn"].rearrange("(c p) n -> p c n", p=128)).then_inc(S["attn_loaded"], 16)
        sp.dma_start(B["wo"][:], A["wo"].rearrange("(c p) n -> p c n", p=128)).then_inc(S["attn_loaded"], 16)
        sp.dma_start(B["router1"][:], A["router1"].rearrange("(c p) n -> p c n", p=128)).then_inc(S["attn_loaded"], 16)
        sp.dma_start(B["rope"][:], A["rope"].rearrange("a (t p) n -> p a t n", p=P)).then_inc(S["attn_loaded"], 16)

    @K.block.gpsimd
    def _(pool):
        pool.memset(B["ident"][:], 0.0).then_inc(S["pool_chain"], 1)
        pool.memset(B["m123"][:], 0.0).then_inc(S["zeroed"], 1)
        pool.memset(B["taylor_a"][:], float(HD0) ** 0.5)
        pool.memset(B["causal"][:], 0.0).then_inc(S["pool_chain"], 1)
        pool.wait_ge(S["pool_chain"], 2)
        pool.affine_select(out=B["ident"][:], in_=B["ident"][:], compare_op=ALU.not_equal, fill=1.0, base=0,
                           pattern=[[-1, 128]], channel_multiplier=1).then_inc(S["consts"], 1)
        pool.affine_select(out=B["causal"][:, N - P:N], in_=B["causal"][:, N - P:N], compare_op=ALU.is_ge, fill=-1e30,
                           base=0, pattern=[[-1, P]], channel_multiplier=1).then_inc(S["consts"], 1)
        pool.iota(B["iota"][:], pattern=[[1, 2 * P]], base=0, channel_multiplier=0,
                  allow_small_or_imprecise_dtypes=True).then_inc(S["consts"], 1)

        pool.iota(B["count"][:], pattern=[[-1, E0]], base=E0, channel_multiplier=0,
                  allow_small_or_imprecise_dtypes=True).then_inc(S["consts"], 1)

    @K.block.scalar
    def _(act):
        act.wait_ge(S["zeroed"], 1)
        for g in range(2):
            act.dma_start(B["m123"][16 * g:16 * g + 16, 0, C * g:C * g + C], A["m1"]).then_inc(S["m123_loaded"], 16)
            act.dma_start(B["m123"][C * g:C * g + C, 1, C * g:C * g + C], A["m2"]).then_inc(S["m123_loaded"], 16)
            act.dma_start(B["m123"][C * g:C * g + C, 2, C * g:C * g + C], A["m3"]).then_inc(S["m123_loaded"], 16)


def row(K, name):
    at, n = ROWS[name]
    return K.buf["rows"][:, at:at + n]


def edge_indices(nc, K, PS):
    S, B = K.sem, K.buf
    cast = K.tmp("ei_f", [128, 3, ET])
    rows_f = K.tmp("ei_rows", [GROUPS, GROUP * 128])
    neg = K.tmp("ei_neg", [GROUPS, GROUP * 128])
    least = K.tmp("ei_least", [GROUPS, 1])
    most = K.tmp("ei_most", [GROUPS, 1])
    stat = K.tmp("ei_stat", [GROUPS, 3])
    past = K.tmp("ei_past", [GROUPS, 4])
    line = K.tmp("ei_line", [1, 3, GROUPS])
    flag = K.tmp("ei_flag", [1, 4])
    first = K.tmp("ei_first", [1, GROUPS])
    ones = K.tmp("ei_ones", [1, 128])
    stat_ps, first_ps = PS[0], PS[1]
    dve_sem, pe_sem = S["ei_dve"], S["ei_pe"]

    @K.block.vector
    def _(dve):
        ch = Chain(dve, S["dve_chain"], K.dve_n)
        dve.wait_ge(S["eint_loaded"], 32)
        ch.step(nc.vector.tensor_copy(rows_f[:], B["dst_rows"][:]))
        ch.step(nc.vector.tensor_reduce(most[:], rows_f[:], AX.X, ALU.max))
        ch.step(nc.vector.tensor_scalar(neg[:], rows_f[:], 0.0, 10000.0, ALU.is_lt, ALU.mult))
        ch.step(nc.vector.tensor_tensor(neg[:], neg[:], rows_f[:], ALU.add))
        ch.step(nc.vector.tensor_reduce(least[:], neg[:], AX.X, ALU.min))
        for k in range(1, NT):
            ch.step(nc.vector.tensor_scalar(past[:, k - 1:k], least[:], float(P * k), None, ALU.is_ge))
        ch.step(nc.vector.tensor_reduce(stat[:, 0:1], past[:], AX.X, ALU.add))
        ch.step(nc.vector.scalar_tensor_tensor(most[:], stat[:, 0:1], -float(P), most[:], ALU.mult, ALU.add))
        nc.vector.tensor_scalar(stat[:, 2:3], most[:], float(P), None, ALU.is_ge)
        nc.vector.tensor_scalar(stat[:, 1:2], most[:], float(2 * P), None, ALU.is_ge).then_inc(dve_sem, 1)
        ch.step(nc.vector.tensor_copy(cast[:], B["eint"][:]))
        nc.vector.tensor_copy(B["src_idx"][:], cast[:, 0, :])
        nc.vector.scalar_tensor_tensor(B["rel_idx"][:], cast[:, 1, :], float(N), cast[:, 0, :], ALU.mult, ALU.add)
        ch.step(nc.vector.memset(ones[:], 1.0))
        dve.wait_ge(pe_sem, 1)
        ch.step(nc.vector.tensor_copy(line[:], stat_ps[0:1, 0:3 * GROUPS].rearrange("p (a t) -> p a t", a=3)))
        ch.step(nc.vector.tensor_reduce(flag[:, 0:1], line[:, 1, :], AX.X, ALU.max))
        ch.step(nc.vector.tensor_scalar(flag[:, 1:2], flag[:, 0:1], -1.0, 1.0, ALU.mult, ALU.add))
        ch.step(nc.vector.tensor_scalar(first[:], line[:, 0, :], flag[:, 1:2], None, ALU.mult))
        nc.vector.tensor_scalar(B["spans"][:, 0, :], line[:, 2, :], flag[:, 0:1], None, ALU.max)
        for p in range(1, PASSES):
            nc.vector.memset(B["spans"][:, p, :], 1)
        nc.vector.tensor_scalar(B["npass"][:], flag[:, 0:1], float(PASSES - 1), 1.0, ALU.mult, ALU.add)
        nc.vector.tensor_scalar(B["chunk_at"][:, 0, :], first[:], float(D), None, ALU.mult)
        for p in range(1, PASSES):
            last = nc.vector.memset(B["chunk_at"][:, p, :], 2 * p * D)
        last.then_inc(dve_sem, 1)
        for p in range(1, PASSES):
            nc.vector.tensor_scalar(B["dst_rel"][:, p, :], cast[:, 2, :], -float(2 * P * p), None, ALU.add)
        dve.wait_ge(pe_sem, 2)
        nc.vector.scalar_tensor_tensor(B["dst_rel"][:, 0, :].rearrange("e (g k) -> e g k", k=GROUP),
                                       first_ps[:, 0:GROUPS].unsqueeze(2).to_broadcast([128, GROUPS, GROUP]), -float(P),
                                       cast[:, 2, :].rearrange("e (g k) -> e g k", k=GROUP), ALU.mult, ALU.add)

    @K.block.tensor
    def _(pe):
        pe.wait_ge(S["consts"], 4)
        pe.wait_ge(dve_sem, 1)
        for a in range(3):
            last = nc.tensor.transpose(stat_ps[0:1, GROUPS * a:GROUPS * (a + 1)], stat[:, a:a + 1], B["ident"][0:GROUPS, 0:GROUPS])
        last.then_inc(pe_sem, 1)
        pe.wait_ge(dve_sem, 2)
        nc.tensor.matmul(first_ps[:, 0:GROUPS], ones[:], first[:], start=True, stop=True).then_inc(pe_sem, 1)


def layer_norm(nc, K, PS, tag, x, xn, xnT):
    S, B = K.sem, K.buf
    st = K.tmp(f"{tag}_st", [P, NT, 6])
    mv = K.tmp(f"{tag}_mv", [P, NT, 2])
    var = K.tmp(f"{tag}_var", [P, NT])
    std = K.tmp(f"{tag}_std", [P, NT])
    rstd = K.tmp(f"{tag}_rstd", [P, NT])
    var_ready = K.shared("var_ready", 1)
    std_ready = K.shared("std_ready", 1)
    xn_ready = K.shared("normalised", NT)
    turned = K.shared("turned", NT)

    @K.block.vector
    def _(dve):
        ch = Chain(dve, S["dve_chain"], K.dve_n)
        dve.wait_ge(S["x_loaded"], 16)
        for t in range(NT):
            ch.step(nc.vector.bn_stats(st[:, t, :], x[:, t, :]))
        for t in range(NT):
            ch.step(nc.vector.bn_aggr(mv[:, t, :], st[:, t, :]))
        nc.vector.tensor_scalar(var[:], mv[:, :, 1], 1e-5, None, ALU.add).then_inc(var_ready.sem, 1)
        dve.wait_ge(std_ready.sem, std_ready.base + 1)
        ch.step(nc.vector.reciprocal(rstd[:], std[:]))
        for t in range(NT):
            nc.vector.tensor_scalar(xn[:, t, :], x[:, t, :], mv[:, t, 0:1], rstd[:, t:t + 1],
                                    ALU.subtract, ALU.mult).then_inc(xn_ready.sem, 1)

    @K.block.scalar
    def _(act):
        act.wait_ge(var_ready.sem, var_ready.base + 1)
        nc.scalar.activation(std[:], var[:], ACT.Sqrt).then_inc(std_ready.sem, 1)
        for t in range(NT):
            act.wait_ge(turned.sem, turned.base + t + 1)
            nc.scalar.copy(xnT[:, :, nodes(t)], PS[t][:, 0:2 * P].rearrange("p (c n) -> p c n", c=2))

    @K.block.tensor
    def _(pe):
        pe.wait_ge(S["consts"], 4)
        for t in range(NT):
            pe.wait_ge(xn_ready.sem, xn_ready.base + t + 1)
            for c in range(2):
                last = nc.tensor.transpose(PS[t][:, P * c:P * c + P], xn[:, t, 128 * c:128 * c + 128], B["ident"][0:P, 0:P])
            last.then_inc(turned.sem, 1)


def to_feature_major(nc, K, PS, tag, parts, out):
    B = K.buf
    turned = K.shared("turned", NT)

    @K.block.tensor
    def _(pe):
        for t in range(NT):
            for i, part in enumerate(parts(t)):
                last = nc.tensor.transpose(PS[t][:, P * i:P * i + P], part, B["ident"][0:P, 0:P])
            last.then_inc(turned.sem, 1)

    @K.block.scalar
    def _(act):
        for t in range(NT):
            act.wait_ge(turned.sem, turned.base + t + 1)
            k = len(parts(t))
            nc.scalar.copy(out[:, :, nodes(t)], PS[t][:, 0:k * P].rearrange("p (c n) -> p c n", c=k))


def rgcn_tables(nc, K, PS, tag, xT, W, self_w, loaded, table, bias, total):
    B = K.buf
    stage = K.tmp(f"{tag}_stage", [P, NT, R, D])
    made = K.shared("rows_made", (R // 2 + 1) * NT)
    stored = K.shared("rows_stored", 16 * NT)
    self_done = K.shared("self_done", NT)
    copied = [K.shared(f"rows_copied{i}", NT * R // 4) for i in range(2)]
    G = R // 2

    @K.block.tensor
    def _(pe):
        pe.wait_ge(loaded, 48)
        for t in range(NT):
            for g in range(G):
                n = t * G + g
                if n >= 4:
                    pe.wait_ge(copied[n % 2].sem, copied[n % 2].base + n // 2 - 1)
                for c in range(2):
                    last = nc.tensor.matmul(PS[n % 4][0:P, 0:2 * D], xT[:, c, nodes(t)],
                                            W[:, c, 2 * g:2 * g + 2, :].rearrange("p r d -> p (r d)"), start=(c == 0), stop=(c == 1))
                last.then_inc(made.sem, 1)
        for t in range(NT):
            if t >= 2:
                pe.wait_ge(self_done.sem, self_done.base + t - 1)
            for c in range(2):
                last = nc.tensor.matmul(PS[4 + t % 2][0:P, 0:D], xT[:, c, nodes(t)], self_w[:, c, :], start=(c == 0), stop=(c == 1))
            last.then_inc(made.sem, 1)

    @K.block.scalar
    def _(act):
        for n in range(0, NT * G, 2):
            act.wait_ge(made.sem, made.base + n + 1)
            t, g = n // G, n % G
            nc.scalar.copy(stage[:, t, 2 * g:2 * g + 2, :], PS[n % 4][0:P, 0:2 * D].rearrange("p (r d) -> p r d", r=2)).then_inc(copied[0].sem, 1)

    @K.block.vector
    def _(dve):
        for n in range(1, NT * G, 2):
            dve.wait_ge(made.sem, made.base + n + 1)
            t, g = n // G, n % G
            nc.vector.tensor_copy(stage[:, t, 2 * g:2 * g + 2, :], PS[n % 4][0:P, 0:2 * D].rearrange("p (r d) -> p r d", r=2)).then_inc(copied[1].sem, 1)
        for t in range(NT):
            dve.wait_ge(made.sem, made.base + NT * G + t + 1)
            nc.vector.tensor_tensor(total[:, t, :], PS[4 + t % 2][0:P, 0:D], bias, ALU.add).then_inc(self_done.sem, 1)

    @K.block.sync
    def _(sp):
        for t in range(NT):
            for c in range(2):
                sp.wait_ge(copied[c].sem, copied[c].base + (t + 1) * G // 2)
            sp.dma_start(table.rearrange("r n d -> n r d")[nodes(t)], stage[:, t, :, :]).then_inc(stored.sem, 16)
        sp.wait_ge(stored.sem, stored.base + 16 * NT)


def segments(eng, K, iteration, slots):
    n_pass = eng.value_load(K.buf["npass"][:], min_val=1, max_val=PASSES)
    for i in range(LOOPS):
        slots(i)
        iteration(0, i)
    with eng.Fori(1, PASSES) as p:
        with eng.If(p < n_pass):
            with eng.Fori(0, LOOPS) as i:
                iteration(p, i)
    return n_pass


def gathers(nc, K, pool, base, table, index, idx, got, free, filled, extra=None):
    S = K.sem

    def iteration(p, i):
        for b in range(BUFS):
            n = (p * LOOPS + i)
            pool.wait_ge(free[b], base + n + 1)
            pool.sem_inc(S["gate"], 1)
            nc.gpsimd.tensor_copy(idx[:, b, :], index[:, bass.ds(i * ITER + b * GROUP, GROUP)]).then_inc(S["idx_copied"], 1)
            pool.wait_ge(S["idx_copied"], (base + n) * BUFS + b + 1)
            pool.sem_inc(S["gate"], 1)
            for k in range(GROUP):
                nc.gpsimd.indirect_dma_start(
                    got[:, b, k, :], None, table,
                    bass.IndirectOffsetOnAxis(ap=idx[:, b, k:k + 1], axis=0)).then_inc(filled[b], 16)
            if extra is not None:
                extra(p, i, b)

    segments(pool, K, iteration, lambda slot: None)


def tile_scalar(a, p, at):
    return a[:, bass.ds(p, 1), bass.ds(at, 1)].rearrange("e a b -> e (a b)")


def group_place(K, pe, g):
    def value(a, most):
        return pe.value_load(a[:].rearrange("e a b -> e (a b)")[:, bass.ds(g, 1)], min_val=0, max_val=most)
    return value(K.buf["chunk_at"], (NT - 1) * D), value(K.buf["spans"], 1)


def add_group(nc, pe, sums, onehot, rows, place, done):
    at, spans = place
    with pe.If(spans > 0):
        for k in range(GROUP):
            nc.tensor.matmul(sums[0:P, bass.ds(at + D, D)], onehot(k)[:, P:2 * P], rows(k), start=False, stop=False, skip_group_check=True)
    for k in range(GROUP):
        last = nc.tensor.matmul(sums[0:P, bass.ds(at, D)], onehot(k)[:, 0:P], rows(k), start=False, stop=False, skip_group_check=True)
    last.then_inc(done, 1)


def rgcn_edges(nc, K, layer, table, total, relu, out, pieces):
    S, B = K.sem, K.buf
    tag = f"e{layer}"
    got = K.tmp(f"{tag}_got", [128, BUFS, GROUP, D])
    idx = K.tmp(f"{tag}_idx", [128, BUFS, GROUP], I32)
    onehot = K.tmp(f"{tag}_onehot", [128, BUFS, GROUP, 2 * P])
    sums = K.psum(f"{tag}_sums", [128, CHUNKS * D])
    free, filled, hot = ([S[f"{n}{b}"] for b in range(BUFS)] for n in ("free", "filled", "hot"))
    zeroed = K.shared("sums_zeroed", 1)

    def base_of(eng):
        return 0 if layer == 0 else eng.value_load(B["npass"][:], min_val=1, max_val=PASSES) * LOOPS

    @K.block.gpsimd
    def _(pool):
        gathers(nc, K, pool, base_of(pool), table, B["rel_idx"], idx, got, free, filled)

    @K.block.vector
    def _(dve):
        base = base_of(dve)
        nc.vector.memset(sums[:], 0.0).then_inc(zeroed.sem, 1)

        def iteration(p, i):
            for b in range(BUFS):
                dve.wait_ge(free[b], base + p * LOOPS + i + 1)
                for k in range(GROUP):
                    last = nc.vector.tensor_scalar(onehot[:, b, k, :], B["iota"][:], tile_scalar(B["dst_rel"], p, i * ITER + b * GROUP + k),
                                                   None, ALU.is_equal)
                last.then_inc(hot[b], 1)

        n_pass = segments(dve, K, iteration, pieces["dve"])
        for b in range(BUFS):
            dve.wait_ge(free[b], base + n_pass * LOOPS + 1)
        ch = Chain(dve, S["dve_chain"], K.dve_n)
        for t in range(NT):
            if relu:
                ch.step(nc.vector.tensor_tensor(total[:, t, :], sums[0:P, t * D:t * D + D], total[:, t, :], ALU.add))
                nc.vector.tensor_scalar(out[:, t, :], total[:, t, :], 0.0, None, ALU.max)
            else:
                nc.vector.tensor_tensor(out[:, t, :], sums[0:P, t * D:t * D + D], total[:, t, :], ALU.add)

    @K.block.scalar
    def _(act):
        for slot in range(LOOPS):
            pieces["act"](slot)

    @K.block.tensor
    def _(pe):
        base = base_of(pe)
        if layer == 0:
            for b in range(BUFS):
                pe.sem_inc(free[b], 1)
        pe.wait_ge(zeroed.sem, zeroed.base + 1)

        def iteration(p, i):
            for b in range(BUFS):
                place = group_place(K, pe, (p * LOOPS + i) * BUFS + b)
                pe.wait_ge(filled[b], (base + p * LOOPS + i + 1) * (16 * GROUP))
                pe.wait_ge(hot[b], base + p * LOOPS + i + 1)
                add_group(nc, pe, sums, lambda k: onehot[:, b, k, :], lambda k: got[:, b, k, :], place, free[b])

        segments(pe, K, iteration, pieces["pe"])


def taylor_qkv(nc, K, PS, qkT, v1, xT):
    S, B = K.sem, K.buf
    s2 = float(HD0) ** 0.5
    qkv = K.tmp("tq_qkv", [P, NT, 3 * D])
    sq = K.tmp("tq_sq", [P, NT, 2 * D])
    norm = K.tmp("tq_norm", [P, NT, 2 * H0])
    factor = K.tmp("tq_factor", [P, NT, 2 * H0])
    turned_out = K.new("tq_turned_out")
    made, evacuated, added, squared, summed, rooted, ready, turned = (
        K.new(f"tq_{n}") for n in ("made", "evacuated", "added", "squared", "summed", "rooted", "ready", "turned"))

    @K.block.tensor
    def _(pe):
        pe.wait_ge(S["mix0_loaded"], 32)
        for t in range(NT):
            if t >= 2:
                pe.wait_ge(evacuated, t - 1)
            for c in range(2):
                nc.tensor.matmul(PS[2 * (t % 2)][0:P, 0:512], xT[:, c, nodes(t)], B["wqkv0"][:, c, 0:512], start=(c == 0), stop=(c == 1))
            for c in range(2):
                last = nc.tensor.matmul(PS[2 * (t % 2) + 1][0:P, 0:D], xT[:, c, nodes(t)], B["wqkv0"][:, c, 512:768], start=(c == 0), stop=(c == 1))
            last.then_inc(made, 1)
        pe.wait_ge(ready, 1)
        for t in range(NT):
            if t >= 4:
                pe.wait_ge(turned_out, t - 3)
            for i in range(4):
                last = nc.tensor.transpose(PS[4 + t % 4][:, P * i:P * i + P], qkv[:, t, 128 * i:128 * i + 128], B["ident"][0:P, 0:P])
            last.then_inc(turned, 1)

    @K.block.vector
    def _(dve):
        ch = Chain(dve, S["dve_chain"], K.dve_n)
        dve.wait_ge(S["rows_loaded"], 16)
        bias = row(K, "bqkv")
        for t in range(NT):
            dve.wait_ge(made, t + 1)
            nc.vector.tensor_tensor(qkv[:, t, 0:512], PS[2 * (t % 2)][0:P, 0:512], bias[:, 0:512], ALU.add).then_inc(added, 1)
            nc.vector.tensor_tensor(qkv[:, t, 512:768], PS[2 * (t % 2) + 1][0:P, 0:D], bias[:, 512:768], ALU.add).then_inc(evacuated, 1)
        dve.wait_ge(squared, NT)
        nc.vector.tensor_reduce(norm[:].rearrange("p t h -> p (t h)"), sq[:].rearrange("p t (h d) -> p (t h) d", d=HD0), AX.X, ALU.add).then_inc(summed, 1)
        dve.wait_ge(rooted, 2)
        ch.step(nc.vector.tensor_scalar(norm[:], norm[:], 1e-12, None, ALU.max))
        ch.step(nc.vector.reciprocal(factor[:], norm[:]))
        temp = row(K, "temp").unsqueeze(1).to_broadcast([P, NT, H0])
        ch.step(nc.vector.scalar_tensor_tensor(factor[:, :, 0:H0], factor[:, :, 0:H0], s2, temp, ALU.mult, ALU.mult))
        ch.step(nc.vector.tensor_scalar(factor[:, :, H0:2 * H0], factor[:, :, H0:2 * H0], float(HD0) ** 0.25, None, ALU.mult))
        for t in range(NT):
            last = nc.vector.tensor_tensor(qkv[:, t, 0:512].rearrange("p (h d) -> p h d", d=HD0), qkv[:, t, 0:512].rearrange("p (h d) -> p h d", d=HD0),
                                           factor[:, t, :].unsqueeze(2).to_broadcast([P, 2 * H0, HD0]), ALU.mult)
        last.then_inc(ready, 1)
        nc.vector.memset(v1[:, :, :, 0:1], 1.0)
        for t in range(NT):
            nc.vector.tensor_copy(v1[:, t, :, 1:HD0 + 1], qkv[:, t, 512:768].rearrange("p (h d) -> p h d", d=HD0))

    @K.block.scalar
    def _(act):
        for t in range(NT):
            act.wait_ge(added, t + 1)
            nc.scalar.activation(sq[:, t, :], qkv[:, t, 0:512], ACT.Square).then_inc(squared, 1)
        act.wait_ge(summed, 1)
        nc.scalar.activation(norm[:, :, 0:H0], norm[:, :, 0:H0], ACT.Sqrt, scale=s2).then_inc(rooted, 1)
        nc.scalar.activation(norm[:, :, H0:2 * H0], norm[:, :, H0:2 * H0], ACT.Sqrt).then_inc(rooted, 1)
        for t in range(NT):
            act.wait_ge(turned, t + 1)
            nc.scalar.copy(qkT[:, :, nodes(t)], PS[4 + t % 4][:, 0:4 * P].rearrange("p (c n) -> p c n", c=4)).then_inc(turned_out, 1)


class Taylor:

    def __init__(self, nc, K, first, qkT, v1, sums):
        self.nc, self.K, self.first, self.qkT, self.v1, self.sums = nc, K, first, qkT, v1, sums
        self.w = K.tmp(f"ta{first}_w", [P, 2, NT, N])
        self.score = [K.psum(f"ta{first}_score{i}", [P, 512]) for i in range(2)]
        self.py = K.psum(f"ta{first}_py", [P, 512])
        self.scored, self.weighted = (K.shared(n, TAYLOR * NT * 2) for n in ("scored", "weighted"))
        self.summed, self.taken = (K.shared(n, TAYLOR) for n in ("summed", "taken"))

    def tiles(self, piece):
        return range(0, 3) if piece % 2 == 0 else range(3, NT)

    def pe(self, piece):
        nc, pe, K = self.nc, self.nc.tensor, self.K
        slot = piece // 2
        for m in self.tiles(piece):
            if slot < TAYLOR:
                h = self.first + slot
                at, blk = 32 * (h % 4), h // 4
                kT = self.qkT[at:at + HD0, 2 + blk, nodes(m)]
                for i, (lo, hi) in enumerate(HALVES):
                    n = (slot * NT + m) * 2 + i
                    if n >= 2:
                        pe.wait_ge(self.weighted.sem, self.weighted.base + n - 1)
                    nc.tensor.matmul(self.score[n % 2][:, 0:hi - lo], kT, self.qkT[at:at + HD0, blk, lo:hi], start=True, stop=True,
                                     tile_position=(at, 0)).then_inc(self.scored.sem, 1)
            if slot >= 1:
                j = slot - 1
                if m == 0:
                    pe.wait_ge(self.weighted.sem, self.weighted.base + 2 * NT * (j + 1))
                    if j >= 1:
                        pe.wait_ge(self.taken.sem, self.taken.base + j)
                for k in range(NT):
                    last = nc.tensor.matmul(self.py[:, m * (HD0 + 1):(m + 1) * (HD0 + 1)], self.w[:, j % 2, k, nodes(m)], self.v1[:, k, self.first + j, :],
                                            start=(k == 0), stop=(k == NT - 1))
                if m == NT - 1:
                    last.then_inc(self.summed.sem, 1)

    def act(self, piece):
        nc, act, K = self.nc, self.nc.scalar, self.K
        slot = piece // 2
        for m in self.tiles(piece) if slot < TAYLOR else ():
            for i, (lo, hi) in enumerate(HALVES):
                n = (slot * NT + m) * 2 + i
                act.wait_ge(self.scored.sem, self.scored.base + n + 1)
                nc.scalar.activation(self.w[:, slot % 2, m, lo:hi], self.score[n % 2][:, 0:hi - lo], ACT.Square,
                                     bias=K.buf["taylor_a"][:]).then_inc(self.weighted.sem, 1)
        if slot >= 1 and piece % 2 == 1:
            act.wait_ge(self.summed.sem, self.summed.base + slot)
            nc.scalar.copy(self.sums[:, :, self.first + slot - 1, :],
                           self.py[:, 0:NT * (HD0 + 1)].rearrange("p (t d) -> p t d", t=NT)).then_inc(self.taken.sem, 1)


def taylor_end(nc, K, PS, v1, sums, y):
    S, B = K.sem, K.buf
    a = float(HD0) ** 0.5
    const = K.tmp("te_const", [P, P])
    vs = K.tmp("te_vs", [P, H0, HD0 + 1])
    rn = K.tmp("te_rn", [P, NT, H0])
    vsum = K.new("te_vsum")

    @K.block.tensor
    def _(pe):
        pe.wait_ge(vsum, 1)
        for t in range(NT):
            last = nc.tensor.matmul(PS[0][0:P, 0:H0 * (HD0 + 1)], const[:], v1[:, t, :, :].rearrange("p h d -> p (h d)"), start=(t == 0), stop=(t == NT - 1))
        last.then_inc(vsum, 1)

    @K.block.vector
    def _(dve):
        ch = Chain(dve, S["dve_chain"], K.dve_n)
        nc.vector.memset(const[:], a * a).then_inc(vsum, 1)
        dve.wait_ge(vsum, 2)
        ch.step(nc.vector.tensor_copy(vs[:].rearrange("p h d -> p (h d)"), PS[0][0:P, 0:H0 * (HD0 + 1)]))
        for t in range(NT):
            last = nc.vector.tensor_tensor(sums[:, t], sums[:, t], vs[:], ALU.add)
        ch.step(last)
        ch.step(nc.vector.reciprocal(rn[:], sums[:, :, :, 0]))
        for t in range(NT):
            nc.vector.tensor_tensor(y[:, t, :].rearrange("p (h d) -> p h d", h=H0), sums[:, t, :, 1:HD0 + 1],
                                    rn[:, t, :].unsqueeze(2).to_broadcast([P, H0, HD0]), ALU.mult)


def project_add(nc, K, PS, tag, yT, W, loaded, adds, out):
    S = K.sem
    made = K.shared("projected", NT)

    @K.block.tensor
    def _(pe):
        pe.wait_ge(loaded[0], loaded[1])
        for t in range(NT):
            k = W.shape[1]
            for c in range(k):
                last = nc.tensor.matmul(PS[t][0:P, 0:D], yT[:, c, nodes(t)], W[:, c, :], start=(c == 0), stop=(c == k - 1))
            last.then_inc(made.sem, 1)

    @K.block.vector
    def _(dve):
        ch = Chain(dve, S["dve_chain"], K.dve_n)
        for t in range(NT):
            dve.wait_ge(made.sem, made.base + t + 1)
            src = PS[t][0:P, 0:D]
            for a in adds(t):
                ch.step(nc.vector.tensor_tensor(out[:, t, :], src, a, ALU.add))
                src = out[:, t, :]


def first_of(nc, ch, value, masked, score, best, count, width, out):
    ch.step(nc.vector.tensor_reduce(best[:], value[:], AX.X, ALU.max))
    ch.step(nc.vector.tensor_tensor(masked[:], value[:], best[:].unsqueeze(2).to_broadcast([P, NT, width]), ALU.is_equal))
    ch.step(nc.vector.tensor_tensor(score[:], masked[:], count[:, 0:width].unsqueeze(1).to_broadcast([P, NT, width]), ALU.mult))
    ch.step(nc.vector.tensor_reduce(best[:], score[:], AX.X, ALU.max))
    ch.step(nc.vector.tensor_tensor(out[:], score[:], best[:].unsqueeze(2).to_broadcast([P, NT, width]), ALU.is_equal))


def routed_ffn(nc, K, PS, x, xT, hidT, f2):
    S, B = K.sem, K.buf
    KC = E0 * HID0 // 128
    logits = K.tmp("rf_logits", [P, NT, E0])
    masked = K.tmp("rf_masked", [P, NT, E0])
    score = K.tmp("rf_score", [P, NT, E0])
    hot = K.tmp("rf_hot", [P, NT, E0])
    best = K.tmp("rf_best", [P, NT])
    hotT = K.tmp("rf_hotT", [E0, N])
    mask = K.tmp("rf_mask", [E0, N], BF16)
    sel = K.tmp("rf_sel", [E0, E0 * HID0], BF16)
    extra = K.tmp("rf_extra", [P, NT, D])
    routed, chosen, turned, copied, made, rectified, masked_out, summed, taken, selected = (
        K.new(f"rf_{n}") for n in ("routed", "chosen", "turned", "copied", "made", "rectified", "masked_out", "summed", "taken", "selected"))
    halves = HALVES
    f1 = B["W"][:].rearrange("p c r n -> p c (r n)")

    @K.block.gpsimd
    def _(pool):
        nc.gpsimd.memset(sel[:], 1.0).then_inc(selected, 1)
        pool.wait_ge(selected, 1)
        nc.gpsimd.affine_select(out=sel[:], in_=sel[:], compare_op=ALU.is_ge, fill=0.0, base=0,
                                pattern=[[1, E0 * HID0]], channel_multiplier=-HID0).then_inc(selected, 1)
        pool.wait_ge(selected, 2)
        nc.gpsimd.affine_select(out=sel[:], in_=sel[:], compare_op=ALU.is_ge, fill=0.0, base=HID0 - 1,
                                pattern=[[-1, E0 * HID0]], channel_multiplier=HID0).then_inc(selected, 1)

    @K.block.tensor
    def _(pe):
        pe.wait_ge(S["ffn0_loaded"], 64)
        for t in range(NT):
            for c in range(2):
                last = nc.tensor.matmul(PS[0][0:P, E0 * t:E0 * t + E0], xT[:, c, nodes(t)], B["router0"][:, c, :], start=(c == 0), stop=(c == 1))
        last.then_inc(routed, 1)
        pe.wait_ge(chosen, 1)
        for t in range(4):
            last = nc.tensor.transpose(PS[1][0:E0, P * t:P * t + P], hot[:, t, :], B["ident"][0:P, 0:P])
        last = nc.tensor.transpose(PS[2][0:E0, 0:P], hot[:, 4, :], B["ident"][0:P, 0:P])
        last.then_inc(turned, 1)
        pe.wait_ge(copied, 3)
        pe.wait_ge(selected, 3)
        for k in range(KC):
            for i, (lo, hi) in enumerate(halves):
                n = 2 * k + i
                if n >= 3:
                    pe.wait_ge(masked_out, n - 2)
                for c in range(2):
                    nc.tensor.matmul(PS[n % 3][:, 0:hi - lo], f1[:, c, 128 * k:128 * k + 128], xT[:, c, lo:hi], start=(c == 0), stop=(c == 1))
                nc.tensor.matmul(PS[3 + n % 3][:, 0:hi - lo], sel[:, 128 * k:128 * k + 128], mask[:, lo:hi], start=True, stop=True).then_inc(made, 1)
        pe.wait_ge(masked_out, 2 * KC)
        pe.wait_ge(S["f2_loaded"], 16)
        for t in range(NT):
            if t >= 2:
                pe.wait_ge(taken, t - 1)
            for k in range(KC):
                nc.tensor.matmul(PS[6 + t % 2][0:P, 0:D], hidT[:, k, nodes(t)], f2[:, k, :], start=(k == 0), stop=False)
            nc.tensor.matmul(PS[6 + t % 2][0:P, 0:D], hotT[:, nodes(t)], B["f2b"][:], start=False, stop=True).then_inc(summed, 1)

    @K.block.scalar
    def _(act):
        for k in range(KC):
            for i, (lo, hi) in enumerate(halves):
                n = 2 * k + i
                act.wait_ge(made, n + 1)
                nc.scalar.activation(hidT[:, k, lo:hi], PS[n % 3][:, 0:hi - lo], ACT.Relu, bias=B["f1b"][:, k:k + 1]).then_inc(rectified, 1)

    @K.block.vector
    def _(dve):
        ch = Chain(dve, S["dve_chain"], K.dve_n)
        dve.wait_ge(routed, 1)
        ch.step(nc.vector.tensor_tensor(logits[:], PS[0][0:P, 0:NT * E0].rearrange("p (t e) -> p t e", t=NT),
                                        row(K, "router_b0").unsqueeze(1).to_broadcast([P, NT, E0]), ALU.add))
        first_of(nc, ch, logits, masked, score, best, B["count"], E0, hot)
        dve.sem_inc(chosen, 1)
        dve.wait_ge(turned, 1)
        nc.vector.tensor_copy(hotT[:, 0:4 * P], PS[1][0:E0, 0:4 * P]).then_inc(copied, 1)
        nc.vector.tensor_copy(hotT[:, 4 * P:N], PS[2][0:E0, 0:P]).then_inc(copied, 1)
        dve.wait_ge(copied, 2)
        nc.vector.tensor_copy(mask[:], hotT[:]).then_inc(copied, 1)
        for k in range(KC):
            for i, (lo, hi) in enumerate(halves):
                n = 2 * k + i
                dve.wait_ge(rectified, n + 1)
                nc.vector.tensor_tensor(hidT[:, k, lo:hi], PS[3 + n % 3][:, 0:hi - lo], hidT[:, k, lo:hi], ALU.mult).then_inc(masked_out, 1)
        for t in range(NT):
            dve.wait_ge(summed, t + 1)
            nc.vector.tensor_scalar(extra[:, t, :], PS[6 + t % 2][0:P, 0:D], 0.0, None, ALU.max).then_inc(taken, 1)
            dve.wait_ge(taken, t + 1)
            nc.vector.tensor_tensor(x[:, t, :], x[:, t, :], extra[:, t, :], ALU.add)


def equivariant_tables(nc, K, PS, xn, hT, table):
    S, B = K.sem, K.buf
    stage = K.tmp("et_stage", [P, NT, 4, C])
    turned, copied, made, staged, stored = (K.new(f"et_{n}") for n in ("turned", "copied", "made", "staged", "stored"))

    def part(t, x):
        return xn[:, t, 0:C] if x == 0 else xn[:, t, C:D].rearrange("p (c x) -> p c x", x=3)[:, :, x - 1]

    @K.block.tensor
    def _(pe):
        pe.wait_ge(S["gnn1_loaded"], 64)
        for t in range(NT):
            for x in range(4):
                last = nc.tensor.transpose(PS[t][0:C, P * x:P * x + P], part(t, x), B["ident"][0:P, 0:P])
            last.then_inc(turned, 1)
        for t in range(NT):
            pe.wait_ge(copied, t + 1)
            for x in range(4):
                W = B["c64"][:, 0:C] if x == 0 else B["c64"][:, C:2 * C]
                last = nc.tensor.matmul(PS[t][0:P, C * x:C * x + C], hT[:, x, nodes(t)], W, start=True, stop=True)
            last.then_inc(made, 1)

    @K.block.scalar
    def _(act):
        for t in range(NT):
            act.wait_ge(turned, t + 1)
            nc.scalar.copy(hT[:, :, nodes(t)], PS[t][0:C, 0:4 * P].rearrange("p (c n) -> p c n", c=4)).then_inc(copied, 1)

    @K.block.vector
    def _(dve):
        for t in range(NT):
            dve.wait_ge(made, t + 1)
            nc.vector.tensor_copy(stage[:, t, :, :], PS[t][0:P, 0:D].rearrange("p (x c) -> p x c", x=4)).then_inc(staged, 1)

    @K.block.sync
    def _(sp):
        sp.wait_ge(staged, NT)
        sp.dma_start(table.rearrange("(t p) d -> p t d", p=P), stage[:].rearrange("p t x c -> p t (x c)")).then_inc(stored, 16)
        sp.wait_ge(stored, 16)


class EdgeNetwork:

    BLOCKS = EP // 1024

    def __init__(self, nc, K, r):
        self.nc, self.K, self.r = nc, K, r
        self.made = [K.new(f"en_made{b}") for b in range(2)]
        self.done = [K.new(f"en_done{b}") for b in range(2)]

    def pieces(self, tag, first, each):
        nc, K = self.nc, self.K
        ps = [K.psum(f"{tag}_en_ps{b}", [128, 512]) for b in range(2)]

        def blocks(slot):
            for at in range(first + slot * each, first + (slot + 1) * each):
                layer, block = at // self.BLOCKS, at % self.BLOCKS
                yield at % 2, at // 2, layer, slice(512 * block, 512 * block + 512)

        def pe(slot):
            if first == 0 and slot == 0:
                nc.tensor.wait_ge(K.sem["rbf_loaded"], 16)
                nc.tensor.wait_ge(K.sem["m123_loaded"], 96)
            for b, n, layer, cols in blocks(slot):
                rows_in = 32 if layer == 0 else 128
                if n >= 1:
                    nc.tensor.wait_ge(self.done[b], n)
                nc.tensor.matmul(ps[b][:], K.buf["m123"][0:rows_in, layer, :], self.r[0:rows_in, cols], start=True, stop=True).then_inc(self.made[b], 1)

        def act(slot):
            for b, n, layer, cols in blocks(slot):
                nc.scalar.wait_ge(self.made[b], n + 1)
                nc.scalar.activation(self.r[:, cols], ps[b][:], ACT.Silu).then_inc(self.done[b], 1)

        return pe, act


def equivariant_edges(nc, K, table, r, msg_nodes):
    S, B = K.sem, K.buf
    G = GROUP
    inv3 = float(1.0 / np.sqrt(np.float32(3.0)))
    got = K.tmp("ee_got", [128, BUFS, G, D])
    idx = K.tmp("ee_idx", [128, BUFS, G], I32)
    onehot = K.tmp("ee_onehot", [128, 2, G, 2 * P])
    rs = K.tmp("ee_rs", [128, 512])
    gs = K.tmp("ee_gs", [128, 2, G, D])
    prod = K.tmp("ee_prod", [128, 2, G, 3, C])
    u = K.tmp("ee_u", [128, 2, G, C])
    dot = K.tmp("ee_dot", [128, 2, G, C])
    first = K.tmp("ee_first", [128, 2, G, D])
    second = K.tmp("ee_second", [128, 2, G, D - C])
    sums = K.psum("ee_sums", [128, CHUNKS * D])
    tp = [K.psum(f"ee_tp{h}", [128, G * D]) for h in range(2)]
    free, filled = ([S[f"{n}{b}"] for b in range(BUFS)] for n in ("free", "filled"))
    hot, weights, used, units, scaled, steps = (K.new(f"ee_{n}") for n in ("hot", "weights", "used", "units", "scaled", "steps"))
    zeroed = K.shared("sums_zeroed", 1)
    STEPS = 7

    def start(eng):
        return eng.value_load(B["npass"][:], min_val=1, max_val=PASSES) * (2 * LOOPS)

    def messages_made(eng, base, n, b, back):
        n, b = (n, b - back) if b >= back else (n - 1, b - back + BUFS)
        if not isinstance(n, int) or n >= 0:
            eng.wait_ge(free[b], base + n + 2)

    def after(eng, sem, count):
        if not isinstance(count, int) or count > 0:
            eng.wait_ge(sem, count)

    @K.block.gpsimd
    def _(pool):
        gathers(nc, K, pool, start(pool), table, B["src_idx"], idx, got, free, filled)

    @K.block.scalar
    def _(act):
        base = start(act)

        def iteration(p, i):
            n = p * LOOPS + i
            for b in range(BUFS):
                h = b % 2
                if not isinstance(p, int):
                    act.wait_ge(weights, n * BUFS + b - 1)
                    nc.scalar.copy(rs[C * h:C * h + C, :], r[C * h:C * h + C, bass.ds(i * (BUFS // 2 * 512) + b // 2 * 512, 512)]).then_inc(units, 1)
                act.wait_ge(filled[b], (base + n + 1) * (16 * G))
                messages_made(act, base, n, b, 2)
                for k in range(G):
                    sh = B["sh"][:, bass.ds(i * ITER + b * G + k, 1), :].rearrange("e a b -> e (a b)")
                    for x in range(3):
                        nc.scalar.activation(prod[:, h, k, x, :], got[:, b, k, C * (x + 1):C * (x + 2)], ACT.Copy, scale=sh[:, x + 1:x + 2])
                    last = nc.scalar.activation(gs[:, h, k, :], got[:, b, k, :], ACT.Copy, scale=sh[:, 0:1])
                last.then_inc(scaled, 1)

        segments(act, K, iteration, lambda slot: None)

    @K.block.vector
    def _(dve):
        base = start(dve)
        nc.vector.memset(sums[:], 0.0).then_inc(zeroed.sem, 1)

        def iteration(p, i):
            for b in range(BUFS):
                h = b % 2
                n = p * LOOPS + i
                g = n * BUFS + b
                before = g * STEPS
                after(dve, used, g - 1)
                for k in range(G):
                    last = nc.vector.tensor_scalar(onehot[:, h, k, :], B["iota"][:], tile_scalar(B["dst_rel"], p, i * ITER + b * G + k), None, ALU.is_equal)
                last.then_inc(hot, 1)
                sv = B["sh"][:, bass.ds(i * ITER + b * G, G), 1:4].unsqueeze(3).to_broadcast([128, G, 3, C])
                w = tp[h][:].rearrange("e (k w c) -> e k w c", k=G, w=4)
                one = first[:, h, :, :].rearrange("e k (x c) -> e k x c", x=4)
                two = second[:, h, :, :].rearrange("e k (x c) -> e k x c", x=3)
                gv = gs[:, h, :, :].rearrange("e k (x c) -> e k x c", x=4)
                dve.wait_ge(weights, g + 1)
                dve.wait_ge(scaled, g + 1)
                nc.vector.tensor_tensor(u[:, h], w[:, :, 1, :], got[:, b, :, 0:C], ALU.mult).then_inc(steps, 1)
                nc.vector.tensor_tensor(dot[:, h], prod[:, h, :, 0, :], prod[:, h, :, 1, :], ALU.add).then_inc(steps, 1)
                nc.vector.tensor_tensor(one[:, :, 0, :], w[:, :, 0, :], gv[:, :, 0, :], ALU.mult).then_inc(steps, 1)
                dve.wait_ge(steps, before + 2)
                nc.vector.tensor_tensor(dot[:, h], dot[:, h], prod[:, h, :, 2, :], ALU.add).then_inc(steps, 1)
                nc.vector.tensor_tensor(two, u[:, h].unsqueeze(2).to_broadcast([128, G, 3, C]), sv, ALU.mult).then_inc(steps, 1)
                dve.wait_ge(steps, before + 4)
                nc.vector.scalar_tensor_tensor(dot[:, h], dot[:, h], inv3, w[:, :, 3, :], ALU.mult, ALU.mult).then_inc(steps, 1)
                nc.vector.tensor_tensor(one[:, :, 1:4, :], w[:, :, 2, :].unsqueeze(2).to_broadcast([128, G, 3, C]), gv[:, :, 1:4, :], ALU.mult).then_inc(steps, 1)
                dve.wait_ge(steps, before + STEPS)
                nc.vector.tensor_tensor(one[:, :, 0, :], one[:, :, 0, :], dot[:, h], ALU.add).then_inc(free[b], 1)

        n_pass = segments(dve, K, iteration, lambda slot: None)
        dve.wait_ge(used, n_pass * GROUPS)
        for t in range(NT):
            nc.vector.tensor_copy(msg_nodes[:, t, :], sums[0:P, t * D:t * D + D])

    @K.block.tensor
    def _(pe):
        base = start(pe)
        pe.wait_ge(zeroed.sem, zeroed.base + 1)

        def edge_weights(p, i, b):
            n, h = p * LOOPS + i, b % 2
            if isinstance(p, int):
                hidden = r[C * h:C * h + C, (i * BUFS + b) // 2 * 512:(i * BUFS + b) // 2 * 512 + 512]
            else:
                hidden = rs[C * h:C * h + C, :]
                pe.wait_ge(units, (n - LOOPS) * BUFS + b + 1)
            messages_made(pe, base, n, b, 2)
            for k in range(G):
                last = nc.tensor.matmul(tp[h][:, k * D:k * D + D], hidden[:, 128 * k:128 * k + 128], B["m4"][C * h:C * h + C, :],
                                        start=(k % 2 == 0), stop=True, tile_position=(C * h, 0), skip_group_check=True)
            last.then_inc(weights, 1)

        def add_up(n, b):
            h = b % 2
            at, spans = group_place(K, pe, n * BUFS + b)
            pe.wait_ge(hot, n * BUFS + b + 1)
            messages_made(pe, base, n, b, 0)
            with pe.If(spans > 0):
                for k in range(G):
                    for part, skip in ((first, 0), (second, C)):
                        nc.tensor.matmul(sums[0:P, bass.ds(at + D + skip, D - skip)], onehot[:, h, k, P:2 * P], part[:, h, k, :], start=False, stop=False, skip_group_check=True)
            for k in range(G):
                for part, skip in ((first, 0), (second, C)):
                    last = nc.tensor.matmul(sums[0:P, bass.ds(at + skip, D - skip)], onehot[:, h, k, 0:P], part[:, h, k, :], start=False, stop=False, skip_group_check=True)
            last.then_inc(used, 1)

        def iteration(p, i):
            for b in range(BUFS):
                edge_weights(p, i, b)
                n = p * LOOPS + i
                if b >= 1:
                    add_up(n, b - 1)
                elif not isinstance(n, int) or n >= 1:
                    add_up(n - 1, BUFS - 1)

        n_pass = segments(pe, K, iteration, lambda slot: None)
        add_up(n_pass * LOOPS - 1, BUFS - 1)


def equivariant_nodes(nc, K, PS, msgs, hT, x):
    S, B = K.sem, K.buf
    mT = K.tmp("eq_mT", [C, 4, N])
    A = K.tmp("eq_A", [C, 4, N])
    sq = K.tmp("eq_sq", [C, 3, N])
    vv = K.tmp("eq_vv", [C, N])
    p1 = K.tmp("eq_p1", [C, N])
    p2 = K.tmp("eq_p2", [C, N])
    Bt = K.tmp("eq_B", [C, 4, N])
    o = K.tmp("eq_o", [C, 4, N])
    st = K.tmp("eq_st", [C, NT, 6])
    mv = K.tmp("eq_mv", [C, 2])
    stats = K.tmp("eq_stats", [C, 2])
    std = K.tmp("eq_std", [C, 2])
    scale = K.tmp("eq_scale", [C, 2])
    vsum = K.tmp("eq_vsum", [C, 1])
    turned, copied, made, taken, squared, products, stats_ready, std_ready, normed, back = (
        K.new(f"eq_{n}") for n in ("turned", "copied", "made", "taken", "squared", "products", "stats_ready", "std_ready", "normed", "back"))
    made2, taken2 = K.new("eq_made2"), K.new("eq_taken2")
    halves = ((0, 313), (313, N))
    w0 = [B["c64"][:, 6 * C + i:6 * C + i + 1] for i in range(5)]
    w1 = [B["c64"][:, 6 * C + 5 + i:6 * C + 6 + i] for i in range(4)]
    gamma0, beta0, gamma1 = (B["c64"][:, 6 * C + 9 + i:6 * C + 10 + i] for i in range(3))
    sc = 6 * C + 12

    @K.block.tensor
    def _(pe):
        for t in range(NT):
            for y in range(4):
                last = nc.tensor.transpose(PS[t][0:C, P * y:P * y + P], msgs[:, t, C * y:C * y + C], B["ident"][0:P, 0:P])
            last.then_inc(turned, 1)
        pe.wait_ge(copied, NT)
        for y in range(4):
            W = B["c64"][:, 2 * C:3 * C] if y == 0 else B["c64"][:, 3 * C:4 * C]
            for i, (lo, hi) in enumerate(halves):
                n = 2 * y + i
                if n >= 3:
                    pe.wait_ge(taken, n - 2)
                nc.tensor.matmul(PS[5 + n % 3][0:C, 0:hi - lo], W, mT[:, y, lo:hi], start=True, stop=True).then_inc(made, 1)
        for y in range(4):
            W = B["c64"][:, 4 * C:5 * C] if y == 0 else B["c64"][:, 5 * C:6 * C]
            pe.wait_ge(products, y + 1)
            for i, (lo, hi) in enumerate(halves):
                n = 2 * y + i
                if n >= 4:
                    pe.wait_ge(taken2, n - 3)
                at = sc if y == 0 else sc + C
                nc.tensor.matmul(PS[n % 4][0:C, 0:hi - lo], W, Bt[:, y, lo:hi], start=True, stop=False)
                nc.tensor.matmul(PS[n % 4][0:C, 0:hi - lo], B["c64"][:, at:at + C], hT[:, y, lo:hi], start=False, stop=True).then_inc(made2, 1)
        pe.wait_ge(normed, 2)
        for t in range(NT):
            for y in range(4):
                last = nc.tensor.transpose(PS[t][0:P, C * y:C * y + C], o[:, y, nodes(t)], B["ident"][0:C, 0:C])
            last.then_inc(back, 1)

    @K.block.scalar
    def _(act):
        for t in range(NT):
            act.wait_ge(turned, t + 1)
            nc.scalar.copy(mT[:, :, nodes(t)], PS[t][0:C, 0:4 * P].rearrange("p (c n) -> p c n", c=4)).then_inc(copied, 1)
        for y in range(4):
            for i, (lo, hi) in enumerate(halves):
                n = 2 * y + i
                act.wait_ge(made, n + 1)
                nc.scalar.copy(A[:, y, lo:hi], PS[5 + n % 3][0:C, 0:hi - lo]).then_inc(taken, 1)
        act.wait_ge(taken, 8)
        nc.scalar.activation(sq[:], A[:, 1:4, :], ACT.Square).then_inc(squared, 1)
        for y in range(4):
            for i, (lo, hi) in enumerate(halves):
                n = 2 * y + i
                act.wait_ge(made2, n + 1)
                nc.scalar.copy(o[:, y, lo:hi], PS[n % 4][0:C, 0:hi - lo]).then_inc(taken2, 1)
        act.wait_ge(stats_ready, 2)
        nc.scalar.activation(std[:], stats[:], ACT.Sqrt).then_inc(std_ready, 1)

    @K.block.vector
    def _(dve):
        ch = Chain(dve, S["dve_chain"], K.dve_n)
        a0 = A[:, 0, :]
        dve.wait_ge(taken, 8)
        ch.step(nc.vector.tensor_scalar(p1[:], a0, w0[3], w0[1], ALU.mult, ALU.add))
        ch.step(nc.vector.tensor_tensor(p1[:], p1[:], a0, ALU.mult))
        ch.step(nc.vector.scalar_tensor_tensor(p1[:], p1[:], w0[0], a0, ALU.add, ALU.mult))
        ch.step(nc.vector.tensor_scalar(p2[:], a0, w0[4], w0[2], ALU.mult, ALU.add))
        dve.wait_ge(squared, 1)
        ch.step(nc.vector.tensor_tensor(vv[:], sq[:, 0, :], sq[:, 1, :], ALU.add))
        ch.step(nc.vector.tensor_tensor(vv[:], vv[:], sq[:, 2, :], ALU.add))
        ch.step(nc.vector.tensor_tensor(p2[:], p2[:], vv[:], ALU.mult))
        nc.vector.tensor_tensor(Bt[:, 0, :], p1[:], p2[:], ALU.add).then_inc(products, 1)
        dve.wait_ge(products, 1)
        ch.step(nc.vector.tensor_scalar(p1[:], a0, w1[2], w1[1], ALU.mult, ALU.add))
        ch.step(nc.vector.tensor_tensor(p1[:], p1[:], a0, ALU.mult))
        ch.step(nc.vector.scalar_tensor_tensor(p1[:], vv[:], w1[3], p1[:], ALU.mult, ALU.add))
        for y in range(1, 4):
            nc.vector.scalar_tensor_tensor(Bt[:, y, :], p1[:], w1[0], A[:, y, :], ALU.add, ALU.mult).then_inc(products, 1)
        dve.wait_ge(taken2, 8)
        for t in range(NT):
            ch.step(nc.vector.bn_stats(st[:, t, :], o[:, 0, nodes(t)]))
        ch.step(nc.vector.bn_aggr(mv[:], st[:]))
        nc.vector.tensor_scalar(stats[:, 0:1], mv[:, 1:2], 1e-5, None, ALU.add).then_inc(stats_ready, 1)
        ch.step(nc.vector.scalar_tensor_tensor(sq[:].rearrange("c x n -> c (x n)"), o[:, 1:4, :].rearrange("c x n -> c (x n)"), 1.0 / (3.0 * N),
                                               o[:, 1:4, :].rearrange("c x n -> c (x n)"), ALU.mult, ALU.mult, accum_out=vsum[:]))
        nc.vector.tensor_scalar(stats[:, 1:2], vsum[:], 1e-5, None, ALU.add).then_inc(stats_ready, 1)
        dve.wait_ge(std_ready, 1)
        ch.step(nc.vector.reciprocal(scale[:], std[:]))
        ch.step(nc.vector.tensor_tensor(scale[:, 0:1], scale[:, 0:1], gamma0, ALU.mult))
        ch.step(nc.vector.tensor_tensor(scale[:, 1:2], scale[:, 1:2], gamma1, ALU.mult))
        ch.step(nc.vector.tensor_scalar(o[:, 0, :], o[:, 0, :], mv[:, 0:1], scale[:, 0:1], ALU.subtract, ALU.mult))
        nc.vector.tensor_scalar(o[:, 0, :], o[:, 0, :], beta0, None, ALU.add).then_inc(normed, 1)
        nc.vector.tensor_scalar(o[:, 1:4, :], o[:, 1:4, :], scale[:, 1:2], None, ALU.mult).then_inc(normed, 1)
        for t in range(NT):
            dve.wait_ge(back, t + 1)
            nc.vector.tensor_tensor(x[:, t, 0:C], PS[t][0:P, 0:C], x[:, t, 0:C], ALU.add)
            into = x[:, t, C:D].rearrange("p (c x) -> p x c", x=3)
            nc.vector.tensor_tensor(into, PS[t][0:P, C:D].rearrange("p (x c) -> p x c", x=3), into, ALU.add)


def linear_attention(nc, K, PS, xT, outT):
    S, B = K.sem, K.buf
    F = H1 * HD1
    q = K.tmp("la_q", [F, N])
    k = K.tmp("la_k", [F, N])
    kn = K.tmp("la_kn", [P, NT, F])
    v = K.tmp("la_v", [P, NT, F])
    context = K.tmp("la_context", [F, F])
    top = K.tmp("la_top", [F, 4])
    made, q_ready, k_ready, top_ready, exped, scaled, turned, kn_ready, vmade, v_ready, ctx_made, ctx_ready, out_made = (
        K.new(f"la_{n}") for n in ("made", "q_ready", "k_ready", "top_ready", "exped", "scaled", "turned", "kn_ready", "vmade", "v_ready",
                                   "ctx_made", "ctx_ready", "out_made"))
    halves = ((0, 313), (313, N))

    @K.block.tensor
    def _(pe):
        pe.wait_ge(S["mix1_loaded"], 32)
        for part in range(2):
            for i, (lo, hi) in enumerate(halves):
                for c in range(2):
                    last = nc.tensor.matmul(PS[2 * part + i][:, 0:hi - lo], B["wqkv1"][:, c, F * part:F * part + F], xT[:, c, lo:hi], start=(c == 0), stop=(c == 1))
                last.then_inc(made, 1)
        for t in range(NT):
            bank, at = (PS[4], F * t) if t < 4 else (PS[5], 0)
            for c in range(2):
                last = nc.tensor.matmul(bank[0:P, at:at + F], xT[:, c, nodes(t)], B["wqkv1"][:, c, 2 * F:3 * F], start=(c == 0), stop=(c == 1))
        last.then_inc(vmade, 1)
        pe.wait_ge(scaled, 1)
        for t in range(NT):
            bank, at = (PS[6], F * t) if t < 4 else (PS[7], 0)
            last = nc.tensor.transpose(bank[0:P, at:at + F], k[:, nodes(t)], B["ident"][:])
        last.then_inc(turned, 1)
        pe.wait_ge(kn_ready, 2)
        pe.wait_ge(v_ready, 2)
        for t in range(NT):
            last = nc.tensor.matmul(PS[4][:, 0:F], kn[:, t, :], v[:, t, :], start=(t == 0), stop=(t == NT - 1))
        last.then_inc(ctx_made, 1)
        pe.wait_ge(q_ready, 2)
        pe.wait_ge(ctx_ready, H1)
        for i, (lo, hi) in enumerate(halves):
            nc.tensor.matmul(PS[i][:, 0:hi - lo], context[:], q[:, lo:hi], start=True, stop=True).then_inc(out_made, 1)

    @K.block.scalar
    def _(act):
        for i, (lo, hi) in enumerate(halves):
            act.wait_ge(made, i + 1)
            nc.scalar.activation(q[:, lo:hi], PS[i][:, 0:hi - lo], ACT.Copy, scale=float(HD1) ** -0.5).then_inc(q_ready, 1)
        act.wait_ge(top_ready, 1)
        nc.scalar.activation(k[:], k[:], ACT.Exp, bias=top[:, 1:2], accum_out=top[:, 2:3]).then_inc(exped, 1)
        act.wait_ge(turned, 1)
        nc.scalar.copy(kn[:, 0:4, :].rearrange("p t f -> p (t f)"), PS[6][0:P, 0:4 * F]).then_inc(kn_ready, 1)
        nc.scalar.copy(kn[:, 4, :], PS[7][0:P, 0:F]).then_inc(kn_ready, 1)
        for i, (lo, hi) in enumerate(halves):
            act.wait_ge(out_made, i + 1)
            nc.scalar.copy(outT[:, 0, lo:hi], PS[i][:, 0:hi - lo])

    @K.block.vector
    def _(dve):
        ch = Chain(dve, S["dve_chain"], K.dve_n)
        for i, (lo, hi) in enumerate(halves):
            dve.wait_ge(made, 3 + i)
            ch.step(nc.vector.tensor_copy(k[:, lo:hi], PS[2 + i][:, 0:hi - lo]))
        dve.wait_ge(vmade, 1)
        nc.vector.tensor_copy(v[:, 0:4, :].rearrange("p t f -> p (t f)"), PS[4][0:P, 0:4 * F]).then_inc(v_ready, 1)
        nc.vector.tensor_copy(v[:, 4, :], PS[5][0:P, 0:F]).then_inc(v_ready, 1)
        ch.step(nc.vector.tensor_reduce(top[:, 0:1], k[:], AX.X, ALU.max))
        nc.vector.tensor_scalar(top[:, 1:2], top[:, 0:1], -1.0, None, ALU.mult).then_inc(top_ready, 1)
        dve.wait_ge(exped, 1)
        ch.step(nc.vector.reciprocal(top[:, 3:4], top[:, 2:3]))
        nc.vector.tensor_scalar(k[:], k[:], top[:, 3:4], None, ALU.mult).then_inc(scaled, 1)
        ch.step(nc.vector.memset(context[:], 0.0))
        dve.wait_ge(ctx_made, 1)
        for h in range(H1):
            s = slice(HD1 * h, HD1 * h + HD1)
            nc.vector.tensor_copy(context[s, s], PS[4][s, s]).then_inc(ctx_ready, 1)


def rms_norm(nc, K, PS, tag, x, weight, out, outT):
    S, B = K.sem, K.buf
    ss = K.tmp(f"{tag}_ss", [P, NT])
    ms = K.tmp(f"{tag}_ms", [P, NT])
    std = K.tmp(f"{tag}_std", [P, NT])
    rstd = K.tmp(f"{tag}_rstd", [P, NT])
    ms_ready = K.shared("var_ready", 1)
    std_ready = K.shared("std_ready", 1)
    ready = K.shared("normalised", NT)
    turned = K.shared("turned", NT)

    @K.block.vector
    def _(dve):
        ch = Chain(dve, S["dve_chain"], K.dve_n)
        for t in range(NT):
            ch.step(nc.vector.scalar_tensor_tensor(out[:, t, :], x[:, t, :], 1.0, x[:, t, :], ALU.mult, ALU.mult, accum_out=ss[:, t:t + 1]))
        nc.vector.tensor_scalar(ms[:], ss[:], 1.0 / D, 1e-6, ALU.mult, ALU.add).then_inc(ms_ready.sem, 1)
        dve.wait_ge(std_ready.sem, std_ready.base + 1)
        ch.step(nc.vector.reciprocal(rstd[:], std[:]))
        for t in range(NT):
            nc.vector.scalar_tensor_tensor(out[:, t, :], x[:, t, :], rstd[:, t:t + 1], weight, ALU.mult, ALU.mult).then_inc(ready.sem, 1)

    @K.block.scalar
    def _(act):
        act.wait_ge(ms_ready.sem, ms_ready.base + 1)
        nc.scalar.activation(std[:], ms[:], ACT.Sqrt).then_inc(std_ready.sem, 1)
        for t in range(NT):
            act.wait_ge(turned.sem, turned.base + t + 1)
            nc.scalar.copy(outT[:, :, nodes(t)], PS[t][:, 0:2 * P].rearrange("p (c n) -> p c n", c=2))

    @K.block.tensor
    def _(pe):
        for t in range(NT):
            pe.wait_ge(ready.sem, ready.base + t + 1)
            for c in range(2):
                last = nc.tensor.transpose(PS[t][:, P * c:P * c + P], out[:, t, 128 * c:128 * c + 128], B["ident"][0:P, 0:P])
            last.then_inc(turned.sem, 1)


def attention_qkv(nc, K, PS, xT, qT, kT, v):
    S, B = K.sem, K.buf
    HQ = NH + NKV
    raw = K.tmp("aq_raw", [P, NT, HQ, HD])
    rot = K.tmp("aq_rot", [P, NT, HQ, HD])
    made, taken, v_taken, ready, turned, turned_out = (K.new(f"aq_{n}") for n in ("made", "taken", "v_taken", "ready", "turned", "turned_out"))

    @K.block.tensor
    def _(pe):
        pe.wait_ge(S["attn_loaded"], 64)
        for t in range(NT):
            if t >= 2:
                pe.wait_ge(taken, t - 1)
                pe.wait_ge(v_taken, t - 1)
            for c in range(2):
                last = nc.tensor.matmul(PS[t % 2][0:P, :], xT[:, c, nodes(t)], B["wattn"][:, c, :], start=(c == 0), stop=(c == 1))
            last.then_inc(made, 1)
        for t in range(NT):
            pe.wait_ge(ready, t + 1)
            if t >= 4:
                pe.wait_ge(turned_out, 2 * (t - 3))
            for b in range(2):
                nc.tensor.transpose(PS[2 + t % 4][:, P * b:P * b + P], rot[:, t, 2 * b:2 * b + 2, :].rearrange("p h d -> p (h d)"), B["ident"][0:P, 0:P])
            nc.tensor.transpose(PS[2 + t % 4][:, 2 * P:3 * P], rot[:, t, NH:HQ, :].rearrange("p h d -> p (h d)"), B["ident"][0:P, 0:P]).then_inc(turned, 1)

    @K.block.vector
    def _(dve):
        ch = Chain(dve, S["dve_chain"], K.dve_n)
        for t in range(NT):
            dve.wait_ge(made, t + 1)
            src = PS[t % 2][0:P, 0:HQ * HD].rearrange("p (h d) -> p h d", h=HQ)
            cos = B["rope"][:, 0, t, :].unsqueeze(1).to_broadcast([P, HQ, HD])
            low = B["rope"][:, 1, t, 0:HD // 2].unsqueeze(1).to_broadcast([P, HQ, HD // 2])
            high = B["rope"][:, 1, t, HD // 2:HD].unsqueeze(1).to_broadcast([P, HQ, HD // 2])
            ch.step(nc.vector.tensor_tensor(rot[:, t, :, 0:HD // 2], src[:, :, HD // 2:HD], low, ALU.mult))
            ch.step(nc.vector.tensor_tensor(rot[:, t, :, HD // 2:HD], src[:, :, 0:HD // 2], high, ALU.mult))
            nc.vector.tensor_tensor(raw[:, t, :, :], src, cos, ALU.mult).then_inc(taken, 1)
            dve.wait_ge(taken, t + 1)
            nc.vector.tensor_tensor(rot[:, t, :, :], rot[:, t, :, :], raw[:, t, :, :], ALU.add).then_inc(ready, 1)

    @K.block.scalar
    def _(act):
        for t in range(NT):
            act.wait_ge(made, t + 1)
            act.wait_ge(taken, t + 1)
            nc.scalar.copy(v[:, t, :], PS[t % 2][0:P, HQ * HD:512]).then_inc(v_taken, 1)
        for t in range(NT):
            act.wait_ge(turned, t + 1)
            nc.scalar.copy(qT[:, :, nodes(t)], PS[2 + t % 4][:, 0:2 * P].rearrange("p (b n) -> p b n", b=2)).then_inc(turned_out, 1)
            nc.scalar.copy(kT[:, nodes(t)], PS[2 + t % 4][:, 2 * P:3 * P]).then_inc(turned_out, 1)


def causal_attention(nc, K, qT, kT, v, y):
    S, B = K.sem, K.buf
    scores = K.tmp("ca_scores", [P, 2, N])
    probs = K.tmp("ca_probs", [P, 2, N])
    probsT = K.tmp("ca_probsT", [P, 2, NT, P])
    top = K.tmp("ca_top", [P, NH * NT, 4])
    ps = [K.psum(f"ca_s{i}", [P, 1024]) for i in range(2)]
    pt = [K.psum(f"ca_t{i}", [P, 512]) for i in range(2)]
    pt4 = K.psum("ca_t4", [P, 512])
    py = K.psum("ca_y", [P, 512])
    scored, masked, topped, exped, turned, copied, summed, normed = (
        K.new(f"ca_{n}") for n in ("scored", "masked", "topped", "exped", "turned", "copied", "summed", "normed"))
    units = [(h, t) for h in range(NH) for t in range(NT)]

    @K.block.tensor
    def _(pe):
        def score(n):
            h, t = units[n]
            at, width = HD * (h // 2), (t + 1) * P
            if n >= 2:
                pe.wait_ge(masked, n - 1)
            for lo in range(0, width, 512):
                hi = min(lo + 512, width)
                last = nc.tensor.matmul(ps[n % 2][:, lo:hi], qT[at:at + HD, h % 2, nodes(t)], kT[at:at + HD, lo:hi], start=True, stop=True, tile_position=(at, 0))
            last.then_inc(scored, 1)

        def turn(n):
            h, t = units[n]
            pe.wait_ge(exped, n + 1)
            if n >= 1:
                pe.wait_ge(copied, n)
            for s in range(t + 1):
                bank, at = (pt[n % 2], P * s) if s < 4 else (pt4, 0)
                last = nc.tensor.transpose(bank[:, at:at + P], probs[:, n % 2, nodes(s)], B["ident"][0:P, 0:P])
            last.then_inc(turned, 1)

        def value(n):
            h, t = units[n]
            pe.wait_ge(copied, n + 1)
            if n >= 1:
                pe.wait_ge(normed, n)
            for s in range(t + 1):
                last = nc.tensor.matmul(py[:, 0:HD], probsT[:, n % 2, s, :], v[:, s, HD * (h // 2):HD * (h // 2) + HD], start=(s == 0), stop=(s == t))
            last.then_inc(summed, 1)

        score(0)
        score(1)
        for n in range(len(units)):
            turn(n)
            if n + 2 < len(units):
                score(n + 2)
            if n >= 1:
                value(n - 1)
        value(len(units) - 1)

    @K.block.vector
    def _(dve):
        ch = Chain(dve, S["dve_chain"], K.dve_n)

        def finish(n):
            h, t = units[n]
            dve.wait_ge(exped, n + 1)
            ch.step(nc.vector.reciprocal(top[:, n, 3:4], top[:, n, 2:3]))
            dve.wait_ge(summed, n + 1)
            nc.vector.tensor_scalar(y[:, t, HD * h:HD * h + HD], py[:, 0:HD], top[:, n, 3:4], None, ALU.mult).then_inc(normed, 1)

        for n, (h, t) in enumerate(units):
            width = (t + 1) * P
            dve.wait_ge(scored, n + 1)
            if n >= 2:
                dve.wait_ge(exped, n - 1)
            nc.vector.scalar_tensor_tensor(scores[:, n % 2, 0:width], ps[n % 2][:, 0:width], float(HD) ** -0.5, B["causal"][:, N - width:N], ALU.mult, ALU.add).then_inc(masked, 1)
            dve.wait_ge(masked, n + 1)
            ch.step(nc.vector.tensor_reduce(top[:, n, 0:1], scores[:, n % 2, 0:width], AX.X, ALU.max))
            nc.vector.tensor_scalar(top[:, n, 1:2], top[:, n, 0:1], -1.0, None, ALU.mult).then_inc(topped, 1)
            if n >= 2:
                finish(n - 2)
        finish(len(units) - 2)
        finish(len(units) - 1)

    @K.block.scalar
    def _(act):
        def copy_turned(n):
            t = units[n][1]
            act.wait_ge(turned, n + 1)
            if n >= 2:
                act.wait_ge(summed, n - 1)
            k = min(t + 1, 4)
            last = nc.scalar.copy(probsT[:, n % 2, 0:k, :].rearrange("p s n -> p (s n)"), pt[n % 2][:, 0:k * P])
            if t == 4:
                last = nc.scalar.copy(probsT[:, n % 2, 4, :], pt4[:, 0:P])
            last.then_inc(copied, 1)

        for n, (h, t) in enumerate(units):
            width = (t + 1) * P
            act.wait_ge(topped, n + 1)
            if n >= 2:
                act.wait_ge(turned, n - 1)
            nc.scalar.activation(probs[:, n % 2, 0:width], scores[:, n % 2, 0:width], ACT.Exp, bias=top[:, n, 1:2], accum_out=top[:, n, 2:3]).then_inc(exped, 1)
            if n >= 1:
                copy_turned(n - 1)
        copy_turned(len(units) - 1)


def load_experts(nc, K, A, w13, w2):
    @K.block.sync
    def _(sp):
        for e in range(NE):
            for j, w in enumerate((A["e1"], A["e3"])):
                at = (2 * e + j) * 2 * HID
                sp.dma_start(w13[:, at:at + 2 * HID].rearrange("p (c n) -> p c n", c=2), w[e].rearrange("(c p) n -> p c n", p=128)).then_inc(K.sem["experts_loaded"], 16)
            at = e * NC * D
            sp.dma_start(w2[:, at:at + (NC - 1) * D].rearrange("p (c d) -> p c d", d=D),
                         A["e2"][e, 0:(NC - 1) * HC, :].rearrange("(c p) d -> p c d", p=HC)).then_inc(K.sem["experts_loaded"], 16)
            sp.dma_start(w2[0:HID - (NC - 1) * HC, at + (NC - 1) * D:at + NC * D], A["e2"][e, (NC - 1) * HC:HID, :]).then_inc(K.sem["experts_loaded"], 16)


def dispatch(nc, K, PS, xT, flat, flat_rows, share, slots, token_of, expert_of):
    S, B = K.sem, K.buf
    names = "logits masked score rest both rank full place inner".split()
    logits, masked, score, rest, both, rank, full, place, inner = (K.tmp(f"di_{n}", [P, NT, NE]) for n in names)
    pick = K.tmp("di_pick", [P, TOP, NT, NE])
    chosen = K.tmp("di_chosen", [P, TOP, NT, NE])
    best = K.tmp("di_best", [P, NT])
    total = K.tmp("di_total", [P, NT])
    tile = K.tmp("di_tile", [P, TOP, NT])
    where = K.tmp("di_where", [P, TOP, NT])
    upto = K.tmp("di_upto", [P, NT + 1, NE])
    tiles = K.tmp("di_tiles", [P, NE])
    base = K.tmp("di_base", [P, NE + 1])
    begun = K.tmp("di_begun", [1, WORK, NE - 1])
    expert = K.tmp("di_expert", [1, WORK])
    node = K.tmp("di_node", [P, NT])
    before = K.tmp("di_before", [P, P])
    ones = K.tmp("di_ones", [P, P])
    in_tile = K.tmp("di_in_tile", [P, TOP, NT, WORK])
    at_place = K.tmp("di_at_place", [P, TOP, NT, 128])
    routed, ready, exped, counting, counted, placing, placed, consts = (
        K.new(f"di_{n}") for n in ("routed", "ready", "exped", "counting", "counted", "placing", "placed", "consts"))

    @K.block.sync
    def _(sp):
        sp.dma_start(flat_rows.rearrange("(t p) d -> p t d", p=P), flat[:]).then_inc(S["flat_stored"], 16)
        sp.wait_ge(S["flat_stored"], 16)

    @K.block.gpsimd
    def _(pool):
        pool.iota(node[:], pattern=[[P, NT]], base=0, channel_multiplier=1, allow_small_or_imprecise_dtypes=True).then_inc(consts, 1)
        pool.memset(ones[:], 1.0).then_inc(consts, 1)
        pool.memset(before[:], 1.0).then_inc(consts, 1)
        pool.wait_ge(consts, 3)
        pool.affine_select(out=before[:], in_=before[:], compare_op=ALU.is_ge, fill=0.0, base=-1,
                           pattern=[[1, P]], channel_multiplier=-1).then_inc(consts, 1)

    @K.block.tensor
    def _(pe):
        for t in range(NT):
            for c in range(2):
                last = nc.tensor.matmul(PS[0][0:P, NE * t:NE * t + NE], xT[:, c, nodes(t)], B["router1"][:, c, :], start=(c == 0), stop=(c == 1))
        last.then_inc(routed, 1)
        pe.wait_ge(consts, 4)
        pe.wait_ge(counting, 1)
        chosen_both = both[:].rearrange("p t e -> p (t e)")
        nc.tensor.matmul(PS[1][0:P, 0:NT * NE], before[:], chosen_both, start=True, stop=True)
        nc.tensor.matmul(PS[2][0:P, 0:NT * NE], ones[:], chosen_both, start=True, stop=True).then_inc(counted, 1)
        pe.wait_ge(placing, 1)
        for s in range(TOP):
            for t in range(NT):
                last = nc.tensor.matmul(PS[3][:, 0:WORK], at_place[:, s, t, :], in_tile[:, s, t, :], start=(s == 0 and t == 0),
                                        stop=(s == TOP - 1 and t == NT - 1))
        last.then_inc(placed, 1)

    @K.block.scalar
    def _(act):
        act.wait_ge(ready, 1)
        nc.scalar.activation(logits[:], logits[:], ACT.Exp).then_inc(exped, 1)

    @K.block.vector
    def _(dve):
        ch = Chain(dve, S["dve_chain"], K.dve_n)

        def wide(a):
            return a[:].unsqueeze(2).to_broadcast([P, NT, NE])

        def both_choices(a):
            return a[:].rearrange("p t e -> p (t e)").unsqueeze(1).to_broadcast([P, TOP, NT * NE])

        def of_choice(a, out):
            ch.step(nc.vector.tensor_tensor(chosen[:].rearrange("p s t e -> p s (t e)"), pick[:].rearrange("p s t e -> p s (t e)"), both_choices(a), ALU.mult))
            ch.step(nc.vector.tensor_reduce(out[:].rearrange("p s t -> p (s t)"), chosen[:].rearrange("p s t e -> p (s t) e"), AX.X, ALU.add))

        dve.wait_ge(routed, 1)
        ch.step(nc.vector.tensor_copy(logits[:], PS[0][0:P, 0:NT * NE].rearrange("p (t e) -> p t e", t=NT)))
        ch.step(nc.vector.tensor_reduce(best[:], logits[:], AX.X, ALU.max))
        nc.vector.tensor_tensor(logits[:], logits[:], wide(best), ALU.subtract).then_inc(ready, 1)
        dve.wait_ge(exped, 1)
        ch.step(nc.vector.tensor_reduce(total[:], logits[:], AX.X, ALU.add))
        ch.step(nc.vector.reciprocal(total[:], total[:]))
        ch.step(nc.vector.tensor_tensor(logits[:], logits[:], wide(total), ALU.mult))
        first_of(nc, ch, logits, masked, score, best, B["count"], NE, pick[:, 0])
        ch.step(nc.vector.scalar_tensor_tensor(rest[:], pick[:, 0], -2.0, logits[:], ALU.mult, ALU.add))
        first_of(nc, ch, rest, masked, score, best, B["count"], NE, pick[:, 1])
        nc.vector.tensor_tensor(both[:], pick[:, 0], pick[:, 1], ALU.add).then_inc(counting, 1)
        of_choice(logits, share)
        ch.step(nc.vector.tensor_tensor(total[:], share[:, 0, :], share[:, 1, :], ALU.add))
        ch.step(nc.vector.tensor_scalar(total[:], total[:], 1e-9, None, ALU.add))
        ch.step(nc.vector.reciprocal(total[:], total[:]))
        nc.vector.tensor_tensor(share[:], share[:], total[:].unsqueeze(1).to_broadcast([P, TOP, NT]), ALU.mult)

        dve.wait_ge(counted, 1)
        ch.step(nc.vector.memset(upto[:, 0, :], 0.0))
        for t in range(NT):
            ch.step(nc.vector.tensor_tensor(upto[:, t + 1, :], PS[2][0:P, NE * t:NE * t + NE], upto[:, t, :], ALU.add))
        ch.step(nc.vector.tensor_tensor(rank[:], PS[1][0:P, 0:NT * NE].rearrange("p (t e) -> p t e", t=NT), upto[:, 0:NT, :], ALU.add))
        ch.step(nc.vector.tensor_scalar(tiles[:], upto[:, NT, :], 0.0, None, ALU.is_gt))
        ch.step(nc.vector.tensor_scalar(full[:], rank[:], 128.0, None, ALU.is_ge))
        for k in range(1, NT):
            ch.step(nc.vector.scalar_tensor_tensor(tiles[:], upto[:, NT, :], 128.0 * k, tiles[:], ALU.is_gt, ALU.add))
        for k in range(2, NT):
            ch.step(nc.vector.scalar_tensor_tensor(full[:], rank[:], 128.0 * k, full[:], ALU.is_ge, ALU.add))
        ch.step(nc.vector.memset(base[:, 0:1], 0.0))
        for e in range(NE):
            ch.step(nc.vector.tensor_tensor(base[:, e + 1:e + 2], base[:, e:e + 1], tiles[:, e:e + 1], ALU.add))
        ch.step(nc.vector.tensor_tensor(place[:], full[:], base[:, 0:NE].unsqueeze(1).to_broadcast([P, NT, NE]), ALU.add))
        ch.step(nc.vector.scalar_tensor_tensor(inner[:], full[:], -128.0, rank[:], ALU.mult, ALU.add))
        of_choice(place, tile)
        of_choice(inner, where)
        counts = B["iota"][0:P, :]
        ch.step(nc.vector.tensor_tensor(in_tile[:].rearrange("p s t w -> p (s t) w"), tile[:].rearrange("p s t -> p (s t)").unsqueeze(2).to_broadcast([P, TOP * NT, WORK]),
                                        counts[:, 0:WORK].unsqueeze(1).to_broadcast([P, TOP * NT, WORK]), ALU.is_equal))
        for s in range(TOP):
            ch.step(nc.vector.tensor_tensor(in_tile[:, s], in_tile[:, s], node[:].unsqueeze(2).to_broadcast([P, NT, WORK]), ALU.mult))
        nc.vector.tensor_tensor(at_place[:].rearrange("p s t q -> p (s t) q"), where[:].rearrange("p s t -> p (s t)").unsqueeze(2).to_broadcast([P, TOP * NT, 128]),
                                counts[:, 0:128].unsqueeze(1).to_broadcast([P, TOP * NT, 128]), ALU.is_equal).then_inc(placing, 1)
        ch.step(nc.vector.memset(slots[:], 0))
        nc.vector.scalar_tensor_tensor(slots[0:P, :], tile[:].rearrange("p s t -> p (s t)"), 128.0, where[:].rearrange("p s t -> p (s t)"), ALU.mult, ALU.add)
        ch.step(nc.vector.tensor_tensor(begun[:], base[0:1, 1:NE].unsqueeze(1).to_broadcast([1, WORK, NE - 1]),
                                        counts[0:1, 0:WORK].unsqueeze(2).to_broadcast([1, WORK, NE - 1]), ALU.is_le))
        ch.step(nc.vector.tensor_reduce(expert[:], begun[:], AX.X, ALU.add))
        nc.vector.tensor_copy(expert_of[:], expert[:])
        dve.wait_ge(placed, 1)
        nc.vector.tensor_copy(token_of[:], PS[3][:, 0:WORK])


def mixture(nc, K, w13, w2, flat_rows, results, share, slots, token_of, expert_of, x, out):
    S, B = K.sem, K.buf
    RING = 4
    got = K.tmp("mx_got", [128, RING, D])
    fT = K.tmp("mx_fT", [128, 2, 2, 128])
    gate = K.tmp("mx_gate", [128, HID])
    hid = K.tmp("mx_hid", [128, 2, HID])
    hidT = K.tmp("mx_hidT", [HC, NC, 128])
    y = K.tmp("mx_y", [128, 2, D])
    a, b = K.psum("mx_a", [128, 1024]), K.psum("mx_b", [128, 1024])
    ta, tb = K.psum("mx_ta", [128, 512]), K.psum("mx_tb", [128, 512])
    down = [K.psum(f"mx_down{i}", [128, 512]) for i in range(2)]
    got_sem = [K.new(f"mx_got{i}") for i in range(RING)]
    stored = [K.new(f"mx_stored{i}") for i in range(2)]
    made1, made3, gated, multiplied, turned, fT_ready, hid_turned, hidT_a, hidT_b, summed, taken, back = (
        K.new(f"mx_{n}") for n in ("made1", "made3", "gated", "multiplied", "turned", "fT_ready", "hid_turned", "hidT_a", "hidT_b",
                                   "summed", "taken", "back"))
    last_rows = HID - (NC - 1) * HC

    def size(c):
        return HC if c < NC - 1 else last_rows

    @K.block.gpsimd
    def _(pool):
        for w in range(WORK):
            if w >= RING:
                pool.wait_ge(turned, w - RING + 1)
            nc.gpsimd.indirect_dma_start(got[:, w % RING, :], None, flat_rows,
                                         bass.IndirectOffsetOnAxis(ap=token_of[:, w:w + 1], axis=0)).then_inc(got_sem[w % RING], 16)
        for i in range(2):
            pool.wait_ge(stored[i], 16 * ((WORK + 1 - i) // 2))
        for i in range(TOP * NT):
            nc.gpsimd.indirect_dma_start(w13[:, i * D:(i + 1) * D], None, results,
                                         bass.IndirectOffsetOnAxis(ap=slots[:, i:i + 1], axis=0)).then_inc(back, 16)

    @K.block.sync
    def _(sp):
        for w in range(WORK):
            sp.wait_ge(taken, w + 1)
            sp.dma_start(results[128 * w:128 * w + 128, :], y[:, w % 2, :]).then_inc(stored[w % 2], 16)

    @K.block.tensor
    def _(pe):
        def up(w, j, e, bank, before, made):
            if w >= 1:
                pe.wait_ge(before, w)
            for lo, hi in ((0, 512), (512, HID)):
                for c in range(2):
                    last = nc.tensor.matmul(bank[:, lo:hi], fT[:, w % 2, c, :], w13[:, bass.ds(e * (4 * HID) + (2 * j + c) * HID + lo, hi - lo)],
                                            start=(c == 0), stop=(c == 1))
            last.then_inc(made, 1)

        def turn(w):
            if w >= 1:
                pe.wait_ge(fT_ready, w)
            pe.wait_ge(got_sem[w % RING], 16 * (w // RING + 1))
            for c in range(2):
                last = nc.tensor.transpose(tb[:, 256 + 128 * c:384 + 128 * c], got[:, w % RING, 128 * c:128 * c + 128], B["ident"][:])
            last.then_inc(turned, 1)

        def turn_hidden(w):
            pe.wait_ge(multiplied, w + 1)
            if w >= 1:
                pe.wait_ge(hidT_a, w)
                pe.wait_ge(hidT_b, w)
            for c in range(NC):
                bank, at = (ta, 128 * c) if c < 4 else (tb, 128 * (c - 4))
                last = nc.tensor.transpose(bank[0:size(c), at:at + 128], hid[:, w % 2, c * HC:c * HC + size(c)], B["ident"][:])
            last.then_inc(hid_turned, 1)

        def bring_down(w, e):
            pe.wait_ge(hidT_a, w + 1)
            pe.wait_ge(hidT_b, w + 1)
            if w >= 2:
                pe.wait_ge(taken, w - 1)
            for c in range(NC):
                last = nc.tensor.matmul(down[w % 2][:, 0:D], hidT[0:size(c), c, :], w2[0:size(c), bass.ds(e * (NC * D) + c * D, D)], start=(c == 0), stop=(c == NC - 1))
            last.then_inc(summed, 1)

        pe.wait_ge(S["experts_loaded"], 16 * 4 * NE)
        turn(0)
        e = [pe.value_load(expert_of[:, w:w + 1], min_val=0, max_val=NE - 1) for w in range(2)]
        for w in range(WORK):
            pe.wait_ge(fT_ready, w + 1)
            up(w, 0, e[w], a, gated, made1)
            if w >= 1:
                turn_hidden(w - 1)
            if w + 1 < WORK:
                turn(w + 1)
            up(w, 1, e[w], b, multiplied, made3)
            if w + 2 < WORK:
                e.append(pe.value_load(expert_of[:, w + 2:w + 3], min_val=0, max_val=NE - 1))
            if w >= 1:
                bring_down(w - 1, e[w - 1])
        turn_hidden(WORK - 1)
        bring_down(WORK - 1, e[WORK - 1])

    @K.block.scalar
    def _(act):
        def copy_hidden(w):
            act.wait_ge(hid_turned, w + 1)
            if w >= 1:
                act.wait_ge(summed, w)
            nc.scalar.copy(hidT[:, 0:4, :].rearrange("p c n -> p (c n)"), ta[0:HC, :]).then_inc(hidT_a, 1)

        for w in range(WORK):
            act.wait_ge(made1, w + 1)
            if w >= 1:
                act.wait_ge(multiplied, w)
            nc.scalar.activation(gate[:], a[:, 0:HID], ACT.Silu).then_inc(gated, 1)
            if w >= 1:
                copy_hidden(w - 1)
        copy_hidden(WORK - 1)

    @K.block.vector
    def _(dve):
        def copy_rows(w):
            dve.wait_ge(turned, w + 1)
            if w >= 2:
                dve.wait_ge(made3, w - 1)
            nc.vector.tensor_copy(fT[:, w % 2, :, :], tb[:, 256:512].rearrange("p (c n) -> p c n", c=2)).then_inc(fT_ready, 1)

        def copy_hidden(w):
            dve.wait_ge(hid_turned, w + 1)
            if w + 2 < WORK:
                dve.wait_ge(turned, w + 3)
            if w >= 1:
                dve.wait_ge(summed, w)
            nc.vector.tensor_copy(hidT[0:HC, 4, :], tb[0:HC, 0:128])
            nc.vector.tensor_copy(hidT[0:last_rows, 5, :], tb[0:last_rows, 128:256]).then_inc(hidT_b, 1)

        def take(w):
            dve.wait_ge(summed, w + 1)
            if w >= 2:
                dve.wait_ge(stored[w % 2], 16 * (w // 2))
            nc.vector.tensor_copy(y[:, w % 2, :], down[w % 2][:, 0:D]).then_inc(taken, 1)

        copy_rows(0)
        ch = Chain(dve, S["dve_chain"], K.dve_n)
        ch.step(nc.vector.tensor_tensor(out[:], x[:], out[:], ALU.add))
        for w in range(WORK):
            if w >= 1:
                copy_hidden(w - 1)
            if w + 1 < WORK:
                copy_rows(w + 1)
            dve.wait_ge(gated, w + 1)
            dve.wait_ge(made3, w + 1)
            if w >= 2:
                dve.wait_ge(hid_turned, w - 1)
            nc.vector.tensor_tensor(hid[:, w % 2, :], b[:, 0:HID], gate[:], ALU.mult).then_inc(multiplied, 1)
            if w >= 1:
                take(w - 1)
        copy_hidden(WORK - 1)
        take(WORK - 1)
        dve.wait_ge(back, 16 * TOP * NT)
        for s in range(TOP):
            for t in range(NT):
                last = nc.vector.scalar_tensor_tensor(out[:, t, :], w13[0:P, (s * NT + t) * D:(s * NT + t + 1) * D], share[:, s, t:t + 1], out[:, t, :], ALU.mult, ALU.add)
            ch.step(last)


def program(nc, A, out):
    with ExitStack() as whole:
        K = Kernel()
        S, B = K.sem, K.buf
        K.new = lambda name: whole.enter_context(nc.semaphore(name))
        for name in ("x_loaded rows_loaded eint_loaded w1_loaded w2_loaded mix0_loaded ffn0_loaded f2_loaded gnn1_loaded mix1_loaded attn_loaded "
                     "experts_loaded flat_stored gate idx_copied m123_loaded rbf_loaded zeroed pool_chain consts dve_chain act_chain ei_dve ei_pe").split():
            S[name] = K.new(name)

        signals = {}

        for n in ("free", "filled", "hot"):
            for b in range(BUFS):
                S[f"{n}{b}"] = K.new(f"{n}{b}")

        def shared(name, total):
            if name not in signals:
                signals[name] = [K.new(name), 0]
            sem, base = signals[name]
            signals[name][1] += total
            return Signal(sem, base)

        K.shared = shared

        def keep(name, shape, dt=F32):
            t = whole.enter_context(nc.sbuf_tensor(name, shape, dt))
            B[name] = t
            return t

        def dram(name, shape):
            return nc.dram_tensor(name, shape, F32).ap()

        keep("x", [P, NT, D])
        keep("rows", [P, NROWS])
        keep("ident", [128, 128])
        keep("causal", [P, N])
        keep("iota", [128, 2 * P])
        keep("count", [P, E0])
        keep("wattn", [128, 2, 512])
        keep("wo", [128, 2, D])
        keep("router1", [128, 2, NE])
        keep("rope", [P, 2, NT, HD])
        keep("actT", [128, 2, N])
        keep("h", [P, NT, D])
        graph = whole.enter_context(ExitStack())
        for name, shape, dt in (
                ("eint", [128, 3, ET], I32), ("dst_rows", [GROUPS, GROUP * 128], I32), ("src_idx", [128, ET], I32),
                ("rel_idx", [128, ET], I32), ("dst_rel", [128, PASSES, ET], F32), ("chunk_at", [1, PASSES, GROUPS], I32),
                ("npass", [1, 1], I32), ("spans", [1, PASSES, GROUPS], I32), ("router0", [128, 2, E0], F32),
                ("f1b", [128, E0 * HID0 // 128], F32), ("f2b", [E0, D], F32), ("c64", [C, 8 * C + 12], F32),
                ("m4", [2 * C, 4 * C], F32), ("m123", [128, 3, 128], F32), ("sh", [128, ET, 4], F32),
                ("wqkv1", [128, 2, 384], F32), ("wout1", [128, D], F32), ("total", [P, NT, D], F32),
                ("taylor_a", [P, 1], F32)):
            B[name] = graph.enter_context(nc.sbuf_tensor(name, shape, dt))
        edge_mem = whole.enter_context(ExitStack())
        B["r"] = edge_mem.enter_context(nc.sbuf_tensor("edge_units", [128, EP // 2], F32))
        wide_mem = whole.enter_context(ExitStack())
        B["W"] = wide_mem.enter_context(nc.sbuf_tensor("wide_weights", [128, 2, R, D], F32))
        early = whole.enter_context(ExitStack())
        for name, shape in (("self1", [128, 2, D]), ("self2", [128, 2, D]), ("wqkv0", [128, 2, 768]), ("wproj0", [128, 2, D])):
            B[name] = early.enter_context(nc.sbuf_tensor(name, shape, F32))
        table0, table1 = dram("table0", [R, N, D]), dram("table1", [R, N, D])

        class stage:

            def __enter__(self):
                self.mem = ExitStack()
                K.tmp = lambda name, shape, dt=F32: self.mem.enter_context(nc.sbuf_tensor(name, shape, dt))
                K.psum = lambda name, shape: self.mem.enter_context(nc.psum_tensor(name, shape, F32))
                self.block = nc.Block()
                K.block = self.block.__enter__()
                return lambda n, tag: [K.psum(f"{tag}_ps{i}", [128, 512]) for i in range(n)]

            def __exit__(self, *args):
                self.block.__exit__(*args)
                self.mem.close()

        def finished():
            with stage() as _:
                stored = K.new("out_stored")

                @K.block.sync
                def _(sp):
                    sp.dma_start(out.rearrange("(t p) d -> p t d", p=P), K.last[:]).then_inc(stored, 16)
                    sp.wait_ge(stored, 16)

        with stage() as banks:
            load_all(nc, K, A)
            edge_indices(nc, K, banks(2, "ei"))
            layer_norm(nc, K, banks(NT, "ln0"), "ln0", B["x"], B["h"], B["actT"])
        K.last = B["h"]
        with stage() as banks:
            rgcn_tables(nc, K, banks(6, "t0"), "t0", B["actT"], B["W"], B["self1"], S["w1_loaded"], table0, row(K, "gnn_b1"), B["total"])
        with ExitStack() as mix:
            qkT = mix.enter_context(nc.sbuf_tensor("mix_qkT", [128, 4, N], F32))
            v1 = mix.enter_context(nc.sbuf_tensor("mix_v1", [P, NT, H0, HD0 + 1], F32))
            with stage() as banks:
                @K.block.sync
                def _(sp):
                    for c in range(2):
                        sp.dma_start(B["W"][:, c, :, :], A["W2"][:, 128 * c:128 * c + 128, :].rearrange("r p n -> p r n")).then_inc(S["w2_loaded"], 16)
                taylor_qkv(nc, K, banks(8, "tq"), qkT, v1, B["actT"])
            sums = B["wqkv0"][0:P].rearrange("p c n -> p (c n)")[:, 0:NT * H0 * (HD0 + 1)].rearrange("p (t h d) -> p t h d", t=NT, h=H0)
            network = EdgeNetwork(nc, K, B["r"])

            def both(one, other):
                def run(slot):
                    one(slot)
                    other(slot)
                return run

            with stage() as _:
                heads = Taylor(nc, K, 0, qkT, v1, sums)
                pe, act = network.pieces("e0", 0, 2)
                rgcn_edges(nc, K, 0, table0.rearrange("r n d -> (r n) d"), B["total"], True, B["h"],
                           {"pe": both(heads.pe, pe), "act": both(heads.act, act), "dve": lambda slot: None})
            with stage() as banks:
                to_feature_major(nc, K, banks(NT, "h1"), "h1", lambda t: [B["h"][:, t, 0:128], B["h"][:, t, 128:256]], B["actT"])
            with stage() as banks:
                rgcn_tables(nc, K, banks(6, "t1"), "t1", B["actT"], B["W"], B["self2"], S["w2_loaded"], table1, row(K, "gnn_b2"), B["total"])
            with stage() as _:
                @K.block.sync
                def _(sp):
                    sp.dma_start(B["W"][:].rearrange("p c r n -> p c (r n)"), A["f1"].rearrange("(c p) n -> p c n", p=128)).then_inc(S["ffn0_loaded"], 16)
                heads = Taylor(nc, K, TAYLOR, qkT, v1, sums)
                pe, act = network.pieces("e1", 2 * LOOPS, 4)
                rgcn_edges(nc, K, 1, table1.rearrange("r n d -> (r n) d"), B["total"], False, B["h"],
                           {"pe": both(heads.pe, pe), "act": both(heads.act, act), "dve": lambda slot: None})
            y = mix.enter_context(nc.sbuf_tensor("mix_y", [P, NT, D], F32))
            with stage() as banks:
                taylor_end(nc, K, banks(1, "te"), v1, sums, y)
            with stage() as banks:
                to_feature_major(nc, K, banks(NT, "ty"), "ty", lambda t: [y[:, t, 0:128], y[:, t, 128:256]], B["actT"])
            with stage() as banks:
                project_add(nc, K, banks(NT, "pm"), "pm", B["actT"], B["wproj0"], (S["mix0_loaded"], 32),
                            lambda t: [B["x"][:, t, :], row(K, "bproj"), B["h"][:, t, :]], B["x"])
        early.close()
        K.last = B["x"]
        with ExitStack() as ffn:
            hidT = ffn.enter_context(nc.sbuf_tensor("ffn_hidT", [128, E0 * HID0 // 128, N], F32))
            f2 = ffn.enter_context(nc.sbuf_tensor("f2", [128, E0 * HID0 // 128, D], F32))
            with stage() as banks:
                @K.block.sync
                def _(sp):
                    sp.dma_start(f2[:], A["f2"].rearrange("(c p) n -> p c n", p=128)).then_inc(S["f2_loaded"], 16)
                layer_norm(nc, K, banks(NT, "ln1"), "ln1", B["x"], B["h"], B["actT"])
            with stage() as banks:
                routed_ffn(nc, K, banks(8, "rf"), B["x"], B["actT"], hidT, f2)
        wide_mem.close()
        up = dram("table2", [N, D])
        with ExitStack() as gnn:
            hT = gnn.enter_context(nc.sbuf_tensor("gnn_hT", [C, 4, N], F32))
            with stage() as banks:
                layer_norm(nc, K, banks(NT, "ln2"), "ln2", B["x"], B["h"], B["actT"])
            with stage() as banks:
                equivariant_tables(nc, K, banks(NT, "et"), B["h"], hT, up)
            with stage() as _:
                equivariant_edges(nc, K, up, B["r"], B["total"])
            with stage() as banks:
                equivariant_nodes(nc, K, banks(8, "eq"), B["total"], hT, B["x"])
        edge_mem.close()
        outT = graph.enter_context(nc.sbuf_tensor("la_outT", [128, 1, N], F32))
        with stage() as banks:
            linear_attention(nc, K, banks(8, "la"), B["actT"], outT)
        with stage() as banks:
            project_add(nc, K, banks(NT, "pl"), "pl", outT, B["wout1"][:].unsqueeze(1), (S["mix1_loaded"], 32),
                        lambda t: [B["x"][:, t, :], row(K, "b_out")], B["x"])
        graph.close()
        xn = whole.enter_context(nc.sbuf_tensor("attn_xn", [P, NT, D], F32))
        w13 = whole.enter_context(nc.sbuf_tensor("experts_w13", [128, NE * 4 * HID], F32))
        w2 = whole.enter_context(nc.sbuf_tensor("experts_w2", [HC, NE * NC * D], F32))
        with ExitStack() as attn:
            qT = attn.enter_context(nc.sbuf_tensor("attn_qT", [128, 2, N], F32))
            kT = attn.enter_context(nc.sbuf_tensor("attn_kT", [128, N], F32))
            v = attn.enter_context(nc.sbuf_tensor("attn_v", [P, NT, NKV * HD], F32))
            with stage() as banks:
                layer_norm(nc, K, banks(NT, "ln3"), "ln3", B["x"], xn, B["actT"])
            with stage() as banks:
                rms_norm(nc, K, banks(NT, "rn1"), "rn1", xn, row(K, "ln1"), B["h"], B["actT"])
            with stage() as banks:
                attention_qkv(nc, K, banks(6, "aq"), B["actT"], qT, kT, v)
            with stage() as _:
                load_experts(nc, K, A, w13, w2)
                causal_attention(nc, K, qT, kT, v, B["h"])
            with stage() as banks:
                to_feature_major(nc, K, banks(NT, "ay"), "ay", lambda t: [B["h"][:, t, 0:128], B["h"][:, t, 128:256]], B["actT"])
            with stage() as banks:
                project_add(nc, K, banks(NT, "pa"), "pa", B["actT"], B["wo"], (S["attn_loaded"], 64), lambda t: [xn[:, t, :]], xn)
        share = whole.enter_context(nc.sbuf_tensor("moe_share", [P, TOP, NT], F32))
        slots = whole.enter_context(nc.sbuf_tensor("moe_slots", [128, TOP * NT], I32))
        token_of = whole.enter_context(nc.sbuf_tensor("moe_token_of", [128, WORK], I32))
        expert_of = whole.enter_context(nc.sbuf_tensor("moe_expert_of", [1, WORK], I32))
        flat_rows, results = dram("flat_rows", [N, D]), dram("expert_results", [WORK * 128, D])
        with stage() as banks:
            rms_norm(nc, K, banks(NT, "rn2"), "rn2", xn, row(K, "ln2"), B["h"], B["actT"])
        with stage() as banks:
            dispatch(nc, K, banks(4, "di"), B["actT"], B["h"], flat_rows, share, slots, token_of, expert_of)
        with stage() as _:
            mixture(nc, K, w13, w2, flat_rows, results, share, slots, token_of, expert_of, B["x"], xn)
        K.last = xn
        finished()


def kernel(**inputs):
    import numpy as _np
    import concourse.bacc as _bacc
    from concourse import mybir as _mybir
    from concourse.bass_utils import run_bass_kernel_spmd as _run

    I = {k: _np.asarray(v) for k, v in inputs.items()}

    def padded(a, fill):
        return _np.concatenate([a, _np.full((EP - E,) + a.shape[1:], fill, a.dtype)])


    src, typ, dst = padded(I["src"], 0), padded(I["edge_type_8"], 0), padded(I["dst"], -1)
    inv_freq = 1.0 / 10000.0 ** (_np.arange(0, HD, 2, dtype=_np.float32) / HD)
    freqs = _np.outer(_np.arange(N, dtype=_np.float32), inv_freq)
    emb = _np.concatenate([freqs, freqs], axis=-1)
    sin = _np.sin(emb)
    rope = _np.stack([_np.cos(emb), _np.concatenate([-sin[:, :HD // 2], sin[:, HD // 2:]], axis=-1)]).astype(_np.float32)
    rows = _np.concatenate([I["L0_gnn_b1"], I["L0_gnn_b2"], I["L0_mix_bqkv"], I["L0_mix_bproj"],
                            I["L0_mix_temperature"].reshape(-1), I["L0_ffn_router_b"], I["L1_mix_b_out"],
                            I["L1_ffn_ln1_w"], I["L1_ffn_ln2_w"]])
    arrays = {
        "x": I["x"], "rows": rows,
        "eint": _np.stack([a.reshape(ET, 128).T for a in (src, typ, dst)], axis=1),
        "dst_rows": dst.reshape(GROUPS, GROUP * 128),
        "W1": I["L0_gnn_W1"], "self1": I["L0_gnn_self_w1"], "W2": I["L0_gnn_W2"], "self2": I["L0_gnn_self_w2"],
        "wqkv0": I["L0_mix_Wqkv"].T, "wproj0": I["L0_mix_Wproj"].T,
        "router0": I["L0_ffn_router_w"].T,
        "f1": I["L0_ffn_W1"].transpose(1, 0, 2).reshape(D, E0 * HID0),
        "f1b": I["L0_ffn_b1"].reshape(-1, 128).T,
        "f2": I["L0_ffn_W2"].reshape(E0 * HID0, D), "f2b": I["L0_ffn_b2"],
        "c64": _np.concatenate([I["L1_gnn_" + n] for n in ("W_up0", "W_up1", "W_lin0", "W_lin1")]
                               + [I["L1_gnn_WB0"], I["L1_gnn_WB1"], I["L1_gnn_Wc0"], I["L1_gnn_Wc1"],
                                  I["L1_gnn_gamma0"][:, None], I["L1_gnn_beta0"][:, None], I["L1_gnn_gamma1"][:, None]], axis=1),
        "m1": I["L1_gnn_M1"], "m2": I["L1_gnn_M2"], "m3": I["L1_gnn_M3"], "m4": I["L1_gnn_M4"],
        "sh": padded(I["edge_attr_4"], 0).reshape(ET, 128, 4).transpose(1, 0, 2),
        "rbf": padded(I["edge_attr_16"], 0).reshape(EP // 1024, 2, 512, 16).transpose(1, 3, 0, 2).reshape(32, EP // 2),
        "wqkv1": I["L1_mix_W_qkv"], "wout1": I["L1_mix_W_out"],
        "wattn": _np.concatenate([I["L1_ffn_wq"].reshape(NH, HD, D)[[0, 2, 1, 3]].reshape(NH * HD, D), I["L1_ffn_wk"], I["L1_ffn_wv"]]).T,
        "wo": I["L1_ffn_wo"].T, "router1": I["L1_ffn_router_w"].T, "rope": rope,
        "e1": I["L1_ffn_w1"].transpose(0, 2, 1), "e3": I["L1_ffn_w3"].transpose(0, 2, 1), "e2": I["L1_ffn_w2"].transpose(0, 2, 1),
    }
    arrays["c64"] = _np.concatenate([arrays["c64"], I["L1_gnn_Wsc0"], I["L1_gnn_Wsc1"]], axis=1)
    nc = _bacc.Bacc("TRN2", target_bir_lowering=False, num_devices=1)
    A, fed = {}, {}
    for name, a in arrays.items():
        fed[f"{name}_dram"] = a = _np.ascontiguousarray(a)
        A[name] = nc.dram_tensor(f"{name}_dram", a.shape, _mybir.dt.from_np(a.dtype), kind="ExternalInput").ap()
    out = nc.dram_tensor("out_dram", (N, D), F32, kind="ExternalOutput").ap()
    program(nc, A, out)
    r = _run(nc, [fed], core_ids=[0])
    return r.results[0]["out_dram"]
```

```python
from contextlib import ExitStack

import numpy as np
import concourse.bass as bass
from concourse import mybir

F32 = mybir.dt.float32
I32 = mybir.dt.int32
BF16 = mybir.dt.bfloat16
ALU = mybir.AluOpType
ACT = mybir.ActivationFunctionType
AX = mybir.AxisListType

N = 625
P = 125
NT = N // P
D = 256
E = 20000
ET = 160
EP = ET * 128
GROUP = 4
BUFS = 4
GROUPS = ET // GROUP
ITER = BUFS * GROUP
LOOPS = ET // ITER
R = 8
PASSES = 3
CHUNKS = NT + 1
H0, HD0 = 8, 32
E0, HID0 = 32, 64
C = 64
H1, HD1 = 4, 32
NH, NKV, HD = 4, 2, 64
NE = 8
HID = 682
HC = 114
NC = 6
TOP = 2
WORK = (TOP * N + NE * 127) // 128
LEAST = (TOP * N + 127) // 128
TAYLOR = H0 // 2
HALVES = ((0, 313), (313, N))

ROWS = {}
_at = 0
for _name, _n in [("gnn_b1", D), ("gnn_b2", D), ("bqkv", 768), ("bproj", D), ("temp", H0),
                  ("router_b0", E0), ("b_out", D), ("ln1", D), ("ln2", D)]:
    ROWS[_name] = (_at, _n)
    _at += _n
NROWS = _at


class Kernel:

    def __init__(self):
        self.sem, self.buf = {}, {}
        self.dve_n = [0]


class Signal:

    def __init__(self, sem, base):
        self.sem, self.base = sem, base


class Chain:

    def __init__(self, eng, sem, n):
        self.eng, self.sem, self.n = eng, sem, n

    def step(self, instruction):
        instruction.then_inc(self.sem, 1)
        self.n[0] += 1
        self.eng.wait_ge(self.sem, self.n[0])


def nodes(t):
    return slice(t * P, (t + 1) * P)


def load_all(nc, K, A):
    S, B = K.sem, K.buf

    @K.block.sync
    def _(sp):
        sp.dma_start(B["x"][:], A["x"].rearrange("(t p) d -> p t d", p=P)).then_inc(S["x_loaded"], 16)
        sp.dma_start(B["rows"][:], A["rows"].partition_broadcast(P)).then_inc(S["rows_loaded"], 16)
        sp.dma_start(B["eint"][:], A["eint"]).then_inc(S["eint_loaded"], 16)
        sp.dma_start(B["dst_rows"][:], A["dst_rows"]).then_inc(S["eint_loaded"], 16)
        for c in range(2):
            sp.dma_start(B["W"][:, c, :, :], A["W1"][:, 128 * c:128 * c + 128, :].rearrange("r p n -> p r n")).then_inc(S["w1_loaded"], 16)
        sp.dma_start(B["self1"][:], A["self1"].rearrange("(c p) n -> p c n", p=128)).then_inc(S["w1_loaded"], 16)
        sp.dma_start(B["self2"][:], A["self2"].rearrange("(c p) n -> p c n", p=128)).then_inc(S["w2_loaded"], 16)
        sp.dma_start(B["wqkv0"][:], A["wqkv0"].rearrange("(c p) n -> p c n", p=128)).then_inc(S["mix0_loaded"], 16)
        sp.dma_start(B["wproj0"][:], A["wproj0"].rearrange("(c p) n -> p c n", p=128)).then_inc(S["mix0_loaded"], 16)
        sp.dma_start(B["router0"][:], A["router0"].rearrange("(c p) n -> p c n", p=128)).then_inc(S["ffn0_loaded"], 16)
        sp.dma_start(B["f1b"][:], A["f1b"]).then_inc(S["ffn0_loaded"], 16)
        sp.dma_start(B["f2b"][:], A["f2b"]).then_inc(S["ffn0_loaded"], 16)
        sp.dma_start(B["c64"][:], A["c64"]).then_inc(S["gnn1_loaded"], 16)
        sp.dma_start(B["m4"][0:C, :], A["m4"]).then_inc(S["gnn1_loaded"], 16)
        sp.dma_start(B["m4"][C:2 * C, :], A["m4"]).then_inc(S["gnn1_loaded"], 16)
        sp.dma_start(B["sh"][:], A["sh"]).then_inc(S["gnn1_loaded"], 16)
        sp.dma_start(B["r"][0:32, :], A["rbf"]).then_inc(S["rbf_loaded"], 16)
        sp.dma_start(B["wqkv1"][:], A["wqkv1"].rearrange("(c p) n -> p c n", p=128)).then_inc(S["mix1_loaded"], 16)
        sp.dma_start(B["wout1"][:], A["wout1"]).then_inc(S["mix1_loaded"], 16)
        sp.dma_start(B["wattn"][:], A["wattn"].rearrange("(c p) n -> p c n", p=128)).then_inc(S["attn_loaded"], 16)
        sp.dma_start(B["wo"][:], A["wo"].rearrange("(c p) n -> p c n", p=128)).then_inc(S["attn_loaded"], 16)
        sp.dma_start(B["router1"][:], A["router1"].rearrange("(c p) n -> p c n", p=128)).then_inc(S["attn_loaded"], 16)
        sp.dma_start(B["rope"][:], A["rope"].rearrange("a (t p) n -> p a t n", p=P)).then_inc(S["attn_loaded"], 16)

    @K.block.gpsimd
    def _(pool):
        pool.memset(B["ident"][:], 0.0).then_inc(S["pool_chain"], 1)
        pool.memset(B["m123"][:], 0.0).then_inc(S["zeroed"], 1)
        pool.memset(B["taylor_a"][:], float(HD0) ** 0.5)
        pool.memset(B["causal"][:], 0.0).then_inc(S["pool_chain"], 1)
        pool.wait_ge(S["pool_chain"], 2)
        pool.affine_select(out=B["ident"][:], in_=B["ident"][:], compare_op=ALU.not_equal, fill=1.0, base=0,
                           pattern=[[-1, 128]], channel_multiplier=1).then_inc(S["consts"], 1)
        pool.affine_select(out=B["causal"][:, N - P:N], in_=B["causal"][:, N - P:N], compare_op=ALU.is_ge, fill=-1e30,
                           base=0, pattern=[[-1, P]], channel_multiplier=1).then_inc(S["consts"], 1)
        pool.iota(B["iota"][:], pattern=[[1, 2 * P]], base=0, channel_multiplier=0,
                  allow_small_or_imprecise_dtypes=True).then_inc(S["consts"], 1)

        pool.iota(B["count"][:], pattern=[[-1, E0]], base=E0, channel_multiplier=0,
                  allow_small_or_imprecise_dtypes=True).then_inc(S["consts"], 1)

    @K.block.scalar
    def _(act):
        act.wait_ge(S["zeroed"], 1)
        for g in range(2):
            act.dma_start(B["m123"][16 * g:16 * g + 16, 0, C * g:C * g + C], A["m1"]).then_inc(S["m123_loaded"], 16)
            act.dma_start(B["m123"][C * g:C * g + C, 1, C * g:C * g + C], A["m2"]).then_inc(S["m123_loaded"], 16)
            act.dma_start(B["m123"][C * g:C * g + C, 2, C * g:C * g + C], A["m3"]).then_inc(S["m123_loaded"], 16)


def row(K, name):
    at, n = ROWS[name]
    return K.buf["rows"][:, at:at + n]


def edge_indices(nc, K, PS):
    S, B = K.sem, K.buf
    cast = K.tmp("ei_f", [128, 3, ET])
    rows_f = K.tmp("ei_rows", [GROUPS, GROUP * 128])
    neg = K.tmp("ei_neg", [GROUPS, GROUP * 128])
    least = K.tmp("ei_least", [GROUPS, 1])
    most = K.tmp("ei_most", [GROUPS, 1])
    stat = K.tmp("ei_stat", [GROUPS, 3])
    past = K.tmp("ei_past", [GROUPS, 4])
    line = K.tmp("ei_line", [1, 3, GROUPS])
    flag = K.tmp("ei_flag", [1, 4])
    first = K.tmp("ei_first", [1, GROUPS])
    ones = K.tmp("ei_ones", [1, 128])
    stat_ps, first_ps = PS[0], PS[1]
    dve_sem, pe_sem = S["ei_dve"], S["ei_pe"]

    @K.block.vector
    def _(dve):
        ch = Chain(dve, S["dve_chain"], K.dve_n)
        dve.wait_ge(S["eint_loaded"], 32)
        ch.step(nc.vector.tensor_copy(rows_f[:], B["dst_rows"][:]))
        ch.step(nc.vector.tensor_reduce(most[:], rows_f[:], AX.X, ALU.max))
        ch.step(nc.vector.tensor_scalar(neg[:], rows_f[:], 0.0, 10000.0, ALU.is_lt, ALU.mult))
        ch.step(nc.vector.tensor_tensor(neg[:], neg[:], rows_f[:], ALU.add))
        ch.step(nc.vector.tensor_reduce(least[:], neg[:], AX.X, ALU.min))
        for k in range(1, NT):
            ch.step(nc.vector.tensor_scalar(past[:, k - 1:k], least[:], float(P * k), None, ALU.is_ge))
        ch.step(nc.vector.tensor_reduce(stat[:, 0:1], past[:], AX.X, ALU.add))
        ch.step(nc.vector.scalar_tensor_tensor(most[:], stat[:, 0:1], -float(P), most[:], ALU.mult, ALU.add))
        nc.vector.tensor_scalar(stat[:, 2:3], most[:], float(P), None, ALU.is_ge)
        nc.vector.tensor_scalar(stat[:, 1:2], most[:], float(2 * P), None, ALU.is_ge).then_inc(dve_sem, 1)
        ch.step(nc.vector.tensor_copy(cast[:], B["eint"][:]))
        nc.vector.tensor_copy(B["src_idx"][:], cast[:, 0, :])
        nc.vector.scalar_tensor_tensor(B["rel_idx"][:], cast[:, 1, :], float(N), cast[:, 0, :], ALU.mult, ALU.add)
        ch.step(nc.vector.memset(ones[:], 1.0))
        dve.wait_ge(pe_sem, 1)
        ch.step(nc.vector.tensor_copy(line[:], stat_ps[0:1, 0:3 * GROUPS].rearrange("p (a t) -> p a t", a=3)))
        ch.step(nc.vector.tensor_reduce(flag[:, 0:1], line[:, 1, :], AX.X, ALU.max))
        ch.step(nc.vector.tensor_scalar(flag[:, 1:2], flag[:, 0:1], -1.0, 1.0, ALU.mult, ALU.add))
        ch.step(nc.vector.tensor_scalar(first[:], line[:, 0, :], flag[:, 1:2], None, ALU.mult))
        nc.vector.tensor_scalar(B["spans"][:, 0, :], line[:, 2, :], flag[:, 0:1], None, ALU.max)
        for p in range(1, PASSES):
            nc.vector.memset(B["spans"][:, p, :], 1)
        nc.vector.tensor_scalar(B["npass"][:], flag[:, 0:1], float(PASSES - 1), 1.0, ALU.mult, ALU.add)
        nc.vector.tensor_scalar(B["chunk_at"][:, 0, :], first[:], float(D), None, ALU.mult)
        for p in range(1, PASSES):
            last = nc.vector.memset(B["chunk_at"][:, p, :], 2 * p * D)
        last.then_inc(dve_sem, 1)
        for p in range(1, PASSES):
            nc.vector.tensor_scalar(B["dst_rel"][:, p, :], cast[:, 2, :], -float(2 * P * p), None, ALU.add)
        dve.wait_ge(pe_sem, 2)
        nc.vector.scalar_tensor_tensor(B["dst_rel"][:, 0, :].rearrange("e (g k) -> e g k", k=GROUP),
                                       first_ps[:, 0:GROUPS].unsqueeze(2).to_broadcast([128, GROUPS, GROUP]), -float(P),
                                       cast[:, 2, :].rearrange("e (g k) -> e g k", k=GROUP), ALU.mult, ALU.add)

    @K.block.tensor
    def _(pe):
        pe.wait_ge(S["consts"], 4)
        pe.wait_ge(dve_sem, 1)
        for a in range(3):
            last = nc.tensor.transpose(stat_ps[0:1, GROUPS * a:GROUPS * (a + 1)], stat[:, a:a + 1], B["ident"][0:GROUPS, 0:GROUPS])
        last.then_inc(pe_sem, 1)
        pe.wait_ge(dve_sem, 2)
        nc.tensor.matmul(first_ps[:, 0:GROUPS], ones[:], first[:], start=True, stop=True).then_inc(pe_sem, 1)


def layer_norm(nc, K, PS, tag, x, xn, xnT):
    S, B = K.sem, K.buf
    st = K.tmp(f"{tag}_st", [P, NT, 6])
    mv = K.tmp(f"{tag}_mv", [P, NT, 2])
    var = K.tmp(f"{tag}_var", [P, NT])
    std = K.tmp(f"{tag}_std", [P, NT])
    rstd = K.tmp(f"{tag}_rstd", [P, NT])
    var_ready = K.shared("var_ready", 1)
    std_ready = K.shared("std_ready", 1)
    xn_ready = K.shared("normalised", NT)
    turned = K.shared("turned", NT)

    @K.block.vector
    def _(dve):
        ch = Chain(dve, S["dve_chain"], K.dve_n)
        dve.wait_ge(S["x_loaded"], 16)
        for t in range(NT):
            last = nc.vector.bn_stats(st[:, t, :], x[:, t, :])
        ch.step(last)
        for t in range(NT):
            last = nc.vector.bn_aggr(mv[:, t, :], st[:, t, :])
        ch.step(last)
        nc.vector.tensor_scalar(var[:], mv[:, :, 1], 1e-5, None, ALU.add).then_inc(var_ready.sem, 1)
        dve.wait_ge(std_ready.sem, std_ready.base + 1)
        ch.step(nc.vector.reciprocal(rstd[:], std[:]))
        for t in range(NT):
            nc.vector.tensor_scalar(xn[:, t, :], x[:, t, :], mv[:, t, 0:1], rstd[:, t:t + 1],
                                    ALU.subtract, ALU.mult).then_inc(xn_ready.sem, 1)

    @K.block.scalar
    def _(act):
        act.wait_ge(var_ready.sem, var_ready.base + 1)
        nc.scalar.activation(std[:], var[:], ACT.Sqrt).then_inc(std_ready.sem, 1)
        for t in range(NT):
            act.wait_ge(turned.sem, turned.base + t + 1)
            nc.scalar.copy(xnT[:, :, nodes(t)], PS[t][:, 0:2 * P].rearrange("p (c n) -> p c n", c=2))

    @K.block.tensor
    def _(pe):
        pe.wait_ge(S["consts"], 4)
        for t in range(NT):
            pe.wait_ge(xn_ready.sem, xn_ready.base + t + 1)
            for c in range(2):
                last = nc.tensor.transpose(PS[t][:, P * c:P * c + P], xn[:, t, 128 * c:128 * c + 128], B["ident"][0:P, 0:P])
            last.then_inc(turned.sem, 1)


def to_feature_major(nc, K, PS, tag, parts, out):
    B = K.buf
    turned = K.shared("turned", NT)

    @K.block.tensor
    def _(pe):
        for t in range(NT):
            for i, part in enumerate(parts(t)):
                last = nc.tensor.transpose(PS[t][:, P * i:P * i + P], part, B["ident"][0:P, 0:P])
            last.then_inc(turned.sem, 1)

    @K.block.scalar
    def _(act):
        for t in range(NT):
            act.wait_ge(turned.sem, turned.base + t + 1)
            k = len(parts(t))
            nc.scalar.copy(out[:, :, nodes(t)], PS[t][:, 0:k * P].rearrange("p (c n) -> p c n", c=k))


def rgcn_tables(nc, K, PS, tag, xT, W, self_w, loaded, table, bias, total):
    B = K.buf
    OUT = 3
    stage = K.tmp(f"{tag}_stage", [P, OUT, R, D])
    made = K.shared("rows_made", (R // 2 + 1) * NT)
    stored = [K.shared(f"rows_stored{i}", 16 * ((NT + OUT - 1 - i) // OUT)) for i in range(OUT)]
    self_done = K.shared("self_done", NT)
    copied = [K.shared(f"rows_copied{i}", NT * R // 4) for i in range(2)]
    G = R // 2

    @K.block.tensor
    def _(pe):
        pe.wait_ge(loaded, 48)
        for t in range(NT):
            for g in range(G):
                n = t * G + g
                if n >= 4:
                    pe.wait_ge(copied[n % 2].sem, copied[n % 2].base + n // 2 - 1)
                for c in range(2):
                    last = nc.tensor.matmul(PS[n % 4][0:P, 0:2 * D], xT[:, c, nodes(t)],
                                            W[:, c, 2 * g:2 * g + 2, :].rearrange("p r d -> p (r d)"), start=(c == 0), stop=(c == 1))
                last.then_inc(made.sem, 1)
        for t in range(NT):
            if t >= 2:
                pe.wait_ge(self_done.sem, self_done.base + t - 1)
            for c in range(2):
                last = nc.tensor.matmul(PS[4 + t % 2][0:P, 0:D], xT[:, c, nodes(t)], self_w[:, c, :], start=(c == 0), stop=(c == 1))
            last.then_inc(made.sem, 1)
        for i in range(2):
            pe.wait_ge(copied[i].sem, copied[i].base + NT * G // 2)

    @K.block.scalar
    def _(act):
        for n in range(0, NT * G, 2):
            act.wait_ge(made.sem, made.base + n + 1)
            t, g = n // G, n % G
            if t >= OUT:
                act.wait_ge(stored[t % OUT].sem, stored[t % OUT].base + 16 * (t // OUT))
            nc.scalar.copy(stage[:, t % OUT, 2 * g:2 * g + 2, :], PS[n % 4][0:P, 0:2 * D].rearrange("p (r d) -> p r d", r=2)).then_inc(copied[0].sem, 1)

    @K.block.vector
    def _(dve):
        for n in range(1, NT * G, 2):
            dve.wait_ge(made.sem, made.base + n + 1)
            t, g = n // G, n % G
            if t >= OUT:
                dve.wait_ge(stored[t % OUT].sem, stored[t % OUT].base + 16 * (t // OUT))
            nc.vector.tensor_copy(stage[:, t % OUT, 2 * g:2 * g + 2, :], PS[n % 4][0:P, 0:2 * D].rearrange("p (r d) -> p r d", r=2)).then_inc(copied[1].sem, 1)
        for t in range(NT):
            dve.wait_ge(made.sem, made.base + NT * G + t + 1)
            nc.vector.tensor_tensor(total[:, t, :], PS[4 + t % 2][0:P, 0:D], bias, ALU.add).then_inc(self_done.sem, 1)

    @K.block.sync
    def _(sp):
        for t in range(NT):
            for c in range(2):
                sp.wait_ge(copied[c].sem, copied[c].base + (t + 1) * G // 2)
            sp.dma_start(table.rearrange("r n d -> n r d")[nodes(t)], stage[:, t % OUT, :, :]).then_inc(stored[t % OUT].sem, 16)
        for i in range(OUT):
            sp.wait_ge(stored[i].sem, stored[i].base + 16 * ((NT + OUT - 1 - i) // OUT))

    return made


def segments(eng, K, iteration, slots):
    n_pass = eng.value_load(K.buf["npass"][:], min_val=1, max_val=PASSES)
    for i in range(LOOPS):
        slots(i)
        iteration(0, i)
    with eng.Fori(1, PASSES) as p:
        with eng.If(p < n_pass):
            with eng.Fori(0, LOOPS) as i:
                iteration(p, i)
    return n_pass


def gathers(nc, K, pool, layer, base, table, index, idx, got, free, filled):
    S = K.sem

    def iteration(p, i):
        for b in range(BUFS):
            n = p * LOOPS + i
            first = i * ITER + b * GROUP
            pool.wait_ge(free[b], base + n + 1)
            if isinstance(p, int):
                if layer > 0:
                    pool.sem_inc(S["gate"], 1)
                at = [index[:, first + k:first + k + 1] for k in range(GROUP)]
            else:
                pool.sem_inc(S["gate"], 1)
                nc.gpsimd.tensor_copy(idx[:, b, :], index[:, bass.ds(first, GROUP)]).then_inc(S["idx_copied"], 1)
                pool.wait_ge(S["idx_copied"], (base + n) * BUFS + b + 1)
                pool.sem_inc(S["gate"], 1)
                at = [idx[:, b, k:k + 1] for k in range(GROUP)]
            for k in range(GROUP):
                nc.gpsimd.indirect_dma_start(got[:, b, k, :], None, table, bass.IndirectOffsetOnAxis(ap=at[k], axis=0)).then_inc(filled[b], 16)

    pool.sem_inc(S["idx_copied"], LOOPS * BUFS)
    segments(pool, K, iteration, lambda slot: None)


def tile_scalar(a, p, at):
    return a[:, bass.ds(p, 1), bass.ds(at, 1)].rearrange("e a b -> e (a b)")


def group_place(K, pe, g):
    def value(a, most):
        return pe.value_load(a[:].rearrange("e a b -> e (a b)")[:, bass.ds(g, 1)], min_val=0, max_val=most)
    return value(K.buf["chunk_at"], (NT - 1) * D), value(K.buf["spans"], 1)


def add_group(nc, pe, sums, onehot, rows, place, done):
    at, spans = place
    with pe.If(spans > 0):
        for k in range(GROUP):
            nc.tensor.matmul(sums[0:P, bass.ds(at + D, D)], onehot(k)[:, P:2 * P], rows(k), start=False, stop=False, skip_group_check=True)
    for k in range(GROUP):
        last = nc.tensor.matmul(sums[0:P, bass.ds(at, D)], onehot(k)[:, 0:P], rows(k), start=False, stop=False, skip_group_check=True)
    last.then_inc(done, 1)


def rgcn_edges(nc, K, layer, table, total, relu, out, pieces):
    S, B = K.sem, K.buf
    tag = f"e{layer}"
    got = K.tmp(f"{tag}_got", [128, BUFS, GROUP, D])
    idx = K.tmp(f"{tag}_idx", [128, BUFS, GROUP], I32)
    onehot = K.tmp(f"{tag}_onehot", [128, BUFS, GROUP, 2 * P])
    sums = K.psum(f"{tag}_sums", [128, CHUNKS * D])
    free, filled, hot = ([S[f"{n}{b}"] for b in range(BUFS)] for n in ("free", "filled", "hot"))
    zeroed = K.shared("sums_zeroed", 1)

    def base_of(eng):
        return 0 if layer == 0 else eng.value_load(B["npass"][:], min_val=1, max_val=PASSES) * LOOPS

    @K.block.gpsimd
    def _(pool):
        gathers(nc, K, pool, layer, base_of(pool), table, B["rel_idx"], idx, got, free, filled)

    @K.block.vector
    def _(dve):
        base = base_of(dve)
        nc.vector.memset(sums[:], 0.0).then_inc(zeroed.sem, 1)

        def iteration(p, i):
            for b in range(BUFS):
                dve.wait_ge(free[b], base + p * LOOPS + i + 1)
                for k in range(GROUP):
                    last = nc.vector.tensor_scalar(onehot[:, b, k, :], B["iota"][:], tile_scalar(B["dst_rel"], p, i * ITER + b * GROUP + k),
                                                   None, ALU.is_equal)
                last.then_inc(hot[b], 1)

        n_pass = segments(dve, K, iteration, pieces["dve"])
        for b in range(BUFS):
            dve.wait_ge(free[b], base + n_pass * LOOPS + 1)
        ch = Chain(dve, S["dve_chain"], K.dve_n)
        for t in range(NT):
            if relu:
                ch.step(nc.vector.tensor_tensor(total[:, t, :], sums[0:P, t * D:t * D + D], total[:, t, :], ALU.add))
                nc.vector.tensor_scalar(out[:, t, :], total[:, t, :], 0.0, None, ALU.max)
            else:
                nc.vector.tensor_tensor(out[:, t, :], sums[0:P, t * D:t * D + D], total[:, t, :], ALU.add)

    @K.block.scalar
    def _(act):
        for slot in range(LOOPS):
            pieces["act"](slot)

    @K.block.tensor
    def _(pe):
        base = base_of(pe)
        if layer == 0:
            for b in range(BUFS):
                pe.sem_inc(free[b], 1)
        pe.wait_ge(zeroed.sem, zeroed.base + 1)

        def iteration(p, i):
            for b in range(BUFS):
                place = group_place(K, pe, (p * LOOPS + i) * BUFS + b)
                pe.wait_ge(filled[b], (base + p * LOOPS + i + 1) * (16 * GROUP))
                pe.wait_ge(hot[b], base + p * LOOPS + i + 1)
                add_group(nc, pe, sums, lambda k: onehot[:, b, k, :], lambda k: got[:, b, k, :], place, free[b])

        segments(pe, K, iteration, pieces["pe"])


def taylor_qkv(nc, K, PS, qkT, v1, xT):
    S, B = K.sem, K.buf
    s2 = float(HD0) ** 0.5
    qkv = K.tmp("tq_qkv", [P, NT, 3 * D])
    sq = K.tmp("tq_sq", [P, NT, 2 * D])
    norm = K.tmp("tq_norm", [P, NT, 2 * H0])
    factor = K.tmp("tq_factor", [P, NT, 2 * H0])
    turned_out = K.new("tq_turned_out")
    made, evacuated, added, squared, summed, rooted, ready, turned = (
        K.new(f"tq_{n}") for n in ("made", "evacuated", "added", "squared", "summed", "rooted", "ready", "turned"))

    @K.block.tensor
    def _(pe):
        pe.wait_ge(S["mix0_loaded"], 32)
        for t in range(NT):
            if t >= 2:
                pe.wait_ge(evacuated, t - 1)
            for c in range(2):
                nc.tensor.matmul(PS[2 * (t % 2)][0:P, 0:512], xT[:, c, nodes(t)], B["wqkv0"][:, c, 0:512], start=(c == 0), stop=(c == 1))
            for c in range(2):
                last = nc.tensor.matmul(PS[2 * (t % 2) + 1][0:P, 0:D], xT[:, c, nodes(t)], B["wqkv0"][:, c, 512:768], start=(c == 0), stop=(c == 1))
            last.then_inc(made, 1)
        pe.wait_ge(ready, 1)
        for t in range(NT):
            if t >= 4:
                pe.wait_ge(turned_out, t - 3)
            for i in range(4):
                last = nc.tensor.transpose(PS[4 + t % 4][:, P * i:P * i + P], qkv[:, t, 128 * i:128 * i + 128], B["ident"][0:P, 0:P])
            last.then_inc(turned, 1)

    @K.block.vector
    def _(dve):
        ch = Chain(dve, S["dve_chain"], K.dve_n)
        dve.wait_ge(S["rows_loaded"], 16)
        bias = row(K, "bqkv")
        for t in range(NT):
            dve.wait_ge(made, t + 1)
            nc.vector.tensor_tensor(qkv[:, t, 0:512], PS[2 * (t % 2)][0:P, 0:512], bias[:, 0:512], ALU.add).then_inc(added, 1)
            nc.vector.tensor_tensor(qkv[:, t, 512:768], PS[2 * (t % 2) + 1][0:P, 0:D], bias[:, 512:768], ALU.add).then_inc(evacuated, 1)
        dve.wait_ge(squared, NT)
        nc.vector.tensor_reduce(norm[:].rearrange("p t h -> p (t h)"), sq[:].rearrange("p t (h d) -> p (t h) d", d=HD0), AX.X, ALU.add).then_inc(summed, 1)
        dve.wait_ge(rooted, 2)
        ch.step(nc.vector.tensor_scalar(norm[:], norm[:], 1e-12, None, ALU.max))
        ch.step(nc.vector.reciprocal(factor[:], norm[:]))
        temp = row(K, "temp").unsqueeze(1).to_broadcast([P, NT, H0])
        ch.step(nc.vector.scalar_tensor_tensor(factor[:, :, 0:H0], factor[:, :, 0:H0], s2, temp, ALU.mult, ALU.mult))
        ch.step(nc.vector.tensor_scalar(factor[:, :, H0:2 * H0], factor[:, :, H0:2 * H0], float(HD0) ** 0.25, None, ALU.mult))
        for t in range(NT):
            last = nc.vector.tensor_tensor(qkv[:, t, 0:512].rearrange("p (h d) -> p h d", d=HD0), qkv[:, t, 0:512].rearrange("p (h d) -> p h d", d=HD0),
                                           factor[:, t, :].unsqueeze(2).to_broadcast([P, 2 * H0, HD0]), ALU.mult)
        last.then_inc(ready, 1)
        nc.vector.memset(v1[:, :, :, 0:1], 1.0)
        for t in range(NT):
            nc.vector.tensor_copy(v1[:, t, :, 1:HD0 + 1], qkv[:, t, 512:768].rearrange("p (h d) -> p h d", d=HD0))

    @K.block.scalar
    def _(act):
        for t in range(NT):
            act.wait_ge(added, t + 1)
            nc.scalar.activation(sq[:, t, :], qkv[:, t, 0:512], ACT.Square).then_inc(squared, 1)
        act.wait_ge(summed, 1)
        nc.scalar.activation(norm[:, :, 0:H0], norm[:, :, 0:H0], ACT.Sqrt, scale=s2).then_inc(rooted, 1)
        nc.scalar.activation(norm[:, :, H0:2 * H0], norm[:, :, H0:2 * H0], ACT.Sqrt).then_inc(rooted, 1)
        for t in range(NT):
            act.wait_ge(turned, t + 1)
            nc.scalar.copy(qkT[:, :, nodes(t)], PS[4 + t % 4][:, 0:4 * P].rearrange("p (c n) -> p c n", c=4)).then_inc(turned_out, 1)


class Taylor:

    def __init__(self, nc, K, first, qkT, v1, sums):
        self.nc, self.K, self.first, self.qkT, self.v1, self.sums = nc, K, first, qkT, v1, sums
        self.w = K.tmp(f"ta{first}_w", [P, 2, NT, N])
        self.score = [K.psum(f"ta{first}_score{i}", [P, 512]) for i in range(2)]
        self.py = K.psum(f"ta{first}_py", [P, 512])
        self.scored, self.weighted = (K.shared(n, TAYLOR * NT * 2) for n in ("scored", "weighted"))
        self.summed, self.taken = (K.shared(n, TAYLOR) for n in ("summed", "taken"))

    def tiles(self, piece):
        return range(0, 3) if piece % 2 == 0 else range(3, NT)

    def pe(self, piece):
        nc, pe, K = self.nc, self.nc.tensor, self.K
        slot = piece // 2
        for m in self.tiles(piece):
            if slot < TAYLOR:
                h = self.first + slot
                at, blk = 32 * (h % 4), h // 4
                kT = self.qkT[at:at + HD0, 2 + blk, nodes(m)]
                for i, (lo, hi) in enumerate(HALVES):
                    n = (slot * NT + m) * 2 + i
                    if n >= 2:
                        pe.wait_ge(self.weighted.sem, self.weighted.base + n - 1)
                    nc.tensor.matmul(self.score[n % 2][:, 0:hi - lo], kT, self.qkT[at:at + HD0, blk, lo:hi], start=True, stop=True,
                                     tile_position=(at, 0)).then_inc(self.scored.sem, 1)
            if slot >= 1:
                j = slot - 1
                if m == 0:
                    pe.wait_ge(self.weighted.sem, self.weighted.base + 2 * NT * (j + 1))
                    if j >= 1:
                        pe.wait_ge(self.taken.sem, self.taken.base + j)
                for k in range(NT):
                    last = nc.tensor.matmul(self.py[:, m * (HD0 + 1):(m + 1) * (HD0 + 1)], self.w[:, j % 2, k, nodes(m)], self.v1[:, k, self.first + j, :],
                                            start=(k == 0), stop=(k == NT - 1))
                if m == NT - 1:
                    last.then_inc(self.summed.sem, 1)

    def act(self, piece):
        nc, act, K = self.nc, self.nc.scalar, self.K
        slot = piece // 2
        for m in self.tiles(piece) if slot < TAYLOR else ():
            for i, (lo, hi) in enumerate(HALVES):
                n = (slot * NT + m) * 2 + i
                act.wait_ge(self.scored.sem, self.scored.base + n + 1)
                nc.scalar.activation(self.w[:, slot % 2, m, lo:hi], self.score[n % 2][:, 0:hi - lo], ACT.Square,
                                     bias=K.buf["taylor_a"][:]).then_inc(self.weighted.sem, 1)
        if slot >= 1 and piece % 2 == 1:
            act.wait_ge(self.summed.sem, self.summed.base + slot)
            nc.scalar.copy(self.sums[:, :, self.first + slot - 1, :],
                           self.py[:, 0:NT * (HD0 + 1)].rearrange("p (t d) -> p t d", t=NT)).then_inc(self.taken.sem, 1)


def taylor_end(nc, K, PS, v1, sums, y):
    S, B = K.sem, K.buf
    a = float(HD0) ** 0.5
    const = K.tmp("te_const", [P, P])
    vs = K.tmp("te_vs", [P, H0, HD0 + 1])
    rn = K.tmp("te_rn", [P, NT, H0])
    vsum = K.new("te_vsum")

    @K.block.tensor
    def _(pe):
        pe.wait_ge(vsum, 1)
        for t in range(NT):
            last = nc.tensor.matmul(PS[0][0:P, 0:H0 * (HD0 + 1)], const[:], v1[:, t, :, :].rearrange("p h d -> p (h d)"), start=(t == 0), stop=(t == NT - 1))
        last.then_inc(vsum, 1)

    @K.block.vector
    def _(dve):
        ch = Chain(dve, S["dve_chain"], K.dve_n)
        nc.vector.memset(const[:], a * a).then_inc(vsum, 1)
        dve.wait_ge(vsum, 2)
        ch.step(nc.vector.tensor_copy(vs[:].rearrange("p h d -> p (h d)"), PS[0][0:P, 0:H0 * (HD0 + 1)]))
        for t in range(NT):
            last = nc.vector.tensor_tensor(sums[:, t], sums[:, t], vs[:], ALU.add)
        ch.step(last)
        ch.step(nc.vector.reciprocal(rn[:], sums[:, :, :, 0]))
        for t in range(NT):
            nc.vector.tensor_tensor(y[:, t, :].rearrange("p (h d) -> p h d", h=H0), sums[:, t, :, 1:HD0 + 1],
                                    rn[:, t, :].unsqueeze(2).to_broadcast([P, H0, HD0]), ALU.mult)


def project_add(nc, K, PS, tag, yT, W, loaded, adds, out):
    S = K.sem
    made = K.shared("projected", NT)

    @K.block.tensor
    def _(pe):
        pe.wait_ge(loaded[0], loaded[1])
        for t in range(NT):
            k = W.shape[1]
            for c in range(k):
                last = nc.tensor.matmul(PS[t][0:P, 0:D], yT[:, c, nodes(t)], W[:, c, :], start=(c == 0), stop=(c == k - 1))
            last.then_inc(made.sem, 1)

    @K.block.vector
    def _(dve):
        ch = Chain(dve, S["dve_chain"], K.dve_n)
        for t in range(NT):
            dve.wait_ge(made.sem, made.base + t + 1)
            src = PS[t][0:P, 0:D]
            for i, a in enumerate(adds(t)):
                last = nc.vector.tensor_tensor(out[:, t, :], src, a, ALU.add)
                if i + 1 < len(adds(t)):
                    ch.step(last)
                src = out[:, t, :]


def first_of(nc, ch, value, masked, score, best, count, width, out):
    ch.step(nc.vector.tensor_reduce(best[:], value[:], AX.X, ALU.max))
    ch.step(nc.vector.tensor_tensor(masked[:], value[:], best[:].unsqueeze(2).to_broadcast([P, NT, width]), ALU.is_equal))
    ch.step(nc.vector.tensor_tensor(score[:], masked[:], count[:, 0:width].unsqueeze(1).to_broadcast([P, NT, width]), ALU.mult))
    ch.step(nc.vector.tensor_reduce(best[:], score[:], AX.X, ALU.max))
    ch.step(nc.vector.tensor_tensor(out[:], score[:], best[:].unsqueeze(2).to_broadcast([P, NT, width]), ALU.is_equal))


def routed_ffn(nc, K, PS, x, xT, hidT, f2):
    S, B = K.sem, K.buf
    KC = E0 * HID0 // 128
    logits = K.tmp("rf_logits", [P, NT, E0])
    masked = K.tmp("rf_masked", [P, NT, E0])
    score = K.tmp("rf_score", [P, NT, E0])
    hot = K.tmp("rf_hot", [P, NT, E0])
    best = K.tmp("rf_best", [P, NT])
    hotT = K.tmp("rf_hotT", [E0, N])
    mask = K.tmp("rf_mask", [E0, N], BF16)
    sel = K.tmp("rf_sel", [E0, E0 * HID0], BF16)
    extra = K.tmp("rf_extra", [P, NT, D])
    routed, chosen, turned, copied, made, rectified, masked_out, summed, taken, selected = (
        K.new(f"rf_{n}") for n in ("routed", "chosen", "turned", "copied", "made", "rectified", "masked_out", "summed", "taken", "selected"))
    halves = HALVES
    f1 = B["W"][:].rearrange("p c r n -> p c (r n)")

    @K.block.gpsimd
    def _(pool):
        nc.gpsimd.memset(sel[:], 1.0).then_inc(selected, 1)
        pool.wait_ge(selected, 1)
        nc.gpsimd.affine_select(out=sel[:], in_=sel[:], compare_op=ALU.is_ge, fill=0.0, base=0,
                                pattern=[[1, E0 * HID0]], channel_multiplier=-HID0).then_inc(selected, 1)
        pool.wait_ge(selected, 2)
        nc.gpsimd.affine_select(out=sel[:], in_=sel[:], compare_op=ALU.is_ge, fill=0.0, base=HID0 - 1,
                                pattern=[[-1, E0 * HID0]], channel_multiplier=HID0).then_inc(selected, 1)

    @K.block.tensor
    def _(pe):
        pe.wait_ge(S["ffn0_loaded"], 64)
        for t in range(NT):
            for c in range(2):
                last = nc.tensor.matmul(PS[0][0:P, E0 * t:E0 * t + E0], xT[:, c, nodes(t)], B["router0"][:, c, :], start=(c == 0), stop=(c == 1))
        last.then_inc(routed, 1)
        pe.wait_ge(chosen, 1)
        for t in range(4):
            last = nc.tensor.transpose(PS[1][0:E0, P * t:P * t + P], hot[:, t, :], B["ident"][0:P, 0:P])
        last = nc.tensor.transpose(PS[2][0:E0, 0:P], hot[:, 4, :], B["ident"][0:P, 0:P])
        last.then_inc(turned, 1)
        pe.wait_ge(copied, 3)
        pe.wait_ge(selected, 3)
        for k in range(KC):
            for i, (lo, hi) in enumerate(halves):
                n = 2 * k + i
                if n >= 3:
                    pe.wait_ge(masked_out, n - 2)
                for c in range(2):
                    nc.tensor.matmul(PS[n % 3][:, 0:hi - lo], f1[:, c, 128 * k:128 * k + 128], xT[:, c, lo:hi], start=(c == 0), stop=(c == 1))
                nc.tensor.matmul(PS[3 + n % 3][:, 0:hi - lo], sel[:, 128 * k:128 * k + 128], mask[:, lo:hi], start=True, stop=True).then_inc(made, 1)
        pe.wait_ge(masked_out, 2 * KC)
        pe.wait_ge(S["f2_loaded"], 16)
        for t in range(NT):
            if t >= 2:
                pe.wait_ge(taken, t - 1)
            for k in range(KC):
                nc.tensor.matmul(PS[6 + t % 2][0:P, 0:D], hidT[:, k, nodes(t)], f2[:, k, :], start=(k == 0), stop=False)
            nc.tensor.matmul(PS[6 + t % 2][0:P, 0:D], hotT[:, nodes(t)], B["f2b"][:], start=False, stop=True).then_inc(summed, 1)

    @K.block.scalar
    def _(act):
        for k in range(KC):
            for i, (lo, hi) in enumerate(halves):
                n = 2 * k + i
                act.wait_ge(made, n + 1)
                nc.scalar.activation(hidT[:, k, lo:hi], PS[n % 3][:, 0:hi - lo], ACT.Relu, bias=B["f1b"][:, k:k + 1]).then_inc(rectified, 1)

    @K.block.vector
    def _(dve):
        ch = Chain(dve, S["dve_chain"], K.dve_n)
        dve.wait_ge(routed, 1)
        ch.step(nc.vector.tensor_tensor(logits[:], PS[0][0:P, 0:NT * E0].rearrange("p (t e) -> p t e", t=NT),
                                        row(K, "router_b0").unsqueeze(1).to_broadcast([P, NT, E0]), ALU.add))
        first_of(nc, ch, logits, masked, score, best, B["count"], E0, hot)
        dve.sem_inc(chosen, 1)
        dve.wait_ge(turned, 1)
        nc.vector.tensor_copy(hotT[:, 0:4 * P], PS[1][0:E0, 0:4 * P]).then_inc(copied, 1)
        nc.vector.tensor_copy(hotT[:, 4 * P:N], PS[2][0:E0, 0:P]).then_inc(copied, 1)
        dve.wait_ge(copied, 2)
        nc.vector.tensor_copy(mask[:], hotT[:]).then_inc(copied, 1)
        for k in range(KC):
            for i, (lo, hi) in enumerate(halves):
                n = 2 * k + i
                dve.wait_ge(rectified, n + 1)
                nc.vector.tensor_tensor(hidT[:, k, lo:hi], PS[3 + n % 3][:, 0:hi - lo], hidT[:, k, lo:hi], ALU.mult).then_inc(masked_out, 1)
        for t in range(NT):
            dve.wait_ge(summed, t + 1)
            nc.vector.tensor_scalar(extra[:, t, :], PS[6 + t % 2][0:P, 0:D], 0.0, None, ALU.max).then_inc(taken, 1)
            dve.wait_ge(taken, t + 1)
            nc.vector.tensor_tensor(x[:, t, :], x[:, t, :], extra[:, t, :], ALU.add)


def equivariant_tables(nc, K, PS, xn, hT, table):
    S, B = K.sem, K.buf
    stage = K.tmp("et_stage", [P, NT, 4, C])
    turned, copied, made, staged, stored = (K.new(f"et_{n}") for n in ("turned", "copied", "made", "staged", "stored"))

    def part(t, x):
        return xn[:, t, 0:C] if x == 0 else xn[:, t, C:D].rearrange("p (c x) -> p c x", x=3)[:, :, x - 1]

    @K.block.tensor
    def _(pe):
        pe.wait_ge(S["gnn1_loaded"], 64)
        for t in range(NT):
            for x in range(4):
                last = nc.tensor.transpose(PS[t][0:C, P * x:P * x + P], part(t, x), B["ident"][0:P, 0:P])
            last.then_inc(turned, 1)
        for t in range(NT):
            pe.wait_ge(copied, t + 1)
            for x in range(4):
                W = B["c64"][:, 0:C] if x == 0 else B["c64"][:, C:2 * C]
                last = nc.tensor.matmul(PS[t][0:P, C * x:C * x + C], hT[:, x, nodes(t)], W, start=True, stop=True)
            last.then_inc(made, 1)

    @K.block.scalar
    def _(act):
        for t in range(NT):
            act.wait_ge(turned, t + 1)
            nc.scalar.copy(hT[:, :, nodes(t)], PS[t][0:C, 0:4 * P].rearrange("p (c n) -> p c n", c=4)).then_inc(copied, 1)

    @K.block.vector
    def _(dve):
        for t in range(NT):
            dve.wait_ge(made, t + 1)
            nc.vector.tensor_copy(stage[:, t, :, :], PS[t][0:P, 0:D].rearrange("p (x c) -> p x c", x=4)).then_inc(staged, 1)

    @K.block.sync
    def _(sp):
        sp.wait_ge(staged, NT)
        sp.dma_start(table.rearrange("(t p) d -> p t d", p=P), stage[:].rearrange("p t x c -> p t (x c)")).then_inc(stored, 16)
        sp.wait_ge(stored, 16)


class EdgeNetwork:

    BLOCKS = EP // 1024

    def __init__(self, nc, K, r):
        self.nc, self.K, self.r = nc, K, r
        self.made = [K.new(f"en_made{b}") for b in range(2)]
        self.done = [K.new(f"en_done{b}") for b in range(2)]

    def pieces(self, tag, first, each):
        nc, K = self.nc, self.K
        ps = [K.psum(f"{tag}_en_ps{b}", [128, 512]) for b in range(2)]

        def blocks(slot):
            for at in range(first + slot * each, first + (slot + 1) * each):
                layer, block = at // self.BLOCKS, at % self.BLOCKS
                yield at % 2, at // 2, layer, slice(512 * block, 512 * block + 512)

        def pe(slot):
            if first == 0 and slot == 0:
                nc.tensor.wait_ge(K.sem["rbf_loaded"], 16)
                nc.tensor.wait_ge(K.sem["m123_loaded"], 96)
            for b, n, layer, cols in blocks(slot):
                rows_in = 32 if layer == 0 else 128
                if n >= 1:
                    nc.tensor.wait_ge(self.done[b], n)
                nc.tensor.matmul(ps[b][:], K.buf["m123"][0:rows_in, layer, :], self.r[0:rows_in, cols], start=True, stop=True).then_inc(self.made[b], 1)

        def act(slot):
            for b, n, layer, cols in blocks(slot):
                nc.scalar.wait_ge(self.made[b], n + 1)
                nc.scalar.activation(self.r[:, cols], ps[b][:], ACT.Silu).then_inc(self.done[b], 1)

        return pe, act


class LinearAttention:

    F = H1 * HD1

    def __init__(self, nc, K, xT, outT):
        assert LOOPS == 10
        self.nc, self.K, self.xT, self.outT = nc, K, xT, outT
        self.q = K.tmp("la_q", [self.F, N])
        self.k = K.tmp("la_k", [self.F, N])
        self.kn = K.tmp("la_kn", [P, NT, self.F])
        self.v = K.tmp("la_v", [P, NT, self.F])
        self.context = K.tmp("la_context", [self.F, self.F])
        self.top = K.tmp("la_top", [self.F, 4])
        self.bank = K.psum("la_bank", [128, 512])
        self.made, self.emptied, self.top_ready, self.exped, self.inverted, self.cleared = (
            K.new(f"la_{n}") for n in ("made", "emptied", "top_ready", "exped", "inverted", "cleared"))

    def pe(self, slot):
        nc, pe, F, bank = self.nc, self.nc.tensor, self.F, self.bank
        W = self.K.buf["wqkv1"]

        def features(part, half, at):
            lo, hi = HALVES[half]
            for c in range(2):
                last = nc.tensor.matmul(bank[:, at:at + hi - lo], W[:, c, F * part:F * part + F], self.xT[:, c, lo:hi], start=(c == 0), stop=(c == 1))
            return last

        def values(tiles):
            for i, t in enumerate(tiles):
                for c in range(2):
                    last = nc.tensor.matmul(bank[0:P, F * i:F * i + F], self.xT[:, c, nodes(t)], W[:, c, 2 * F:3 * F], start=(c == 0), stop=(c == 1))
            return last

        def turned(tiles):
            for i, t in enumerate(tiles):
                last = nc.tensor.transpose(bank[0:P, F * i:F * i + F], self.k[:, nodes(t)], self.K.buf["ident"][:])
            return last

        if slot == 0:
            pe.wait_ge(self.K.sem["mix1_loaded"], 32)
        else:
            pe.wait_ge(self.emptied, slot)
        if slot <= 1:
            last = features(1, slot, 0)
        elif slot == 2:
            last = values(range(4))
        elif slot == 3:
            values((4,))
            last = features(0, 0, F)
        elif slot == 4:
            last = features(0, 1, 0)
        elif slot == 5:
            pe.wait_ge(self.exped, 1)
            last = turned(range(4))
        elif slot == 6:
            last = turned((4,))
        elif slot == 7:
            for t in range(NT):
                last = nc.tensor.matmul(bank[:, 0:F], self.kn[:, t, :], self.v[:, t, :], start=(t == 0), stop=(t == NT - 1))
        else:
            lo, hi = HALVES[slot - 8]
            last = nc.tensor.matmul(bank[:, 0:hi - lo], self.context[:], self.q[:, lo:hi], start=True, stop=True)
        last.then_inc(self.made, 1)

    def act(self, slot):
        nc, act, F, bank = self.nc, self.nc.scalar, self.F, self.bank
        s = slot - 1
        if s < 0:
            return
        (lo0, hi0), (lo1, hi1) = HALVES
        act.wait_ge(self.made, s + 1)
        if s == 0:
            last = nc.scalar.copy(self.k[:, lo0:hi0], bank[:, 0:hi0])
        elif s == 1:
            last = nc.scalar.copy(self.k[:, lo1:hi1], bank[:, 0:hi1 - lo1])
        elif s == 2:
            last = nc.scalar.copy(self.v[:, 0:4, :].rearrange("p t f -> p (t f)"), bank[0:P, 0:4 * F])
        elif s == 3:
            nc.scalar.copy(self.v[:, 4, :], bank[0:P, 0:F])
            last = nc.scalar.activation(self.q[:, lo0:hi0], bank[:, F:F + hi0], ACT.Copy, scale=float(HD1) ** -0.5)
        elif s == 4:
            last = nc.scalar.activation(self.q[:, lo1:hi1], bank[:, 0:hi1 - lo1], ACT.Copy, scale=float(HD1) ** -0.5)
        elif s == 5:
            last = nc.scalar.copy(self.kn[:, 0:4, :].rearrange("p t f -> p (t f)"), bank[0:P, 0:4 * F])
        elif s == 6:
            last = nc.scalar.copy(self.kn[:, 4, :], bank[0:P, 0:F])
        elif s == 7:
            act.wait_ge(self.inverted, 1)
            act.wait_ge(self.cleared, 1)
            for h in range(H1):
                own = slice(HD1 * h, HD1 * h + HD1)
                last = nc.scalar.activation(self.context[own, own], bank[own, own], ACT.Copy, scale=self.top[own, 3:4])
        else:
            lo, hi = HALVES[s - 8]
            last = nc.scalar.copy(self.outT[:, lo:hi], bank[:, 0:hi - lo])
        last.then_inc(self.emptied, 1)
        if slot == 4:
            act.wait_ge(self.top_ready, 1)
            nc.scalar.activation(self.k[:], self.k[:], ACT.Exp, bias=self.top[:, 1:2], accum_out=self.top[:, 2:3]).then_inc(self.exped, 1)

    def dve(self, slot):
        nc, dve = self.nc, self.nc.vector
        if slot == 0:
            nc.vector.memset(self.context[:], 0.0).then_inc(self.cleared, 1)
        elif slot == 3:
            ch = Chain(dve, self.K.sem["dve_chain"], self.K.dve_n)
            dve.wait_ge(self.emptied, 2)
            ch.step(nc.vector.tensor_reduce(self.top[:, 0:1], self.k[:], AX.X, ALU.max))
            nc.vector.tensor_scalar(self.top[:, 1:2], self.top[:, 0:1], -1.0, None, ALU.mult).then_inc(self.top_ready, 1)
        elif slot == 6:
            dve.wait_ge(self.exped, 1)
            nc.vector.reciprocal(self.top[:, 3:4], self.top[:, 2:3]).then_inc(self.inverted, 1)


def equivariant_edges(nc, K, table, r, msg_nodes):
    S, B = K.sem, K.buf
    G = GROUP
    inv3 = float(1.0 / np.sqrt(np.float32(3.0)))
    got = K.tmp("ee_got", [128, BUFS, G, D])
    idx = K.tmp("ee_idx", [128, BUFS, G], I32)
    onehot = K.tmp("ee_onehot", [128, 2, G, 2 * P])
    rs = K.tmp("ee_rs", [128, 512])
    gs = K.tmp("ee_gs", [128, 2, G, D])
    prod = K.tmp("ee_prod", [128, 2, G, 3, C])
    u = K.tmp("ee_u", [128, 2, G, C])
    dot = K.tmp("ee_dot", [128, 2, G, C])
    first = K.tmp("ee_first", [128, 2, G, D])
    second = K.tmp("ee_second", [128, 2, G, D - C])
    sums = K.psum("ee_sums", [128, CHUNKS * D])
    tp = [K.psum(f"ee_tp{h}", [128, G * D]) for h in range(2)]
    free, filled = ([S[f"{n}{b}"] for b in range(BUFS)] for n in ("free", "filled"))
    hot, weights, used, units, scaled, steps = (K.new(f"ee_{n}") for n in ("hot", "weights", "used", "units", "scaled", "steps"))
    zeroed = K.shared("sums_zeroed", 1)
    STEPS = 7

    linear = LinearAttention(nc, K, B["actT"], B["outT"])

    def start(eng):
        return eng.value_load(B["npass"][:], min_val=1, max_val=PASSES) * (2 * LOOPS)

    def messages_made(eng, base, n, b, back):
        n, b = (n, b - back) if b >= back else (n - 1, b - back + BUFS)
        if not isinstance(n, int) or n >= 0:
            eng.wait_ge(free[b], base + n + 2)

    def after(eng, sem, count):
        if not isinstance(count, int) or count > 0:
            eng.wait_ge(sem, count)

    @K.block.gpsimd
    def _(pool):
        gathers(nc, K, pool, 2, start(pool), table, B["src_idx"], idx, got, free, filled)

    @K.block.scalar
    def _(act):
        base = start(act)

        def iteration(p, i):
            n = p * LOOPS + i
            for b in range(BUFS):
                h = b % 2
                if not isinstance(p, int):
                    act.wait_ge(weights, n * BUFS + b - 1)
                    nc.scalar.copy(rs[C * h:C * h + C, :], r[C * h:C * h + C, bass.ds(i * (BUFS // 2 * 512) + b // 2 * 512, 512)]).then_inc(units, 1)
                act.wait_ge(filled[b], (base + n + 1) * (16 * G))
                messages_made(act, base, n, b, 2)
                for k in range(G):
                    sh = B["sh"][:, bass.ds(i * ITER + b * G + k, 1), :].rearrange("e a b -> e (a b)")
                    for x in range(3):
                        nc.scalar.activation(prod[:, h, k, x, :], got[:, b, k, C * (x + 1):C * (x + 2)], ACT.Copy, scale=sh[:, x + 1:x + 2])
                    last = nc.scalar.activation(gs[:, h, k, :], got[:, b, k, :], ACT.Copy, scale=sh[:, 0:1])
                last.then_inc(scaled, 1)

        segments(act, K, iteration, linear.act)
        linear.act(LOOPS)

    @K.block.vector
    def _(dve):
        base = start(dve)
        nc.vector.memset(sums[:], 0.0).then_inc(zeroed.sem, 1)

        def iteration(p, i):
            for b in range(BUFS):
                h = b % 2
                n = p * LOOPS + i
                g = n * BUFS + b
                before = g * STEPS
                after(dve, used, g - 1)
                for k in range(G):
                    last = nc.vector.tensor_scalar(onehot[:, h, k, :], B["iota"][:], tile_scalar(B["dst_rel"], p, i * ITER + b * G + k), None, ALU.is_equal)
                last.then_inc(hot, 1)
                sv = B["sh"][:, bass.ds(i * ITER + b * G, G), 1:4].unsqueeze(3).to_broadcast([128, G, 3, C])
                w = tp[h][:].rearrange("e (k w c) -> e k w c", k=G, w=4)
                one = first[:, h, :, :].rearrange("e k (x c) -> e k x c", x=4)
                two = second[:, h, :, :].rearrange("e k (x c) -> e k x c", x=3)
                gv = gs[:, h, :, :].rearrange("e k (x c) -> e k x c", x=4)
                dve.wait_ge(weights, g + 1)
                dve.wait_ge(scaled, g + 1)
                nc.vector.tensor_tensor(u[:, h], w[:, :, 1, :], got[:, b, :, 0:C], ALU.mult).then_inc(steps, 1)
                nc.vector.tensor_tensor(dot[:, h], prod[:, h, :, 0, :], prod[:, h, :, 1, :], ALU.add).then_inc(steps, 1)
                nc.vector.tensor_tensor(one[:, :, 0, :], w[:, :, 0, :], gv[:, :, 0, :], ALU.mult).then_inc(steps, 1)
                dve.wait_ge(steps, before + 2)
                nc.vector.tensor_tensor(dot[:, h], dot[:, h], prod[:, h, :, 2, :], ALU.add).then_inc(steps, 1)
                nc.vector.tensor_tensor(two, u[:, h].unsqueeze(2).to_broadcast([128, G, 3, C]), sv, ALU.mult).then_inc(steps, 1)
                dve.wait_ge(steps, before + 4)
                nc.vector.scalar_tensor_tensor(dot[:, h], dot[:, h], inv3, w[:, :, 3, :], ALU.mult, ALU.mult).then_inc(steps, 1)
                nc.vector.tensor_tensor(one[:, :, 1:4, :], w[:, :, 2, :].unsqueeze(2).to_broadcast([128, G, 3, C]), gv[:, :, 1:4, :], ALU.mult).then_inc(steps, 1)
                dve.wait_ge(steps, before + STEPS)
                nc.vector.tensor_tensor(one[:, :, 0, :], one[:, :, 0, :], dot[:, h], ALU.add).then_inc(free[b], 1)

        n_pass = segments(dve, K, iteration, linear.dve)
        dve.wait_ge(used, n_pass * GROUPS)
        for t in range(NT):
            nc.vector.tensor_copy(msg_nodes[:, t, :], sums[0:P, t * D:t * D + D])

    @K.block.tensor
    def _(pe):
        base = start(pe)
        pe.wait_ge(zeroed.sem, zeroed.base + 1)

        def edge_weights(p, i, b):
            n, h = p * LOOPS + i, b % 2
            if isinstance(p, int):
                hidden = r[C * h:C * h + C, (i * BUFS + b) // 2 * 512:(i * BUFS + b) // 2 * 512 + 512]
            else:
                hidden = rs[C * h:C * h + C, :]
                pe.wait_ge(units, (n - LOOPS) * BUFS + b + 1)
            messages_made(pe, base, n, b, 2)
            for k in range(G):
                last = nc.tensor.matmul(tp[h][:, k * D:k * D + D], hidden[:, 128 * k:128 * k + 128], B["m4"][C * h:C * h + C, :],
                                        start=(k % 2 == 0), stop=True, tile_position=(C * h, 0), skip_group_check=True)
            last.then_inc(weights, 1)

        def add_up(n, b):
            h = b % 2
            at, spans = group_place(K, pe, n * BUFS + b)
            pe.wait_ge(hot, n * BUFS + b + 1)
            messages_made(pe, base, n, b, 0)
            with pe.If(spans > 0):
                for k in range(G):
                    for part, skip in ((first, 0), (second, C)):
                        nc.tensor.matmul(sums[0:P, bass.ds(at + D + skip, D - skip)], onehot[:, h, k, P:2 * P], part[:, h, k, :], start=False, stop=False, skip_group_check=True)
            for k in range(G):
                for part, skip in ((first, 0), (second, C)):
                    last = nc.tensor.matmul(sums[0:P, bass.ds(at + skip, D - skip)], onehot[:, h, k, 0:P], part[:, h, k, :], start=False, stop=False, skip_group_check=True)
            last.then_inc(used, 1)

        def iteration(p, i):
            for b in range(BUFS):
                edge_weights(p, i, b)
                n = p * LOOPS + i
                if b >= 1:
                    add_up(n, b - 1)
                elif not isinstance(n, int) or n >= 1:
                    add_up(n - 1, BUFS - 1)

        n_pass = segments(pe, K, iteration, linear.pe)
        add_up(n_pass * LOOPS - 1, BUFS - 1)


def equivariant_nodes(nc, K, PS, msgs, hT, x):
    S, B = K.sem, K.buf
    mT = K.tmp("eq_mT", [C, 4, N])
    A = K.tmp("eq_A", [C, 4, N])
    sq = K.tmp("eq_sq", [C, 3, N])
    vv = K.tmp("eq_vv", [C, N])
    p1 = K.tmp("eq_p1", [C, N])
    p2 = K.tmp("eq_p2", [C, N])
    Bt = K.tmp("eq_B", [C, 4, N])
    o = K.tmp("eq_o", [C, 4, N])
    st = K.tmp("eq_st", [C, NT, 6])
    mv = K.tmp("eq_mv", [C, 2])
    stats = K.tmp("eq_stats", [C, 2])
    std = K.tmp("eq_std", [C, 2])
    scale = K.tmp("eq_scale", [C, 2])
    vsum = K.tmp("eq_vsum", [C, 1])
    turned, copied, made, taken, squared, products, stats_ready, std_ready, normed, back = (
        K.new(f"eq_{n}") for n in ("turned", "copied", "made", "taken", "squared", "products", "stats_ready", "std_ready", "normed", "back"))
    made2, taken2 = K.new("eq_made2"), K.new("eq_taken2")
    halves = ((0, 313), (313, N))
    w0 = [B["c64"][:, 6 * C + i:6 * C + i + 1] for i in range(5)]
    w1 = [B["c64"][:, 6 * C + 5 + i:6 * C + 6 + i] for i in range(4)]
    gamma0, beta0, gamma1 = (B["c64"][:, 6 * C + 9 + i:6 * C + 10 + i] for i in range(3))
    sc = 6 * C + 12

    @K.block.tensor
    def _(pe):
        for t in range(NT):
            for y in range(4):
                last = nc.tensor.transpose(PS[t][0:C, P * y:P * y + P], msgs[:, t, C * y:C * y + C], B["ident"][0:P, 0:P])
            last.then_inc(turned, 1)
        pe.wait_ge(copied, NT)
        for y in range(4):
            W = B["c64"][:, 2 * C:3 * C] if y == 0 else B["c64"][:, 3 * C:4 * C]
            for i, (lo, hi) in enumerate(halves):
                n = 2 * y + i
                if n >= 3:
                    pe.wait_ge(taken, n - 2)
                nc.tensor.matmul(PS[5 + n % 3][0:C, 0:hi - lo], W, mT[:, y, lo:hi], start=True, stop=True).then_inc(made, 1)
        for y in range(4):
            for i, (lo, hi) in enumerate(halves):
                n = 2 * y + i
                if n == 5:
                    pe.wait_ge(taken, 8)
                at = sc if y == 0 else sc + C
                nc.tensor.matmul(PS[n][0:C, 0:hi - lo], B["c64"][:, at:at + C], hT[:, y, lo:hi], start=True, stop=False)
        for y in range(4):
            W = B["c64"][:, 4 * C:5 * C] if y == 0 else B["c64"][:, 5 * C:6 * C]
            pe.wait_ge(products, y + 1)
            for i, (lo, hi) in enumerate(halves):
                nc.tensor.matmul(PS[2 * y + i][0:C, 0:hi - lo], W, Bt[:, y, lo:hi], start=False, stop=True).then_inc(made2, 1)
        pe.wait_ge(normed, 2)
        for t in range(NT):
            for y in range(4):
                last = nc.tensor.transpose(PS[t][0:P, C * y:C * y + C], o[:, y, nodes(t)], B["ident"][0:C, 0:C])
            last.then_inc(back, 1)

    @K.block.scalar
    def _(act):
        for t in range(NT):
            act.wait_ge(turned, t + 1)
            nc.scalar.copy(mT[:, :, nodes(t)], PS[t][0:C, 0:4 * P].rearrange("p (c n) -> p c n", c=4)).then_inc(copied, 1)
        for y in range(4):
            for i, (lo, hi) in enumerate(halves):
                n = 2 * y + i
                act.wait_ge(made, n + 1)
                nc.scalar.copy(A[:, y, lo:hi], PS[5 + n % 3][0:C, 0:hi - lo]).then_inc(taken, 1)
            if y >= 1:
                act.wait_ge(taken, 2 * y + 2)
                nc.scalar.activation(sq[:, y - 1, :], A[:, y, :], ACT.Square).then_inc(squared, 1)
        for y in range(4):
            for i, (lo, hi) in enumerate(halves):
                n = 2 * y + i
                act.wait_ge(made2, n + 1)
                nc.scalar.copy(o[:, y, lo:hi], PS[n][0:C, 0:hi - lo]).then_inc(taken2, 1)
        act.wait_ge(stats_ready, 2)
        nc.scalar.activation(std[:], stats[:], ACT.Sqrt).then_inc(std_ready, 1)

    @K.block.vector
    def _(dve):
        ch = Chain(dve, S["dve_chain"], K.dve_n)
        a0 = A[:, 0, :]
        dve.wait_ge(taken, 2)
        ch.step(nc.vector.tensor_scalar(p1[:], a0, w0[3], w0[1], ALU.mult, ALU.add))
        ch.step(nc.vector.tensor_tensor(p1[:], p1[:], a0, ALU.mult))
        ch.step(nc.vector.scalar_tensor_tensor(p1[:], p1[:], w0[0], a0, ALU.add, ALU.mult))
        ch.step(nc.vector.tensor_scalar(p2[:], a0, w0[4], w0[2], ALU.mult, ALU.add))
        dve.wait_ge(squared, 3)
        ch.step(nc.vector.tensor_tensor(vv[:], sq[:, 0, :], sq[:, 1, :], ALU.add))
        ch.step(nc.vector.tensor_tensor(vv[:], vv[:], sq[:, 2, :], ALU.add))
        ch.step(nc.vector.tensor_tensor(p2[:], p2[:], vv[:], ALU.mult))
        nc.vector.tensor_tensor(Bt[:, 0, :], p1[:], p2[:], ALU.add).then_inc(products, 1)
        dve.wait_ge(products, 1)
        ch.step(nc.vector.tensor_scalar(p1[:], a0, w1[2], w1[1], ALU.mult, ALU.add))
        ch.step(nc.vector.tensor_tensor(p1[:], p1[:], a0, ALU.mult))
        ch.step(nc.vector.scalar_tensor_tensor(p1[:], vv[:], w1[3], p1[:], ALU.mult, ALU.add))
        for y in range(1, 4):
            nc.vector.scalar_tensor_tensor(Bt[:, y, :], p1[:], w1[0], A[:, y, :], ALU.add, ALU.mult).then_inc(products, 1)
        dve.wait_ge(taken2, 2)
        for t in range(NT):
            last = nc.vector.bn_stats(st[:, t, :], o[:, 0, nodes(t)])
        ch.step(last)
        ch.step(nc.vector.bn_aggr(mv[:], st[:]))
        nc.vector.tensor_scalar(stats[:, 0:1], mv[:, 1:2], 1e-5, None, ALU.add).then_inc(stats_ready, 1)
        dve.wait_ge(taken2, 8)
        ch.step(nc.vector.scalar_tensor_tensor(sq[:].rearrange("c x n -> c (x n)"), o[:, 1:4, :].rearrange("c x n -> c (x n)"), 1.0 / (3.0 * N),
                                               o[:, 1:4, :].rearrange("c x n -> c (x n)"), ALU.mult, ALU.mult, accum_out=vsum[:]))
        nc.vector.tensor_scalar(stats[:, 1:2], vsum[:], 1e-5, None, ALU.add).then_inc(stats_ready, 1)
        dve.wait_ge(std_ready, 1)
        ch.step(nc.vector.reciprocal(scale[:], std[:]))
        ch.step(nc.vector.tensor_tensor(scale[:, 0:1], scale[:, 0:1], gamma0, ALU.mult))
        ch.step(nc.vector.tensor_tensor(scale[:, 1:2], scale[:, 1:2], gamma1, ALU.mult))
        ch.step(nc.vector.tensor_scalar(o[:, 0, :], o[:, 0, :], mv[:, 0:1], scale[:, 0:1], ALU.subtract, ALU.mult))
        nc.vector.tensor_scalar(o[:, 0, :], o[:, 0, :], beta0, None, ALU.add).then_inc(normed, 1)
        nc.vector.tensor_scalar(o[:, 1:4, :], o[:, 1:4, :], scale[:, 1:2], None, ALU.mult).then_inc(normed, 1)
        for t in range(NT):
            dve.wait_ge(back, t + 1)
            nc.vector.tensor_tensor(x[:, t, 0:C], PS[t][0:P, 0:C], x[:, t, 0:C], ALU.add)
            into = x[:, t, C:D].rearrange("p (c x) -> p x c", x=3)
            nc.vector.tensor_tensor(into, PS[t][0:P, C:D].rearrange("p (x c) -> p x c", x=3), into, ALU.add)


def rms_norm(nc, K, PS, tag, x, weight, out, outT):
    S, B = K.sem, K.buf
    ss = K.tmp(f"{tag}_ss", [P, NT])
    ms = K.tmp(f"{tag}_ms", [P, NT])
    std = K.tmp(f"{tag}_std", [P, NT])
    rstd = K.tmp(f"{tag}_rstd", [P, NT])
    ms_ready = K.shared("var_ready", 1)
    std_ready = K.shared("std_ready", 1)
    ready = K.shared("normalised", NT)
    turned = K.shared("turned", NT)

    @K.block.vector
    def _(dve):
        ch = Chain(dve, S["dve_chain"], K.dve_n)
        for t in range(NT):
            last = nc.vector.scalar_tensor_tensor(out[:, t, :], x[:, t, :], 1.0, x[:, t, :], ALU.mult, ALU.mult, accum_out=ss[:, t:t + 1])
        ch.step(last)
        nc.vector.tensor_scalar(ms[:], ss[:], 1.0 / D, 1e-6, ALU.mult, ALU.add).then_inc(ms_ready.sem, 1)
        dve.wait_ge(std_ready.sem, std_ready.base + 1)
        ch.step(nc.vector.reciprocal(rstd[:], std[:]))
        for t in range(NT):
            nc.vector.scalar_tensor_tensor(out[:, t, :], x[:, t, :], rstd[:, t:t + 1], weight, ALU.mult, ALU.mult).then_inc(ready.sem, 1)

    @K.block.scalar
    def _(act):
        act.wait_ge(ms_ready.sem, ms_ready.base + 1)
        nc.scalar.activation(std[:], ms[:], ACT.Sqrt).then_inc(std_ready.sem, 1)
        for t in range(NT):
            act.wait_ge(turned.sem, turned.base + t + 1)
            nc.scalar.copy(outT[:, :, nodes(t)], PS[t][:, 0:2 * P].rearrange("p (c n) -> p c n", c=2))

    @K.block.tensor
    def _(pe):
        for t in range(NT):
            pe.wait_ge(ready.sem, ready.base + t + 1)
            for c in range(2):
                last = nc.tensor.transpose(PS[t][:, P * c:P * c + P], out[:, t, 128 * c:128 * c + 128], B["ident"][0:P, 0:P])
            last.then_inc(turned.sem, 1)


def attention_qkv(nc, K, PS, xT, qT, kT, v):
    S, B = K.sem, K.buf
    HQ = NH + NKV
    raw = K.tmp("aq_raw", [P, NT, HQ, HD])
    rot = K.tmp("aq_rot", [P, NT, HQ, HD])
    made, taken, v_taken, ready, turned, turned_out = (K.new(f"aq_{n}") for n in ("made", "taken", "v_taken", "ready", "turned", "turned_out"))

    @K.block.tensor
    def _(pe):
        pe.wait_ge(S["attn_loaded"], 64)
        for t in range(NT):
            if t >= 2:
                pe.wait_ge(taken, t - 1)
                pe.wait_ge(v_taken, t - 1)
            for c in range(2):
                last = nc.tensor.matmul(PS[t % 2][0:P, :], xT[:, c, nodes(t)], B["wattn"][:, c, :], start=(c == 0), stop=(c == 1))
            last.then_inc(made, 1)
        for t in range(NT):
            pe.wait_ge(ready, t + 1)
            if t >= 4:
                pe.wait_ge(turned_out, 2 * (t - 3))
            for b in range(2):
                nc.tensor.transpose(PS[2 + t % 4][:, P * b:P * b + P], rot[:, t, 2 * b:2 * b + 2, :].rearrange("p h d -> p (h d)"), B["ident"][0:P, 0:P])
            nc.tensor.transpose(PS[2 + t % 4][:, 2 * P:3 * P], rot[:, t, NH:HQ, :].rearrange("p h d -> p (h d)"), B["ident"][0:P, 0:P]).then_inc(turned, 1)

    @K.block.vector
    def _(dve):
        ch = Chain(dve, S["dve_chain"], K.dve_n)
        for t in range(NT):
            dve.wait_ge(made, t + 1)
            src = PS[t % 2][0:P, 0:HQ * HD].rearrange("p (h d) -> p h d", h=HQ)
            cos = B["rope"][:, 0, t, :].unsqueeze(1).to_broadcast([P, HQ, HD])
            low = B["rope"][:, 1, t, 0:HD // 2].unsqueeze(1).to_broadcast([P, HQ, HD // 2])
            high = B["rope"][:, 1, t, HD // 2:HD].unsqueeze(1).to_broadcast([P, HQ, HD // 2])
            ch.step(nc.vector.tensor_tensor(rot[:, t, :, 0:HD // 2], src[:, :, HD // 2:HD], low, ALU.mult))
            ch.step(nc.vector.tensor_tensor(rot[:, t, :, HD // 2:HD], src[:, :, 0:HD // 2], high, ALU.mult))
            nc.vector.tensor_tensor(raw[:, t, :, :], src, cos, ALU.mult).then_inc(taken, 1)
            dve.wait_ge(taken, t + 1)
            nc.vector.tensor_tensor(rot[:, t, :, :], rot[:, t, :, :], raw[:, t, :, :], ALU.add).then_inc(ready, 1)

    @K.block.scalar
    def _(act):
        for t in range(NT):
            act.wait_ge(made, t + 1)
            act.wait_ge(taken, t + 1)
            nc.scalar.copy(v[:, t, :], PS[t % 2][0:P, HQ * HD:512]).then_inc(v_taken, 1)
        for t in range(NT):
            act.wait_ge(turned, t + 1)
            nc.scalar.copy(qT[:, :, nodes(t)], PS[2 + t % 4][:, 0:2 * P].rearrange("p (b n) -> p b n", b=2)).then_inc(turned_out, 1)
            nc.scalar.copy(kT[:, nodes(t)], PS[2 + t % 4][:, 2 * P:3 * P]).then_inc(turned_out, 1)


def causal_attention(nc, K, qT, kT, v, y):
    S, B = K.sem, K.buf
    scores = K.tmp("ca_scores", [P, 2, N])
    probs = K.tmp("ca_probs", [P, 2, N])
    probsT = K.tmp("ca_probsT", [P, 2, NT, P])
    top = K.tmp("ca_top", [P, NH * NT, 4])
    ps = [K.psum(f"ca_s{i}", [P, 1024]) for i in range(2)]
    pt = [K.psum(f"ca_t{i}", [P, 512]) for i in range(2)]
    pt4 = K.psum("ca_t4", [P, 512])
    py = K.psum("ca_y", [P, 512])
    scored, masked, topped, exped, turned, copied, summed, normed, inverted = (
        K.new(f"ca_{n}") for n in ("scored", "masked", "topped", "exped", "turned", "copied", "summed", "normed", "inverted"))
    units = [(h, t) for h in range(NH) for t in range(NT)]

    @K.block.tensor
    def _(pe):
        def score(n):
            h, t = units[n]
            at, width = HD * (h // 2), (t + 1) * P
            if n >= 2:
                pe.wait_ge(masked, n - 1)
            for lo in range(0, width, 512):
                hi = min(lo + 512, width)
                last = nc.tensor.matmul(ps[n % 2][:, lo:hi], qT[at:at + HD, h % 2, nodes(t)], kT[at:at + HD, lo:hi], start=True, stop=True, tile_position=(at, 0))
            last.then_inc(scored, 1)

        def turn(n):
            h, t = units[n]
            pe.wait_ge(exped, n + 1)
            if n >= 1:
                pe.wait_ge(copied, n)
            for s in range(t + 1):
                bank, at = (pt[n % 2], P * s) if s < 4 else (pt4, 0)
                last = nc.tensor.transpose(bank[:, at:at + P], probs[:, n % 2, nodes(s)], B["ident"][0:P, 0:P])
            last.then_inc(turned, 1)

        def value(n):
            h, t = units[n]
            pe.wait_ge(copied, n + 1)
            if n >= 1:
                pe.wait_ge(normed, n)
            for s in range(t + 1):
                last = nc.tensor.matmul(py[:, 0:HD], probsT[:, n % 2, s, :], v[:, s, HD * (h // 2):HD * (h // 2) + HD], start=(s == 0), stop=(s == t))
            last.then_inc(summed, 1)

        score(0)
        score(1)
        for n in range(len(units)):
            turn(n)
            if n + 2 < len(units):
                score(n + 2)
            if n >= 1:
                value(n - 1)
        value(len(units) - 1)

    @K.block.vector
    def _(dve):
        ch = Chain(dve, S["dve_chain"], K.dve_n)

        def invert(n):
            dve.wait_ge(exped, n + 1)
            nc.vector.reciprocal(top[:, n, 3:4], top[:, n, 2:3]).then_inc(inverted, 1)

        for n, (h, t) in enumerate(units):
            width = (t + 1) * P
            dve.wait_ge(scored, n + 1)
            if n >= 2:
                dve.wait_ge(exped, n - 1)
            nc.vector.scalar_tensor_tensor(scores[:, n % 2, 0:width], ps[n % 2][:, 0:width], float(HD) ** -0.5, B["causal"][:, N - width:N], ALU.mult, ALU.add).then_inc(masked, 1)
            dve.wait_ge(masked, n + 1)
            ch.step(nc.vector.tensor_reduce(top[:, n, 0:1], scores[:, n % 2, 0:width], AX.X, ALU.max))
            nc.vector.tensor_scalar(top[:, n, 1:2], top[:, n, 0:1], -1.0, None, ALU.mult).then_inc(topped, 1)
            if n >= 1:
                invert(n - 1)
        invert(len(units) - 1)

    @K.block.scalar
    def _(act):
        def copy_turned(n):
            t = units[n][1]
            act.wait_ge(turned, n + 1)
            if n >= 2:
                act.wait_ge(summed, n - 1)
            k = min(t + 1, 4)
            last = nc.scalar.copy(probsT[:, n % 2, 0:k, :].rearrange("p s n -> p (s n)"), pt[n % 2][:, 0:k * P])
            if t == 4:
                last = nc.scalar.copy(probsT[:, n % 2, 4, :], pt4[:, 0:P])
            last.then_inc(copied, 1)

        def finish(n):
            h, t = units[n]
            act.wait_ge(inverted, n + 1)
            act.wait_ge(summed, n + 1)
            nc.scalar.activation(y[:, t, HD * h:HD * h + HD], py[:, 0:HD], ACT.Copy, scale=top[:, n, 3:4]).then_inc(normed, 1)

        for n, (h, t) in enumerate(units):
            width = (t + 1) * P
            act.wait_ge(topped, n + 1)
            if n >= 2:
                act.wait_ge(turned, n - 1)
            nc.scalar.activation(probs[:, n % 2, 0:width], scores[:, n % 2, 0:width], ACT.Exp, bias=top[:, n, 1:2], accum_out=top[:, n, 2:3]).then_inc(exped, 1)
            if n >= 1:
                copy_turned(n - 1)
            if n >= 2:
                finish(n - 2)
        copy_turned(len(units) - 1)
        finish(len(units) - 2)
        finish(len(units) - 1)


def load_experts(nc, K, A, w13, w2):
    @K.block.sync
    def _(sp):
        for e in range(NE):
            for j, w in enumerate((A["e1"], A["e3"])):
                at = (2 * e + j) * 2 * HID
                sp.dma_start(w13[:, at:at + 2 * HID].rearrange("p (c n) -> p c n", c=2), w[e].rearrange("(c p) n -> p c n", p=128)).then_inc(K.sem["experts_loaded"], 16)
            at = e * NC * D
            sp.dma_start(w2[:, at:at + (NC - 1) * D].rearrange("p (c d) -> p c d", d=D),
                         A["e2"][e, 0:(NC - 1) * HC, :].rearrange("(c p) d -> p c d", p=HC)).then_inc(K.sem["experts_loaded"], 16)
            sp.dma_start(w2[0:HID - (NC - 1) * HC, at + (NC - 1) * D:at + NC * D], A["e2"][e, (NC - 1) * HC:HID, :]).then_inc(K.sem["experts_loaded"], 16)


def dispatch(nc, K, PS, xT, flat, flat_rows, share, slots, token_of, expert_of):
    S, B = K.sem, K.buf
    names = "logits masked score rest full place inner".split()
    logits, masked, score, rest, full, place, inner = (K.tmp(f"di_{n}", [P, NT, NE]) for n in names)
    pick = K.tmp("di_pick", [P, TOP, NT, NE])
    chosen = K.tmp("di_chosen", [P, TOP, NT, NE])
    best = K.tmp("di_best", [P, NT])
    total = K.tmp("di_total", [P, NT])
    tile = K.tmp("di_tile", [P, TOP, NT])
    where = K.tmp("di_where", [P, TOP, NT])
    hundreds = K.tmp("di_hundreds", [P, NT])
    more = K.tmp("di_more", [P, NE, NT])
    fuller = K.tmp("di_fuller", [P, NT * NE, NT - 1])
    PAD = NE // 2
    before_e = [K.tmp(f"di_before_e{i}", [P, PAD + NE]) for i in range(2)]
    begun = K.tmp("di_begun", [1, WORK, NE - 1])
    expert = K.tmp("di_expert", [1, WORK])
    total_e = K.tmp("di_total_e", [P, NE])
    own_row = K.tmp("di_own_row", [P, 1])
    own_tile = K.tmp("di_own_tile", [P, TOP * NT])
    both = K.tmp("di_both", [P, NT, NE], BF16)
    before = K.tmp("di_before", [P, P], BF16)
    ones = K.tmp("di_ones", [P, P], BF16)
    in_tile = K.tmp("di_in_tile", [P, TOP * NT, WORK])
    rows_in_tile = K.tmp("di_rows_in_tile", [P, TOP * NT, 2, WORK], BF16)
    at_place = K.tmp("di_at_place", [P, TOP * NT, 128], BF16)
    tile_part = K.tmp("di_tile_part", [128, WORK])
    routed, ready, exped, counting, counted, placing, placed, consts = (
        K.new(f"di_{n}") for n in ("routed", "ready", "exped", "counting", "counted", "placing", "placed", "consts"))

    @K.block.sync
    def _(sp):
        sp.dma_start(flat_rows.rearrange("(t p) d -> p t d", p=P), flat[:]).then_inc(S["flat_stored"], 16)
        sp.wait_ge(S["flat_stored"], 16)

    @K.block.gpsimd
    def _(pool):
        pool.iota(own_row[:], pattern=[[0, 1]], base=0, channel_multiplier=1, allow_small_or_imprecise_dtypes=True).then_inc(consts, 1)
        pool.iota(own_tile[:], pattern=[[0, TOP], [1, NT]], base=0, channel_multiplier=0, allow_small_or_imprecise_dtypes=True).then_inc(consts, 1)
        pool.iota(hundreds[:], pattern=[[128, NT]], base=0, channel_multiplier=0, allow_small_or_imprecise_dtypes=True).then_inc(consts, 1)
        for i in range(2):
            pool.memset(before_e[i][:], 0.0).then_inc(consts, 1)
        pool.memset(ones[:], 1.0).then_inc(consts, 1)
        pool.memset(before[:], 1.0).then_inc(consts, 1)
        pool.wait_ge(consts, 7)
        pool.affine_select(out=before[:], in_=before[:], compare_op=ALU.is_ge, fill=0.0, base=-1,
                           pattern=[[1, P]], channel_multiplier=-1).then_inc(consts, 1)

    @K.block.tensor
    def _(pe):
        for t in range(NT):
            for c in range(2):
                last = nc.tensor.matmul(PS[0][0:P, NE * t:NE * t + NE], xT[:, c, nodes(t)], B["router1"][:, c, :], start=(c == 0), stop=(c == 1))
        last.then_inc(routed, 1)
        pe.wait_ge(consts, 8)
        pe.wait_ge(counting, 1)
        nc.tensor.matmul(PS[2][0:P, 0:NT * NE], ones[:], both[:].rearrange("p t e -> p (t e)"), start=True, stop=True).then_inc(counted, 1)
        last = nc.tensor.matmul(PS[1][0:P, 0:NT * NE], before[:], both[:].rearrange("p t e -> p (t e)"), start=True, stop=False)
        for t in range(1, NT):
            for u in range(t):
                last = nc.tensor.matmul(PS[1][0:P, NE * t:NE * t + NE], ones[:], both[:, u, :], start=False, stop=(t == NT - 1 and u == t - 1))
        last.then_inc(counted, 1)
        pe.wait_ge(placing, 1)
        for i in range(TOP * NT):
            last = nc.tensor.matmul(PS[3][:, 0:2 * WORK], at_place[:, i, :], rows_in_tile[:, i, :, :].rearrange("p a w -> p (a w)"), start=(i == 0), stop=(i == TOP * NT - 1))
        last.then_inc(placed, 1)

    @K.block.scalar
    def _(act):
        act.wait_ge(ready, 1)
        nc.scalar.activation(logits[:], logits[:], ACT.Exp).then_inc(exped, 1)

    @K.block.vector
    def _(dve):
        ch = Chain(dve, S["dve_chain"], K.dve_n)

        def wide(a):
            return a[:].unsqueeze(2).to_broadcast([P, NT, NE])

        def both_choices(a):
            return a[:].rearrange("p t e -> p (t e)").unsqueeze(1).to_broadcast([P, TOP, NT * NE])

        def of_choice(a, out):
            ch.step(nc.vector.tensor_tensor(chosen[:].rearrange("p s t e -> p s (t e)"), pick[:].rearrange("p s t e -> p s (t e)"), both_choices(a), ALU.mult))
            ch.step(nc.vector.tensor_reduce(out[:].rearrange("p s t -> p (s t)"), chosen[:].rearrange("p s t e -> p (s t) e"), AX.X, ALU.add))

        dve.wait_ge(routed, 1)
        ch.step(nc.vector.tensor_copy(logits[:], PS[0][0:P, 0:NT * NE].rearrange("p (t e) -> p t e", t=NT)))
        ch.step(nc.vector.tensor_reduce(best[:], logits[:], AX.X, ALU.max))
        nc.vector.tensor_tensor(logits[:], logits[:], wide(best), ALU.subtract).then_inc(ready, 1)
        dve.wait_ge(exped, 1)
        ch.step(nc.vector.tensor_reduce(total[:], logits[:], AX.X, ALU.add))
        ch.step(nc.vector.reciprocal(total[:], total[:]))
        ch.step(nc.vector.tensor_tensor(logits[:], logits[:], wide(total), ALU.mult))
        first_of(nc, ch, logits, masked, score, best, B["count"], NE, pick[:, 0])
        ch.step(nc.vector.scalar_tensor_tensor(rest[:], pick[:, 0], -2.0, logits[:], ALU.mult, ALU.add))
        first_of(nc, ch, rest, masked, score, best, B["count"], NE, pick[:, 1])
        nc.vector.tensor_tensor(both[:], pick[:, 0], pick[:, 1], ALU.add).then_inc(counting, 1)
        of_choice(logits, share)
        ch.step(nc.vector.tensor_tensor(total[:], share[:, 0, :], share[:, 1, :], ALU.add))
        ch.step(nc.vector.tensor_scalar(total[:], total[:], 1e-9, None, ALU.add))
        ch.step(nc.vector.reciprocal(total[:], total[:]))
        nc.vector.tensor_tensor(share[:], share[:], total[:].unsqueeze(1).to_broadcast([P, TOP, NT]), ALU.mult)

        dve.wait_ge(consts, 8)
        dve.wait_ge(counted, 1)
        ch.step(nc.vector.tensor_reduce(total_e[:], PS[2][0:P, 0:NT * NE].rearrange("p (t e) -> p e t", t=NT), AX.X, ALU.add))
        ch.step(nc.vector.tensor_tensor(more[:], total_e[:].unsqueeze(2).to_broadcast([P, NE, NT]), hundreds[:].unsqueeze(1).to_broadcast([P, NE, NT]), ALU.is_gt))
        ch.step(nc.vector.tensor_reduce(before_e[0][:, PAD:], more[:], AX.X, ALU.add))
        for i, k in enumerate((1, 2, 4)):
            a, b = before_e[i % 2], before_e[1 - i % 2]
            ch.step(nc.vector.tensor_tensor(b[:, PAD:], a[:, PAD:], a[:, PAD - k:PAD - k + NE], ALU.add))
        base = before_e[1][:, PAD - 1:PAD + NE - 1]
        dve.wait_ge(counted, 2)
        rank = PS[1][0:P, 0:NT * NE]
        ch.step(nc.vector.tensor_tensor(fuller[:], rank.unsqueeze(2).to_broadcast([P, NT * NE, NT - 1]),
                                        hundreds[:, 1:NT].unsqueeze(1).to_broadcast([P, NT * NE, NT - 1]), ALU.is_ge))
        ch.step(nc.vector.tensor_reduce(full[:].rearrange("p t e -> p (t e)"), fuller[:], AX.X, ALU.add))
        ch.step(nc.vector.tensor_tensor(place[:], full[:], base.unsqueeze(1).to_broadcast([P, NT, NE]), ALU.add))
        ch.step(nc.vector.scalar_tensor_tensor(inner[:].rearrange("p t e -> p (t e)"), full[:].rearrange("p t e -> p (t e)"), -128.0, rank, ALU.mult, ALU.add))
        of_choice(place, tile)
        of_choice(inner, where)
        counts = B["iota"][0:P, :]

        def over(a, n):
            return a[:].rearrange("p s t -> p (s t)").unsqueeze(2).to_broadcast([P, TOP * NT, n])

        nc.vector.tensor_tensor(at_place[:], over(where, 128), counts[:, 0:128].unsqueeze(1).to_broadcast([P, TOP * NT, 128]), ALU.is_equal)
        ch.step(nc.vector.tensor_tensor(in_tile[:], over(tile, WORK), counts[:, 0:WORK].unsqueeze(1).to_broadcast([P, TOP * NT, WORK]), ALU.is_equal))
        nc.vector.tensor_scalar(rows_in_tile[:, :, 0, :], in_tile[:], own_row[:, 0:1], None, ALU.mult)
        nc.vector.tensor_tensor(rows_in_tile[:, :, 1, :], in_tile[:], own_tile[:].unsqueeze(2).to_broadcast([P, TOP * NT, WORK]), ALU.mult).then_inc(placing, 1)
        ch.step(nc.vector.memset(slots[:], 0))
        nc.vector.scalar_tensor_tensor(slots[0:P, :], tile[:].rearrange("p s t -> p (s t)"), 128.0, where[:].rearrange("p s t -> p (s t)"), ALU.mult, ALU.add)
        ch.step(nc.vector.tensor_tensor(begun[:], base[0:1, 1:NE].unsqueeze(1).to_broadcast([1, WORK, NE - 1]),
                                        counts[0:1, 0:WORK].unsqueeze(2).to_broadcast([1, WORK, NE - 1]), ALU.is_le))
        ch.step(nc.vector.tensor_reduce(expert[:], begun[:], AX.X, ALU.add))
        nc.vector.tensor_copy(expert_of[:, 0:WORK], expert[:])
        nc.vector.tensor_copy(expert_of[:, WORK:WORK + 1], before_e[1][0:1, PAD + NE - 1:PAD + NE])
        dve.wait_ge(placed, 1)
        ch.step(nc.vector.tensor_copy(tile_part[:], PS[3][:, WORK:2 * WORK]))
        nc.vector.scalar_tensor_tensor(token_of[:], tile_part[:], float(P), PS[3][:, 0:WORK], ALU.mult, ALU.add)


def mixture(nc, K, w13, w2, flat_rows, results, share, slots, token_of, expert_of, x, out):
    S, B = K.sem, K.buf
    RING = 4
    got = K.tmp("mx_got", [128, RING, D])
    fT = K.tmp("mx_fT", [128, 2, 2, 128])
    gate = K.tmp("mx_gate", [128, HID])
    hid = K.tmp("mx_hid", [128, 2, HID])
    hidT = K.tmp("mx_hidT", [HC, NC, 128])
    y = K.tmp("mx_y", [128, 2, D])
    a, b = K.psum("mx_a", [128, 1024]), K.psum("mx_b", [128, 1024])
    ta, tb = K.psum("mx_ta", [128, 512]), K.psum("mx_tb", [128, 512])
    down = [K.psum(f"mx_down{i}", [128, 512]) for i in range(2)]
    got_sem = [K.new(f"mx_got{i}") for i in range(RING)]
    stored = [K.new(f"mx_stored{i}") for i in range(2)]
    made1, made3, gated, multiplied, turned, fT_ready, hid_turned, hidT_a, hidT_b, summed, taken = (
        K.new(f"mx_{n}") for n in ("made1", "made3", "gated", "multiplied", "turned", "fT_ready", "hid_turned", "hidT_a", "hidT_b",
                                   "summed", "taken"))
    back = [Signal(got_sem[t], 16 * ((WORK + RING - 1 - t) // RING)) for t in range(RING)] + [Signal(K.new("mx_back"), 0)]
    last_rows = HID - (NC - 1) * HC

    def size(c):
        return HC if c < NC - 1 else last_rows

    @K.block.gpsimd
    def _(pool):
        for w in range(WORK):
            if w >= RING:
                pool.wait_ge(turned, w - RING + 1)
            nc.gpsimd.indirect_dma_start(got[:, w % RING, :], None, flat_rows,
                                         bass.IndirectOffsetOnAxis(ap=token_of[:, w:w + 1], axis=0)).then_inc(got_sem[w % RING], 16)
        for i in range(2):
            pool.wait_ge(stored[i], 16 * ((WORK + 1 - i) // 2))
        for t in range(NT):
            for i in (t, NT + t):
                nc.gpsimd.indirect_dma_start(w13[:, i * D:(i + 1) * D], None, results,
                                             bass.IndirectOffsetOnAxis(ap=slots[:, i:i + 1], axis=0)).then_inc(back[t].sem, 16)

    @K.block.sync
    def _(sp):
        for w in range(WORK):
            sp.wait_ge(taken, w + 1)
            sp.dma_start(results[128 * w:128 * w + 128, :], y[:, w % 2, :]).then_inc(stored[w % 2], 16)

    @K.block.tensor
    def _(pe):
        tiles = pe.value_load(expert_of[:, WORK:WORK + 1], min_val=LEAST, max_val=WORK)

        def in_use(w, products):
            if w < LEAST:
                products()
            else:
                with pe.If(tiles > w):
                    products()

        def up(w, j, e, bank, before, made):
            if w >= 1:
                pe.wait_ge(before, w)
            def product(lo, hi):
                for c in range(2):
                    last = nc.tensor.matmul(bank[:, lo:hi], fT[:, w % 2, c, :], w13[:, bass.ds(e * (4 * HID) + (2 * j + c) * HID + lo, hi - lo)],
                                            start=(c == 0), stop=(c == 1))
                return last

            in_use(w, lambda: product(0, 512))
            product(512, HID).then_inc(made, 1)

        def turn(w):
            if w >= 1:
                pe.wait_ge(fT_ready, w)
            pe.wait_ge(got_sem[w % RING], 16 * (w // RING + 1))
            for c in range(2):
                last = nc.tensor.transpose(tb[:, 256 + 128 * c:384 + 128 * c], got[:, w % RING, 128 * c:128 * c + 128], B["ident"][:])
            last.then_inc(turned, 1)

        def turn_hidden(w):
            pe.wait_ge(multiplied, w + 1)
            if w >= 1:
                pe.wait_ge(hidT_a, w)
                pe.wait_ge(hidT_b, w)
            for c in range(NC):
                bank, at = (ta, 128 * c) if c < 4 else (tb, 128 * (c - 4))
                last = nc.tensor.transpose(bank[0:size(c), at:at + 128], hid[:, w % 2, c * HC:c * HC + size(c)], B["ident"][:])
            last.then_inc(hid_turned, 1)

        def bring_down(w, e):
            pe.wait_ge(hidT_a, w + 1)
            pe.wait_ge(hidT_b, w + 1)
            if w >= 2:
                pe.wait_ge(taken, w - 1)
            def product(c):
                return nc.tensor.matmul(down[w % 2][:, 0:D], hidT[0:size(c), c, :], w2[0:size(c), bass.ds(e * (NC * D) + c * D, D)], start=(c == 0), stop=(c == NC - 1))

            product(0)
            in_use(w, lambda: [product(c) for c in range(1, NC - 1)])
            product(NC - 1).then_inc(summed, 1)

        pe.wait_ge(S["experts_loaded"], 16 * 4 * NE)
        turn(0)
        e = [pe.value_load(expert_of[:, w:w + 1], min_val=0, max_val=NE - 1) for w in range(2)]
        for w in range(WORK):
            pe.wait_ge(fT_ready, w + 1)
            up(w, 0, e[w], a, gated, made1)
            if w >= 1:
                turn_hidden(w - 1)
            if w + 1 < WORK:
                turn(w + 1)
            up(w, 1, e[w], b, multiplied, made3)
            if w + 2 < WORK:
                e.append(pe.value_load(expert_of[:, w + 2:w + 3], min_val=0, max_val=NE - 1))
            if w >= 1:
                bring_down(w - 1, e[w - 1])
        turn_hidden(WORK - 1)
        bring_down(WORK - 1, e[WORK - 1])

    @K.block.scalar
    def _(act):
        def copy_hidden(w):
            act.wait_ge(hid_turned, w + 1)
            if w >= 1:
                act.wait_ge(summed, w)
            nc.scalar.copy(hidT[:, 0:4, :].rearrange("p c n -> p (c n)"), ta[0:HC, :]).then_inc(hidT_a, 1)

        for w in range(WORK):
            act.wait_ge(made1, w + 1)
            if w >= 1:
                act.wait_ge(multiplied, w)
            nc.scalar.activation(gate[:], a[:, 0:HID], ACT.Silu).then_inc(gated, 1)
            if w >= 1:
                copy_hidden(w - 1)
        copy_hidden(WORK - 1)

    @K.block.vector
    def _(dve):
        def copy_rows(w):
            dve.wait_ge(turned, w + 1)
            if w >= 2:
                dve.wait_ge(made3, w - 1)
            nc.vector.tensor_copy(fT[:, w % 2, :, :], tb[:, 256:512].rearrange("p (c n) -> p c n", c=2)).then_inc(fT_ready, 1)

        def copy_hidden(w):
            dve.wait_ge(hid_turned, w + 1)
            if w + 2 < WORK:
                dve.wait_ge(turned, w + 3)
            if w >= 1:
                dve.wait_ge(summed, w)
            nc.vector.tensor_copy(hidT[0:HC, 4, :], tb[0:HC, 0:128])
            nc.vector.tensor_copy(hidT[0:last_rows, 5, :], tb[0:last_rows, 128:256]).then_inc(hidT_b, 1)

        def take(w):
            dve.wait_ge(summed, w + 1)
            if w >= 2:
                dve.wait_ge(stored[w % 2], 16 * (w // 2))
            nc.vector.tensor_copy(y[:, w % 2, :], down[w % 2][:, 0:D]).then_inc(taken, 1)

        copy_rows(0)
        ch = Chain(dve, S["dve_chain"], K.dve_n)
        ch.step(nc.vector.tensor_tensor(out[:], x[:], out[:], ALU.add))
        for w in range(WORK):
            if w >= 1:
                copy_hidden(w - 1)
            if w + 1 < WORK:
                copy_rows(w + 1)
            dve.wait_ge(gated, w + 1)
            dve.wait_ge(made3, w + 1)
            if w >= 2:
                dve.wait_ge(hid_turned, w - 1)
            nc.vector.tensor_tensor(hid[:, w % 2, :], b[:, 0:HID], gate[:], ALU.mult).then_inc(multiplied, 1)
            if w >= 1:
                take(w - 1)
        copy_hidden(WORK - 1)
        take(WORK - 1)
        for t in range(NT):
            dve.wait_ge(back[t].sem, back[t].base + 16 * TOP)
            for s in range(TOP):
                ch.step(nc.vector.scalar_tensor_tensor(out[:, t, :], w13[0:P, (s * NT + t) * D:(s * NT + t + 1) * D], share[:, s, t:t + 1], out[:, t, :], ALU.mult, ALU.add))


def program(nc, A, out):
    with ExitStack() as whole:
        K = Kernel()
        S, B = K.sem, K.buf
        K.new = lambda name: whole.enter_context(nc.semaphore(name))
        for name in ("x_loaded rows_loaded eint_loaded w1_loaded w2_loaded mix0_loaded ffn0_loaded f2_loaded gnn1_loaded mix1_loaded attn_loaded "
                     "experts_loaded flat_stored gate idx_copied m123_loaded rbf_loaded zeroed pool_chain consts dve_chain ei_dve ei_pe").split():
            S[name] = K.new(name)

        signals = {}

        for n in ("free", "filled", "hot"):
            for b in range(BUFS):
                S[f"{n}{b}"] = K.new(f"{n}{b}")

        def shared(name, total):
            if name not in signals:
                signals[name] = [K.new(name), 0]
            sem, base = signals[name]
            signals[name][1] += total
            return Signal(sem, base)

        K.shared = shared

        def keep(name, shape, dt=F32):
            t = whole.enter_context(nc.sbuf_tensor(name, shape, dt))
            B[name] = t
            return t

        def dram(name, shape):
            return nc.dram_tensor(name, shape, F32).ap()

        keep("x", [P, NT, D])
        keep("rows", [P, NROWS])
        keep("ident", [128, 128])
        keep("causal", [P, N])
        keep("iota", [128, 2 * P])
        keep("count", [P, E0])
        keep("wattn", [128, 2, 512])
        keep("wo", [128, 2, D])
        keep("router1", [128, 2, NE])
        keep("rope", [P, 2, NT, HD])
        keep("actT", [128, 2, N])
        keep("h", [P, NT, D])
        graph = whole.enter_context(ExitStack())
        for name, shape, dt in (
                ("eint", [128, 3, ET], I32), ("dst_rows", [GROUPS, GROUP * 128], I32), ("src_idx", [128, ET], I32),
                ("rel_idx", [128, ET], I32), ("dst_rel", [128, PASSES, ET], F32), ("chunk_at", [1, PASSES, GROUPS], I32),
                ("npass", [1, 1], I32), ("spans", [1, PASSES, GROUPS], I32), ("router0", [128, 2, E0], F32),
                ("f1b", [128, E0 * HID0 // 128], F32), ("f2b", [E0, D], F32), ("c64", [C, 8 * C + 12], F32),
                ("m4", [2 * C, 4 * C], F32), ("m123", [128, 3, 128], F32), ("sh", [128, ET, 4], F32),
                ("wqkv1", [128, 2, 384], F32), ("wout1", [128, D], F32), ("total", [P, NT, D], F32), ("outT", [128, N], F32),
                ("taylor_a", [P, 1], F32)):
            B[name] = graph.enter_context(nc.sbuf_tensor(name, shape, dt))
        edge_mem = whole.enter_context(ExitStack())
        B["r"] = edge_mem.enter_context(nc.sbuf_tensor("edge_units", [128, EP // 2], F32))
        wide_mem = whole.enter_context(ExitStack())
        B["W"] = wide_mem.enter_context(nc.sbuf_tensor("wide_weights", [128, 2, R, D], F32))
        early = whole.enter_context(ExitStack())
        for name, shape in (("self1", [128, 2, D]), ("self2", [128, 2, D]), ("wqkv0", [128, 2, 768]), ("wproj0", [128, 2, D])):
            B[name] = early.enter_context(nc.sbuf_tensor(name, shape, F32))
        table0, table1 = dram("table0", [R, N, D]), dram("table1", [R, N, D])

        class stage:

            def __enter__(self):
                self.mem = ExitStack()
                K.tmp = lambda name, shape, dt=F32: self.mem.enter_context(nc.sbuf_tensor(name, shape, dt))
                K.psum = lambda name, shape: self.mem.enter_context(nc.psum_tensor(name, shape, F32))
                self.block = nc.Block()
                K.block = self.block.__enter__()
                return lambda n, tag: [K.psum(f"{tag}_ps{i}", [128, 512]) for i in range(n)]

            def __exit__(self, *args):
                self.block.__exit__(*args)
                self.mem.close()

        def finished():
            with stage() as _:
                stored = K.new("out_stored")

                @K.block.sync
                def _(sp):
                    sp.dma_start(out.rearrange("(t p) d -> p t d", p=P), K.last[:]).then_inc(stored, 16)
                    sp.wait_ge(stored, 16)

        with stage() as banks:
            load_all(nc, K, A)
            layer_norm(nc, K, banks(NT, "ln0"), "ln0", B["x"], B["h"], B["actT"])
            edge_indices(nc, K, banks(2, "ei"))
        K.last = B["h"]
        with ExitStack() as mix:
            qkT = mix.enter_context(nc.sbuf_tensor("mix_qkT", [128, 4, N], F32))
            v1 = mix.enter_context(nc.sbuf_tensor("mix_v1", [P, NT, H0, HD0 + 1], F32))
            with stage() as banks:
                ps = banks(8, "t0")
                made = rgcn_tables(nc, K, ps[0:6], "t0", B["actT"], B["W"], B["self1"], S["w1_loaded"], table0, row(K, "gnn_b1"), B["total"])

                @K.block.sync
                def _(sp):
                    sp.wait_ge(made.sem, made.base + (R // 2 + 1) * NT)
                    for c in range(2):
                        sp.dma_start(B["W"][:, c, :, :], A["W2"][:, 128 * c:128 * c + 128, :].rearrange("r p n -> p r n")).then_inc(S["w2_loaded"], 16)
                taylor_qkv(nc, K, ps, qkT, v1, B["actT"])
            sums = B["wqkv0"][0:P].rearrange("p c n -> p (c n)")[:, 0:NT * H0 * (HD0 + 1)].rearrange("p (t h d) -> p t h d", t=NT, h=H0)
            network = EdgeNetwork(nc, K, B["r"])

            def both(one, other):
                def run(slot):
                    one(slot)
                    other(slot)
                return run

            with stage() as _:
                heads = Taylor(nc, K, 0, qkT, v1, sums)
                pe, act = network.pieces("e0", 0, 2)
                rgcn_edges(nc, K, 0, table0.rearrange("r n d -> (r n) d"), B["total"], True, B["h"],
                           {"pe": both(heads.pe, pe), "act": both(heads.act, act), "dve": lambda slot: None})
            with stage() as banks:
                to_feature_major(nc, K, banks(NT, "h1"), "h1", lambda t: [B["h"][:, t, 0:128], B["h"][:, t, 128:256]], B["actT"])
            with stage() as banks:
                rgcn_tables(nc, K, banks(6, "t1"), "t1", B["actT"], B["W"], B["self2"], S["w2_loaded"], table1, row(K, "gnn_b2"), B["total"])
            with stage() as _:
                @K.block.sync
                def _(sp):
                    sp.dma_start(B["W"][:].rearrange("p c r n -> p c (r n)"), A["f1"].rearrange("(c p) n -> p c n", p=128)).then_inc(S["ffn0_loaded"], 16)
                heads = Taylor(nc, K, TAYLOR, qkT, v1, sums)
                pe, act = network.pieces("e1", 2 * LOOPS, 4)
                rgcn_edges(nc, K, 1, table1.rearrange("r n d -> (r n) d"), B["total"], False, B["h"],
                           {"pe": both(heads.pe, pe), "act": both(heads.act, act), "dve": lambda slot: None})
            y = mix.enter_context(nc.sbuf_tensor("mix_y", [P, NT, D], F32))
            with stage() as banks:
                taylor_end(nc, K, banks(1, "te"), v1, sums, y)
            with stage() as banks:
                to_feature_major(nc, K, banks(NT, "ty"), "ty", lambda t: [y[:, t, 0:128], y[:, t, 128:256]], B["actT"])
            with stage() as banks:
                project_add(nc, K, banks(NT, "pm"), "pm", B["actT"], B["wproj0"], (S["mix0_loaded"], 32),
                            lambda t: [B["x"][:, t, :], row(K, "bproj"), B["h"][:, t, :]], B["x"])
        early.close()
        K.last = B["x"]
        with ExitStack() as ffn:
            hidT = ffn.enter_context(nc.sbuf_tensor("ffn_hidT", [128, E0 * HID0 // 128, N], F32))
            f2 = ffn.enter_context(nc.sbuf_tensor("f2", [128, E0 * HID0 // 128, D], F32))
            with stage() as banks:
                @K.block.sync
                def _(sp):
                    sp.dma_start(f2[:], A["f2"].rearrange("(c p) n -> p c n", p=128)).then_inc(S["f2_loaded"], 16)
                layer_norm(nc, K, banks(NT, "ln1"), "ln1", B["x"], B["h"], B["actT"])
            with stage() as banks:
                routed_ffn(nc, K, banks(8, "rf"), B["x"], B["actT"], hidT, f2)
        wide_mem.close()
        up = dram("table2", [N, D])
        with ExitStack() as gnn:
            hT = gnn.enter_context(nc.sbuf_tensor("gnn_hT", [C, 4, N], F32))
            with stage() as banks:
                layer_norm(nc, K, banks(NT, "ln2"), "ln2", B["x"], B["h"], B["actT"])
            with stage() as banks:
                equivariant_tables(nc, K, banks(NT, "et"), B["h"], hT, up)
            with stage() as _:
                equivariant_edges(nc, K, up, B["r"], B["total"])
            with stage() as banks:
                equivariant_nodes(nc, K, banks(8, "eq"), B["total"], hT, B["x"])
        edge_mem.close()
        with stage() as banks:
            project_add(nc, K, banks(NT, "pl"), "pl", B["outT"][:].unsqueeze(1), B["wout1"][:].unsqueeze(1), (S["mix1_loaded"], 32),
                        lambda t: [B["x"][:, t, :], row(K, "b_out")], B["x"])
        graph.close()
        xn = whole.enter_context(nc.sbuf_tensor("attn_xn", [P, NT, D], F32))
        w13 = whole.enter_context(nc.sbuf_tensor("experts_w13", [128, NE * 4 * HID], F32))
        w2 = whole.enter_context(nc.sbuf_tensor("experts_w2", [HC, NE * NC * D], F32))
        with ExitStack() as attn:
            qT = attn.enter_context(nc.sbuf_tensor("attn_qT", [128, 2, N], F32))
            kT = attn.enter_context(nc.sbuf_tensor("attn_kT", [128, N], F32))
            v = attn.enter_context(nc.sbuf_tensor("attn_v", [P, NT, NKV * HD], F32))
            with stage() as banks:
                layer_norm(nc, K, banks(NT, "ln3"), "ln3", B["x"], xn, B["actT"])
            with stage() as banks:
                rms_norm(nc, K, banks(NT, "rn1"), "rn1", xn, row(K, "ln1"), B["h"], B["actT"])
            with stage() as banks:
                attention_qkv(nc, K, banks(6, "aq"), B["actT"], qT, kT, v)
            with stage() as _:
                load_experts(nc, K, A, w13, w2)
                causal_attention(nc, K, qT, kT, v, B["h"])
            with stage() as banks:
                to_feature_major(nc, K, banks(NT, "ay"), "ay", lambda t: [B["h"][:, t, 0:128], B["h"][:, t, 128:256]], B["actT"])
            with stage() as banks:
                project_add(nc, K, banks(NT, "pa"), "pa", B["actT"], B["wo"], (S["attn_loaded"], 64), lambda t: [xn[:, t, :]], xn)
        share = whole.enter_context(nc.sbuf_tensor("moe_share", [P, TOP, NT], F32))
        slots = whole.enter_context(nc.sbuf_tensor("moe_slots", [128, TOP * NT], I32))
        token_of = whole.enter_context(nc.sbuf_tensor("moe_token_of", [128, WORK], I32))
        expert_of = whole.enter_context(nc.sbuf_tensor("moe_expert_of", [1, WORK + 1], I32))
        flat_rows, results = dram("flat_rows", [N, D]), dram("expert_results", [WORK * 128, D])
        with stage() as banks:
            rms_norm(nc, K, banks(NT, "rn2"), "rn2", xn, row(K, "ln2"), B["h"], B["actT"])
        with stage() as banks:
            dispatch(nc, K, banks(4, "di"), B["actT"], B["h"], flat_rows, share, slots, token_of, expert_of)
        with stage() as _:
            mixture(nc, K, w13, w2, flat_rows, results, share, slots, token_of, expert_of, B["x"], xn)
        K.last = xn
        finished()


def kernel(**inputs):
    import numpy as _np
    import concourse.bacc as _bacc
    from concourse import mybir as _mybir
    from concourse.bass_utils import run_bass_kernel_spmd as _run

    I = {k: _np.asarray(v) for k, v in inputs.items()}

    def padded(a, fill):
        return _np.concatenate([a, _np.full((EP - E,) + a.shape[1:], fill, a.dtype)])


    src, typ, dst = padded(I["src"], 0), padded(I["edge_type_8"], 0), padded(I["dst"], -1)
    inv_freq = 1.0 / 10000.0 ** (_np.arange(0, HD, 2, dtype=_np.float32) / HD)
    freqs = _np.outer(_np.arange(N, dtype=_np.float32), inv_freq)
    emb = _np.concatenate([freqs, freqs], axis=-1)
    sin = _np.sin(emb)
    rope = _np.stack([_np.cos(emb), _np.concatenate([-sin[:, :HD // 2], sin[:, HD // 2:]], axis=-1)]).astype(_np.float32)
    rows = _np.concatenate([I["L0_gnn_b1"], I["L0_gnn_b2"], I["L0_mix_bqkv"], I["L0_mix_bproj"],
                            I["L0_mix_temperature"].reshape(-1), I["L0_ffn_router_b"], I["L1_mix_b_out"],
                            I["L1_ffn_ln1_w"], I["L1_ffn_ln2_w"]])
    arrays = {
        "x": I["x"], "rows": rows,
        "eint": _np.stack([a.reshape(ET, 128).T for a in (src, typ, dst)], axis=1),
        "dst_rows": dst.reshape(GROUPS, GROUP * 128),
        "W1": I["L0_gnn_W1"], "self1": I["L0_gnn_self_w1"], "W2": I["L0_gnn_W2"], "self2": I["L0_gnn_self_w2"],
        "wqkv0": I["L0_mix_Wqkv"].T, "wproj0": I["L0_mix_Wproj"].T,
        "router0": I["L0_ffn_router_w"].T,
        "f1": I["L0_ffn_W1"].transpose(1, 0, 2).reshape(D, E0 * HID0),
        "f1b": I["L0_ffn_b1"].reshape(-1, 128).T,
        "f2": I["L0_ffn_W2"].reshape(E0 * HID0, D), "f2b": I["L0_ffn_b2"],
        "c64": _np.concatenate([I["L1_gnn_" + n] for n in ("W_up0", "W_up1", "W_lin0", "W_lin1")]
                               + [I["L1_gnn_WB0"], I["L1_gnn_WB1"], I["L1_gnn_Wc0"], I["L1_gnn_Wc1"],
                                  I["L1_gnn_gamma0"][:, None], I["L1_gnn_beta0"][:, None], I["L1_gnn_gamma1"][:, None]], axis=1),
        "m1": I["L1_gnn_M1"], "m2": I["L1_gnn_M2"], "m3": I["L1_gnn_M3"], "m4": I["L1_gnn_M4"],
        "sh": padded(I["edge_attr_4"], 0).reshape(ET, 128, 4).transpose(1, 0, 2),
        "rbf": padded(I["edge_attr_16"], 0).reshape(EP // 1024, 2, 512, 16).transpose(1, 3, 0, 2).reshape(32, EP // 2),
        "wqkv1": I["L1_mix_W_qkv"], "wout1": I["L1_mix_W_out"],
        "wattn": _np.concatenate([I["L1_ffn_wq"].reshape(NH, HD, D)[[0, 2, 1, 3]].reshape(NH * HD, D), I["L1_ffn_wk"], I["L1_ffn_wv"]]).T,
        "wo": I["L1_ffn_wo"].T, "router1": I["L1_ffn_router_w"].T, "rope": rope,
        "e1": I["L1_ffn_w1"].transpose(0, 2, 1), "e3": I["L1_ffn_w3"].transpose(0, 2, 1), "e2": I["L1_ffn_w2"].transpose(0, 2, 1),
    }
    arrays["c64"] = _np.concatenate([arrays["c64"], I["L1_gnn_Wsc0"], I["L1_gnn_Wsc1"]], axis=1)
    nc = _bacc.Bacc("TRN2", target_bir_lowering=False, num_devices=1)
    A, fed = {}, {}
    for name, a in arrays.items():
        fed[f"{name}_dram"] = a = _np.ascontiguousarray(a)
        A[name] = nc.dram_tensor(f"{name}_dram", a.shape, _mybir.dt.from_np(a.dtype), kind="ExternalInput").ap()
    out = nc.dram_tensor("out_dram", (N, D), F32, kind="ExternalOutput").ap()
    program(nc, A, out)
    r = _run(nc, [fed], core_ids=[0])
    return r.results[0]["out_dram"]
```
